# Optimizing a Trainium2 kernel written in Bass

```python
import numpy as np
import jax
import jax.numpy as jnp

def _softmax(x, axis=-1):
    return jax.nn.softmax(x, axis=axis)

def _gelu(x):
    return jax.nn.gelu(x, approximate=True)

def _silu(x):
    return jax.nn.silu(x)

def _sigmoid(x):
    return jax.nn.sigmoid(x)

def _layernorm(x, axis=-1, eps=1e-05):
    m = jnp.mean(x, axis=axis, keepdims=True)
    v = jnp.var(x, axis=axis, keepdims=True)
    return (x - m) / jnp.sqrt(v + eps)

def _scatter_add(tgt, idx, src, axis=0):
    return tgt.at[idx].add(src)

def _segment_sum(src, seg, n):
    return jax.ops.segment_sum(src, seg, n)
kernel_name = 'mk_macaron_d1_jaxref_r4_0bc460'

def setup_inputs(seed: int=0):
    np.random.seed(seed)
    _w = jnp.asarray

    def _L0_attn_setup():
        import jax, jax.numpy as jnp
        import numpy as np
        import math
        HIDDEN = 1024
        N_HEADS = 32
        N_KV_HEADS = 8
        HEAD_DIM = HIDDEN // N_HEADS
        GROUPS = N_HEADS // N_KV_HEADS
        ROPE_THETA = 10000.0
        TOKEN_BUDGET = 128
        INIT_BUDGET = 128
        RECENT_BUDGET = 128
        CHUNK = 16
        B, S = (1, 512)

        def _rotate_half(x):
            x1, x2 = jnp.split(x, 2, axis=-1)
            return jnp.concatenate([-x2, x1], axis=-1)

        def _rope(seq_len, dtype):
            inv_freq = 1.0 / ROPE_THETA ** (jnp.arange(0, HEAD_DIM, 2, dtype=jnp.float32) / HEAD_DIM)
            freqs = jnp.arange(seq_len, dtype=jnp.float32)[:, None] * inv_freq[None, :]
            emb = jnp.concatenate([freqs, freqs], axis=-1)
            return (jnp.cos(emb).astype(dtype), jnp.sin(emb).astype(dtype))
        key = jax.random.key(seed)
        ks = jax.random.split(key, 5)
        sc = 0.02
        return {'hidden_states': jax.random.normal(ks[0], (B, S, HIDDEN), dtype=jnp.float32), 'wq': jax.random.normal(ks[1], (N_HEADS * HEAD_DIM, HIDDEN), dtype=jnp.float32) * sc, 'wk': jax.random.normal(ks[2], (N_KV_HEADS * HEAD_DIM, HIDDEN), dtype=jnp.float32) * sc, 'wv': jax.random.normal(ks[3], (N_KV_HEADS * HEAD_DIM, HIDDEN), dtype=jnp.float32) * sc, 'wo': jax.random.normal(ks[4], (HIDDEN, N_HEADS * HEAD_DIM), dtype=jnp.float32) * sc}
    _L0_attn_in = _L0_attn_setup()

    def _L0_ffn_setup():
        import jax, jax.numpy as jnp
        import numpy as np
        NF4 = jnp.array([-1.0, -0.6961928009986877, -0.5250730514526367, -0.39491748809814453, -0.28444138169288635, -0.18477343022823334, -0.09105003625154495, 0.0, 0.07958029955625534, 0.16093020141124725, 0.24611230194568634, 0.33791524171829224, 0.44070982933044434, 0.5626170039176941, 0.7229568362236023, 1.0], dtype=jnp.float32)
        BLOCK = 64
        B, S, D, H, R = (2, 512, 1024, 2752, 16)

        def dequant_nf4(codes, absmax, shape):
            vals = NF4[codes] * jnp.repeat(absmax, BLOCK)
            return vals.reshape(shape)
        key = jax.random.key(seed)
        ks = jax.random.split(key, 11)
        n_w = H * D
        return {'x1': jax.random.normal(ks[0], (B, S, D), dtype=jnp.float32), 'w_up_codes': jax.random.randint(ks[1], (n_w,), 0, 16, dtype=jnp.int32), 'w_up_absmax': jax.random.uniform(ks[2], (n_w // BLOCK,), dtype=jnp.float32) * 0.05, 'b_up': jax.random.normal(ks[3], (H,), dtype=jnp.float32) * 0.02, 'w_up_lora_a': jax.random.normal(ks[4], (D, R), dtype=jnp.float32) * 0.02, 'w_up_lora_b': jax.random.normal(ks[5], (R, H), dtype=jnp.float32) * 0.02, 'w_down_codes': jax.random.randint(ks[6], (n_w,), 0, 16, dtype=jnp.int32), 'w_down_absmax': jax.random.uniform(ks[7], (n_w // BLOCK,), dtype=jnp.float32) * 0.05, 'b_down': jax.random.normal(ks[8], (D,), dtype=jnp.float32) * 0.02, 'w_down_lora_a': jax.random.normal(ks[9], (H, R), dtype=jnp.float32) * 0.02, 'w_down_lora_b': jax.random.normal(ks[10], (R, D), dtype=jnp.float32) * 0.02}
    _L0_ffn_in = _L0_ffn_setup()
    _d = {'L0_attn_hidden_states': _L0_attn_in['hidden_states'], 'L0_attn_wq': _L0_attn_in['wq'], 'L0_attn_wk': _L0_attn_in['wk'], 'L0_attn_wv': _L0_attn_in['wv'], 'L0_attn_wo': _L0_attn_in['wo'], 'L0_ffn_w_up_codes': _L0_ffn_in['w_up_codes'], 'L0_ffn_w_up_absmax': _L0_ffn_in['w_up_absmax'], 'L0_ffn_b_up': _L0_ffn_in['b_up'], 'L0_ffn_w_up_lora_a': _L0_ffn_in['w_up_lora_a'], 'L0_ffn_w_up_lora_b': _L0_ffn_in['w_up_lora_b'], 'L0_ffn_w_down_codes': _L0_ffn_in['w_down_codes'], 'L0_ffn_w_down_absmax': _L0_ffn_in['w_down_absmax'], 'L0_ffn_b_down': _L0_ffn_in['b_down'], 'L0_ffn_w_down_lora_a': _L0_ffn_in['w_down_lora_a'], 'L0_ffn_w_down_lora_b': _L0_ffn_in['w_down_lora_b']}
    _x0 = _d['L0_attn_hidden_states']
    _d['L0_attn_hidden_states'] = jax.random.normal(jax.random.fold_in(jax.random.key(seed), 1), (4, 512, 1024), dtype=_x0.dtype)
    del _x0
    return _d

def reference(L0_attn_hidden_states, L0_attn_wq, L0_attn_wk, L0_attn_wv, L0_attn_wo, L0_ffn_w_up_codes, L0_ffn_w_up_absmax, L0_ffn_b_up, L0_ffn_w_up_lora_a, L0_ffn_w_up_lora_b, L0_ffn_w_down_codes, L0_ffn_w_down_absmax, L0_ffn_b_down, L0_ffn_w_down_lora_a, L0_ffn_w_down_lora_b):

    def _L0_attn_ref(hidden_states, wq, wk, wv, wo):
        import jax, jax.numpy as jnp
        import numpy as np
        import math
        HIDDEN = 1024
        N_HEADS = 32
        N_KV_HEADS = 8
        HEAD_DIM = HIDDEN // N_HEADS
        GROUPS = N_HEADS // N_KV_HEADS
        ROPE_THETA = 10000.0
        TOKEN_BUDGET = 128
        INIT_BUDGET = 128
        RECENT_BUDGET = 128
        CHUNK = 16
        B, S = (1, 512)

        def _rotate_half(x):
            x1, x2 = jnp.split(x, 2, axis=-1)
            return jnp.concatenate([-x2, x1], axis=-1)

        def _rope(seq_len, dtype):
            inv_freq = 1.0 / ROPE_THETA ** (jnp.arange(0, HEAD_DIM, 2, dtype=jnp.float32) / HEAD_DIM)
            freqs = jnp.arange(seq_len, dtype=jnp.float32)[:, None] * inv_freq[None, :]
            emb = jnp.concatenate([freqs, freqs], axis=-1)
            return (jnp.cos(emb).astype(dtype), jnp.sin(emb).astype(dtype))
        b, s, _ = hidden_states.shape
        dtype = hidden_states.dtype
        NEG = jnp.finfo(dtype).min
        q = (hidden_states @ wq.T).reshape(b, s, N_HEADS, HEAD_DIM).transpose(0, 2, 1, 3)
        k = (hidden_states @ wk.T).reshape(b, s, N_KV_HEADS, HEAD_DIM).transpose(0, 2, 1, 3)
        v = (hidden_states @ wv.T).reshape(b, s, N_KV_HEADS, HEAD_DIM).transpose(0, 2, 1, 3)
        cos, sin = _rope(s, dtype)
        q = q * cos[None, None] + _rotate_half(q) * sin[None, None]
        k = k * cos[None, None] + _rotate_half(k) * sin[None, None]
        k = jnp.repeat(k, GROUPS, axis=1)
        v = jnp.repeat(v, GROUPS, axis=1)
        scores = jnp.einsum('bhqd,bhkd->bhqk', q, k) / math.sqrt(HEAD_DIM)
        q_pos = jnp.arange(s)[:, None]
        k_pos = jnp.arange(s)[None, :]
        causal = k_pos <= q_pos
        masked = jnp.where(causal[None, None], scores, NEG)
        pad = -s % CHUNK
        padded = jnp.pad(masked, ((0, 0), (0, 0), (0, 0), (0, pad)), constant_values=NEG)
        n_chunks = (s + pad) // CHUNK
        chunk_max = padded.reshape(b, N_HEADS, s, n_chunks, CHUNK).max(axis=-1)
        k_top = min(max(3, TOKEN_BUDGET // CHUNK), n_chunks)
        _, topk_idx = jax.lax.top_k(chunk_max, k_top)
        chunk_mask = jnp.any(topk_idx[..., None] == jnp.arange(n_chunks), axis=-2)
        tok_mask = jnp.repeat(chunk_mask, CHUNK, axis=-1)[..., :s]
        init_mask = k_pos < INIT_BUDGET
        recent_mask = k_pos > q_pos - RECENT_BUDGET
        allowed = causal[None, None] & (tok_mask | init_mask[None, None] | recent_mask[None, None])
        final = jnp.where(allowed, scores, NEG)
        attn = jax.nn.softmax(final, axis=-1)
        out = jnp.einsum('bhqk,bhkd->bhqd', attn, v)
        out = out.transpose(0, 2, 1, 3).reshape(b, s, N_HEADS * HEAD_DIM)
        return out @ wo.T

    def _L0_ffn_ref(x1, w_up_codes, w_up_absmax, b_up, w_up_lora_a, w_up_lora_b, w_down_codes, w_down_absmax, b_down, w_down_lora_a, w_down_lora_b):
        import jax, jax.numpy as jnp
        import numpy as np
        NF4 = jnp.array([-1.0, -0.6961928009986877, -0.5250730514526367, -0.39491748809814453, -0.28444138169288635, -0.18477343022823334, -0.09105003625154495, 0.0, 0.07958029955625534, 0.16093020141124725, 0.24611230194568634, 0.33791524171829224, 0.44070982933044434, 0.5626170039176941, 0.7229568362236023, 1.0], dtype=jnp.float32)
        BLOCK = 64
        B, S, D, H, R = (2, 512, 1024, 2752, 16)

        def dequant_nf4(codes, absmax, shape):
            vals = NF4[codes] * jnp.repeat(absmax, BLOCK)
            return vals.reshape(shape)
        w_up = dequant_nf4(w_up_codes, w_up_absmax, (H, D)).T
        y1 = x1 @ w_up + b_up + x1 @ w_up_lora_a @ w_up_lora_b
        x2 = jax.nn.relu(y1)
        w_down = dequant_nf4(w_down_codes, w_down_absmax, (D, H)).T
        y2 = x2 @ w_down + b_down + x2 @ w_down_lora_a @ w_down_lora_b
        return y2
    x = L0_attn_hidden_states
    x = x + 0.5 * _L0_ffn_ref(_layernorm(x, axis=-1), L0_ffn_w_up_codes, L0_ffn_w_up_absmax, L0_ffn_b_up, L0_ffn_w_up_lora_a, L0_ffn_w_up_lora_b, L0_ffn_w_down_codes, L0_ffn_w_down_absmax, L0_ffn_b_down, L0_ffn_w_down_lora_a, L0_ffn_w_down_lora_b)
    x = x + _L0_attn_ref(_layernorm(x, axis=-1), L0_attn_wq, L0_attn_wk, L0_attn_wv, L0_attn_wo)
    x = x + 0.5 * _L0_ffn_ref(_layernorm(x, axis=-1), L0_ffn_w_up_codes, L0_ffn_w_up_absmax, L0_ffn_b_up, L0_ffn_w_up_lora_a, L0_ffn_w_up_lora_b, L0_ffn_w_down_codes, L0_ffn_w_down_absmax, L0_ffn_b_down, L0_ffn_w_down_lora_a, L0_ffn_w_down_lora_b)
    return x

_drawn_inputs = setup_inputs


def setup_inputs(seed=0):
    import zlib

    import numpy as np

    out = dict(_drawn_inputs(seed))
    spreads = {}
    factors = {'L0_ffn_b_up': 5.725, 'L0_ffn_b_down': 3.168}
    for name, (base, spread) in spreads.items():
        noise = np.random.default_rng([zlib.crc32(name.encode()), seed]).standard_normal(out[name].shape)
        drawn = base * np.exp(spread * noise) if base else spread * noise
        out[name] = jnp.asarray(drawn.astype(out[name].dtype))
    for name, factor in factors.items():
        out[name] = (out[name] * factor).astype(out[name].dtype)
    return out
```

```python
from contextlib import ExitStack

import concourse.bass as bass
from concourse import mybir

F32 = mybir.dt.float32
F32R = mybir.dt.float32r
BF16 = mybir.dt.bfloat16
I16 = mybir.dt.int16
ALU = mybir.AluOpType
ACT = mybir.ActivationFunctionType
AX = mybir.AxisListType

P = 128
NF4 = [-1.0, -0.6961928009986877, -0.5250730514526367, -0.39491748809814453, -0.28444138169288635,
       -0.18477343022823334, -0.09105003625154495, 0.0, 0.07958029955625534, 0.16093020141124725,
       0.24611230194568634, 0.33791524171829224, 0.44070982933044434, 0.5626170039176941,
       0.7229568362236023, 1.0]
QBLK = 64
D = 1024
DK = D // P
H = 2752
RANK = 16
CH = 256
NCH = -(-H // CH)
HT = NCH * CH // P
LAST = H - (NCH - 1) * CH
BATCH, SEQ = 4, 512
T = BATCH * SEQ
TB = 1024
NTB = T // TB
TM = TB // P
EPS = 1e-5
NHEAD, NKV, HD = 32, 8, 32
GROUP = NHEAD // NKV
QKW = (NHEAD + NKV) * HD
QKVW = (NHEAD + 2 * NKV) * HD
CHUNK = 16
BIG = 1e30
SCALE = float(HD) ** -0.5


def after(eng, sem, n):
    if not (isinstance(n, int) and n <= 0):
        eng.wait_ge(sem, n)


def gate(eng, sem, n, passed):
    after(eng, sem, n)
    if not isinstance(n, int):
        eng.sem_inc(passed, 1)


class Pool:

    def __init__(self, nc, ctx, tag):
        self.nc, self.ctx, self.tag = nc, ctx, tag

    def sb(self, name, shape, dt=F32):
        return self.ctx.enter_context(self.nc.sbuf_tensor(f"{self.tag}_{name}", shape, dt))

    def ps(self, name, shape, dt=F32):
        return self.ctx.enter_context(self.nc.psum_tensor(f"{self.tag}_{name}", shape, dt))

    def sem(self, name):
        return self.ctx.enter_context(self.nc.semaphore(f"{self.tag}_{name}"))


def leaf(i):
    import numpy as np
    lo, hi = np.float32(NF4[2 * i]), np.float32(NF4[2 * i + 1])
    s = np.float32(hi - lo)
    for cand in (s, np.nextafter(s, np.float32(4)), np.nextafter(s, np.float32(-4))):
        if np.float32(np.float64(cand) + np.float64(lo)) == hi:
            return float(cand), float(lo)
    raise AssertionError(i)


def dequantise(nc, up_codes, up_absmax, up_a, up_b, dn_codes, dn_absmax, dn_a, dn_b, ident_dram,
               wup_dram, wdn_dram):
    SUB, PART = 4, 512
    with ExitStack() as ctx:
        m = Pool(nc, ctx, "dq")
        ident = m.sb("ident", [P, P])
        codes = m.sb("codes", [P, 2, SUB * PART], I16)
        bits = m.sb("bits", [P, 2, 4, SUB * PART], I16)
        amax_up = m.sb("amax_up", [P, HT, D // QBLK])
        amax_dn = m.sb("amax_dn", [P, DK, NCH * CH // QBLK])
        even = m.sb("even", [P, 2, 4, PART])
        wnat = m.sb("wnat", [P, 2, PART])
        stage = m.sb("stage", [P, 2, 2, SUB * PART], F32R)
        a_nat = m.sb("a_nat", [P, DK, RANK])
        dna_nat = m.sb("dna_nat", [P, HT, RANK])
        upa_t = m.sb("upa_t", [RANK, D])
        upb = m.sb("upb", [RANK, NCH * CH])
        dna_t = m.sb("dna_t", [RANK, NCH * CH])
        dnb = m.sb("dnb", [RANK, D])
        upb_c = m.sb("upb_c", [RANK, 2, CH])
        dna_c = m.sb("dna_c", [RANK, 2, CH])
        ps = m.ps("ps", [P, 8, PART])
        s_in = m.sem("in")
        s_passed = m.sem("passed")
        s_zero = m.sem("zero")
        s_code = [m.sem("code_up"), m.sem("code_dn")]
        s_lt, s_ltc = m.sem("lora_t"), m.sem("lora_copied")
        s_chunk = m.sem("lora_chunk")
        s_bits, s_leaf, s_sel = m.sem("bits"), m.sem("leaf"), m.sem("selected")
        s_w, s_tr, s_hi, s_lo = m.sem("scaled"), m.sem("transposed"), m.sem("hi"), m.sem("lo")
        s_out = [m.sem("out_up"), m.sem("out_dn")]

        code_up = up_codes.rearrange("(h d) -> h d", d=D)
        code_dn = dn_codes.rearrange("(k p h) -> p k h", p=P, h=H)
        abs_up = up_absmax.rearrange("(h b) -> h b", b=D // QBLK)
        abs_dn = dn_absmax.rearrange("(k p b) -> p k b", p=P, b=H // QBLK)
        FULL = H // P
        REST = H - FULL * P

        def part_in(kind, e):
            bank = ps[:, 4 + e % 2, :]
            if kind == 0:
                return bank.rearrange("p (k h) -> p k h", k=4)
            return bank.rearrange("p (k t d) -> p t k d", k=2, t=2)

        def part_out(kind, s, hl):
            if kind == 0:
                t, half = s // 2, s % 2
                return stage[:, 0, hl, :].rearrange("p (k h) -> p k h", k=DK)[:, half * 4:half * 4 + 4, t * P:(t + 1) * P]
            return stage[:, 1, hl, :].rearrange("p (t k d) -> p t k d", t=2, k=DK)[:, :, 2 * s:2 * s + 2, :]

        def order(e):
            return e // SUB, e % SUB

        def steps(eng, step):
            step(0, 0)
            with eng.Fori(1, NCH - 3, 2) as c:
                step(c, 1)
                step(c + 1, 0)
            for c in range(NCH - 2, NCH):
                step(c, c % 2)

        block = ctx.enter_context(nc.Block())

        @block.sync
        def _(sp):
            sp.dma_start(ident[:], ident_dram).then_inc(s_in, 16)
            sp.dma_start(a_nat[:], up_a.rearrange("(k p) r -> p k r", p=P)).then_inc(s_in, 16)
            sp.wait_ge(s_zero, 4)
            sp.dma_start(dna_nat[:, 0:FULL, :], dn_a[0:FULL * P, :].rearrange("(k p) r -> p k r", p=P)).then_inc(s_in, 16)
            sp.dma_start(dna_nat[0:REST, FULL, :], dn_a[FULL * P:H, :]).then_inc(s_in, 16)
            sp.dma_start(upb[:, 0:H], up_b).then_inc(s_in, 16)
            sp.dma_start(dnb[:], dn_b).then_inc(s_in, 16)
            sp.dma_start(amax_up[:, 0:FULL, :], abs_up[0:FULL * P, :].rearrange("(k p) b -> p k b", p=P)).then_inc(s_in, 16)
            sp.dma_start(amax_up[0:REST, FULL, :], abs_up[FULL * P:H, :]).then_inc(s_in, 16)
            sp.dma_start(amax_dn[:, :, 0:H // QBLK], abs_dn).then_inc(s_in, 16)

            def step(c, par):
                for kind, dram in ((0, wup_dram), (1, wdn_dram)):
                    sp.wait_ge(s_lo, c * 8 + 4 * (kind + 1))
                    sp.dma_start(dram[bass.ds(c, 1), :, :].rearrange("o p n -> (o p) n"),
                                 stage[:, kind, :, :].rearrange("p a n -> p (a n)").bitcast(F32)).then_inc(s_out[kind], 16)
            steps(sp, step)
            for kind in range(2):
                sp.wait_ge(s_out[kind], 16 * NCH)

        @block.gpsimd
        def _(pool):
            for tile in (amax_up[:, FULL, :], amax_dn[:, :, H // QBLK:], dna_nat[:, FULL, :], upb[:, H:]):
                pool.memset(tile, 0.0).then_inc(s_zero, 1)

            def load(c, kind):
                if kind == 0:
                    src = code_up[bass.ds(c * CH, CH), :].rearrange("(t p) d -> p t d", p=P)
                    pool.dma_start(codes[:, 0, :].rearrange("p (t d) -> p t d", t=2), src).then_inc(s_code[0], 16)
                else:
                    pool.dma_start(codes[:, 1, :].rearrange("p (k h) -> p k h", k=DK),
                                   code_dn[:, :, bass.ds(c * CH, CH)]).then_inc(s_code[1], 16)

            def load_last(kind):
                c0 = (NCH - 1) * CH
                if kind == 0:
                    pool.dma_start(codes[:, 0, 0:D], code_up[c0:c0 + P, :]).then_inc(s_code[0], 16)
                    pool.dma_start(codes[0:REST, 0, D:2 * D], code_up[c0 + P:H, :]).then_inc(s_code[0], 16)
                else:
                    pool.dma_start(codes[:, 1, :].rearrange("p (k h) -> p k h", k=DK)[:, :, 0:LAST],
                                   code_dn[:, :, c0:H]).then_inc(s_code[1], 16)

            load(0, 0)
            load(0, 1)
            pool.wait_ge(s_in, 16 * 9)
            pool.wait_ge(s_ltc, 2)

            def step(c, par):
                after(pool, s_tr, c * 8 - 8)
                pool.tensor_copy(upb_c[:, par, :], upb[:, bass.ds(c * CH, CH)]).then_inc(s_chunk, 1)
                pool.tensor_copy(dna_c[:, par, :], dna_t[:, bass.ds(c * CH, CH)]).then_inc(s_chunk, 1)
                for e in range(8):
                    kind, s = order(e)
                    n = c * 8 + e
                    pool.wait_ge(s_sel, 7 * n + 7)
                    after(pool, s_tr, n - 1)
                    if kind == 0:
                        t, half = s // 2, s % 2
                        am = amax_up[:, bass.ds(c * 2 + t, 1), half * 8:half * 8 + 8].rearrange("p o b -> p (o b)")\
                            .unsqueeze(2).to_broadcast([P, 8, QBLK])
                        pool.tensor_tensor(wnat[:, e % 2, :].rearrange("p (b q) -> p b q", q=QBLK),
                                           even[:, e % 2, 0, :].rearrange("p (b q) -> p b q", q=QBLK),
                                           am, ALU.mult).then_inc(s_w, 1)
                    else:
                        am = amax_dn[:, 2 * s:2 * s + 2, bass.ds(c * 4, 4)].unsqueeze(3).to_broadcast([P, 2, 4, QBLK])
                        pool.tensor_tensor(wnat[:, e % 2, :].rearrange("p (k b q) -> p k b q", k=2, q=QBLK),
                                           even[:, e % 2, 0, :].rearrange("p (k b q) -> p k b q", k=2, q=QBLK),
                                           am, ALU.mult).then_inc(s_w, 1)
                    if s == 0 and not (isinstance(c, int) and c == NCH - 1):
                        pool.wait_ge(s_bits, c * 2 + kind + 1)
                        if isinstance(c, int) and c == NCH - 2:
                            load_last(kind)
                        else:
                            load(c + 1, kind)
            steps(pool, step)

        @block.scalar
        def _(act):
            act.wait_ge(s_lt, 1)
            act.activation(upa_t[:], ps[0:RANK, 0:2, :].rearrange("p a n -> p (a n)"), ACT.Copy).then_inc(s_ltc, 1)
            act.activation(dna_t[:], ps[0:RANK, 2:8, :].rearrange("p a n -> p (a n)")[:, 0:NCH * CH], ACT.Copy).then_inc(s_ltc, 1)

            def leaves(c, e):
                kind, s = order(e)
                n = c * 8 + e
                if s == 0:
                    act.wait_ge(s_bits, c * 2 + kind + 1)
                bit = bits[:, kind, 0, s * PART:(s + 1) * PART]
                for i in range(4):
                    after(act, s_sel, 7 * n - 6 + i)
                    sc, off = leaf(2 * i + 1)
                    act.activation(ps[:, i, :], bit, ACT.Copy, scale=sc, bias=off).then_inc(s_leaf, 1)
                    if i == 0:
                        after(act, s_w, n - 1)
                    sc, off = leaf(2 * i)
                    act.activation(even[:, e % 2, i, :], bit, ACT.Copy, scale=sc, bias=off).then_inc(s_leaf, 1)

            def hi(c, e):
                kind, s = order(e)
                n = c * 8 + e
                act.wait_ge(s_tr, n + 1)
                if s == 0:
                    after(act, s_out[kind], c * 16)
                act.activation(part_out(kind, s, 0), part_in(kind, e), ACT.Copy).then_inc(s_hi, 1)

            def step(c, par):
                for e in range(8):
                    leaves(c, e)
                    if e >= 2:
                        hi(c, e - 2)
                    elif not (isinstance(c, int) and c == 0):
                        hi(c - 1, e + 6)
            act.wait_ge(s_ltc, 2)
            steps(act, step)
            hi(NCH - 1, 6)
            hi(NCH - 1, 7)

        @block.vector
        def _(dve):
            def lo(c, e):
                kind, s = order(e)
                dve.wait_ge(s_hi, c * 8 + e + 1)
                hi_half = part_out(kind, s, 0)
                low, src = part_out(kind, s, 1), part_in(kind, e)
                if kind == 0:
                    dve.tensor_tensor(low, src, hi_half.bitcast(F32), ALU.subtract).then_inc(s_lo, 1)
                else:
                    dve.tensor_tensor(low, src, hi_half.bitcast(F32), ALU.subtract).then_inc(s_lo, 1)

            def step(c, par):
                for e in range(8):
                    kind, s = order(e)
                    n = c * 8 + e
                    if s == 0:
                        last = isinstance(c, int) and c == NCH - 1 and kind == 0
                        dve.wait_ge(s_code[kind], c * 16 + (32 if last else 16))
                        after(dve, s_leaf, 8 * n - 32)
                        for b in range(3, -1, -1):
                            ins = dve.tensor_scalar(bits[:, kind, b, :], codes[:, kind, :], 1 << b, None, ALU.bitwise_and)
                        ins.then_inc(s_bits, 1)
                        dve.wait_ge(s_bits, c * 2 + kind + 1)
                    cols = slice(s * PART, (s + 1) * PART)
                    ev = even[:, e % 2, :, :]
                    for i in range(4):
                        gate(dve, s_leaf, 8 * n + 2 * i + 2, s_passed)
                        dve.copy_predicated(ev[:, i, :], bits[:, kind, 1, cols], ps[:, i, :]).then_inc(s_sel, 1)
                    for k, (a, b, bit) in enumerate(((0, 1, 2), (2, 3, 2), (0, 2, 3))):
                        gate(dve, s_sel, 7 * n + (2, 4, 6)[k], s_passed)
                        dve.copy_predicated(ev[:, a, :], bits[:, kind, bit, cols], ev[:, b, :]).then_inc(s_sel, 1)
                    if e >= 2:
                        lo(c, e - 2)
                    elif not (isinstance(c, int) and c == 0):
                        lo(c - 1, e + 6)
            steps(dve, step)
            lo(NCH - 1, 6)
            lo(NCH - 1, 7)

        @block.tensor
        def _(pe):
            pe.wait_ge(s_in, 16 * 9)
            for k in range(DK):
                pe.transpose(ps[0:RANK, k // 4, (k % 4) * P:(k % 4 + 1) * P], a_nat[:, k, :], ident[:])
            for t in range(HT):
                ins = pe.transpose(ps[0:RANK, 2 + t // 4, (t % 4) * P:(t % 4 + 1) * P], dna_nat[:, t, :], ident[:])
            ins.then_inc(s_lt, 1)
            pe.wait_ge(s_ltc, 2)

            def step(c, par):
                pe.wait_ge(s_chunk, c * 2 + 2)
                for e in range(8):
                    kind, s = order(e)
                    n = c * 8 + e
                    pe.wait_ge(s_w, n + 1)
                    after(pe, s_lo, n - 1)
                    for j in range(4):
                        dst = ps[:, 4 + e % 2, j * P:(j + 1) * P]
                        pe.matmul(dst, wnat[:, e % 2, j * P:(j + 1) * P], ident[:], is_transpose=True, start=True, stop=False)
                        if kind == 0:
                            t, k = s // 2, (s % 2) * 4 + j
                            ins = pe.matmul(dst, upa_t[:, k * P:(k + 1) * P], upb_c[:, par, t * P:(t + 1) * P], start=False, stop=True)
                        else:
                            k, t = 2 * s + j // 2, j % 2
                            ins = pe.matmul(dst, dna_c[:, par, t * P:(t + 1) * P], dnb[:, k * P:(k + 1) * P], start=False, stop=True)
                    ins.then_inc(s_tr, 1)
            steps(pe, step)


class Count:

    def __init__(self, eng, sem, base=0):
        self.eng, self.sem, self.n = eng, sem, base

    def link(self, ins):
        ins.then_inc(self.sem, 1)
        self.n = self.n + 1
        self.eng.wait_ge(self.sem, self.n)


def inverse_root(dve, link, rstd, var, tmp):
    link(dve.tensor_tensor(tmp, rstd, rstd, ALU.mult))
    link(dve.tensor_tensor(tmp, tmp, var, ALU.mult))
    link(dve.tensor_scalar(tmp, tmp, -0.5, 1.5, ALU.mult, ALU.add))
    link(dve.tensor_tensor(rstd, rstd, tmp, ALU.mult))


def ffn(nc, tag, x_dram, y_dram, b_up, b_down, ident_dram, wup_dram, wdn_dram):
    NH = TB // 512
    UPG = 2 * NH
    DNG = TM * 2
    with ExitStack() as ctx:
        m = Pool(nc, ctx, tag)
        ident = m.sb("ident", [P, P])
        bup = m.sb("bup", [P, HT])
        bup_c = m.sb("bup_c", [P, 2, 2])
        bdn = m.sb("bdn", [P, D])
        y = m.sb("y", [P, TM, D])
        xn = m.sb("xn", [P, 2, 512])
        xt = m.sb("xt", [P, 2, DK, TB], F32R)
        wu = m.sb("wu", [P, 2, 2, DK, CH], F32R)
        wd = m.sb("wd", [P, 2, 2, 2, D], F32R)
        ht = m.sb("ht", [P, 2, 2, 2, TB], F32R)
        hraw = m.sb("hraw", [P, 2, 512])
        stats = m.sb("stats", [P, 2, 6])
        mv = m.sb("mv", [P, TM, 2])
        var = m.sb("var", [P, TM])
        rstd = m.sb("rstd", [P, TM])
        tmp = m.sb("tmp", [P, TM])
        pt = m.ps("pt", [P, 2, 512])
        pu = m.ps("pu", [P, 2, 512])
        pd = m.ps("pd", [P, 4, 512])
        s_const, s_x, s_store = m.sem("const"), m.sem("x"), m.sem("store")
        s_seq = m.sem("vector_seq")
        s_bdn, s_yi = m.sem("bdn"), m.sem("y_started")
        s_var, s_sd, s_xn = m.sem("var"), m.sem("sd"), m.sem("xn")
        s_pt, s_xhi, s_xlo = m.sem("x_transposed"), m.sem("x_hi"), m.sem("x_lo")
        s_wu = [m.sem("wu0"), m.sem("wu1")]
        s_wd = [m.sem("wd0"), m.sem("wd1")]
        s_upg, s_bc = m.sem("up_group"), m.sem("bias_chunk")
        s_raw, s_hhi, s_hlo = m.sem("h_raw"), m.sem("h_hi"), m.sem("h_lo")
        s_dng, s_y = m.sem("down_group"), m.sem("y_added")
        x_rows = x_dram.rearrange("(b m p) d -> b p m d", m=TM, p=P)
        y_rows = y_dram.rearrange("(b m p) d -> b p m d", m=TM, p=P)
        FULL = H // P

        block = ctx.enter_context(nc.Block())

        def loads_before(b, par):
            return b * ((NCH + 1) // 2 if par == 0 else NCH // 2)

        @block.sync
        def _(sp):
            sp.dma_start(ident[:], ident_dram).then_inc(s_const, 16)
            sp.dma_start(bdn[:], b_down.rearrange("(o d) -> o d", o=1).to_broadcast([P, D])).then_inc(s_const, 16)
            sp.wait_ge(s_bdn, 1)
            sp.dma_start(bup[:, 0:FULL], b_up[0:FULL * P].rearrange("(t p) -> p t", p=P), allow_slow_non_contiguous=True).then_inc(s_const, 16)
            sp.dma_start(bup[0:H - FULL * P, FULL:FULL + 1], b_up[FULL * P:H].rearrange("(p o) -> p o", o=1)).then_inc(s_const, 16)
            for b in range(NTB):
                after(sp, s_store, b * 16 * TM)
                for i in range(TM):
                    sp.dma_start(y[:, i, :], x_rows[b, :, i, :]).then_inc(s_x, 16)

                def load(c, par):
                    after(sp, s_upg, (b * NCH + c - 1) * UPG)
                    sp.dma_start(wu[:, par, :, :, :].rearrange("p a k h -> p (a k h)").bitcast(F32),
                                 wup_dram[bass.ds(c, 1), :, :].rearrange("o p n -> (o p) n")).then_inc(s_wu[par], 16)
                    after(sp, s_y, (b * NCH + c - 1) * DNG)
                    sp.dma_start(wd[:, par, :, :, :].rearrange("p a k h -> p (a k h)").bitcast(F32),
                                 wdn_dram[bass.ds(c, 1), :, :].rearrange("o p n -> (o p) n")).then_inc(s_wd[par], 16)
                load(0, 0)
                load(1, 1)
                with sp.Fori(1, NCH // 2) as q:
                    load(2 * q, 0)
                    load(2 * q + 1, 1)
                load(NCH - 1, (NCH - 1) % 2)
                for i in range(TM):
                    sp.wait_ge(s_y, ((b + 1) * NCH - 1) * DNG + 2 * (i + 1))
                    sp.dma_start(y_rows[b, :, i, :], y[:, i, :]).then_inc(s_store, 16)
            sp.wait_ge(s_store, 16 * TM * NTB)

        @block.gpsimd
        def _(pool):
            pool.memset(bup[:, FULL:FULL + 1], 0.0).then_inc(s_bdn, 1)
            pool.wait_ge(s_const, 64)
            pool.tensor_scalar(bdn[:], bdn[:], 0.5, 0.0, ALU.mult, ALU.add).then_inc(s_bdn, 1)
            pool.wait_ge(s_bdn, 2)
            for b in range(NTB):
                for i in range(TM):
                    pool.wait_ge(s_xn, 2 * (b * TM + i + 1))
                    pool.tensor_tensor(y[:, i, :], y[:, i, :], bdn[:], ALU.add).then_inc(s_yi, 1)

        @block.scalar
        def _(act):
            def up_out(c, par, base):
                for t in range(2):
                    for h in range(NH):
                        g = t * NH + h
                        n = base + c * UPG + g
                        act.wait_ge(s_upg, n + 1)
                        if g == 0:
                            after(act, s_dng, (base // UPG + c - 1) * DNG)
                        bias = bup_c[:, par, t:t + 1]
                        after(act, s_hlo, n - 1)
                        act.activation(hraw[:, h, :], pu[:, h, :], ACT.Relu, bias=bias).then_inc(s_raw, 1)
                        act.activation(ht[:, par, 0, t, h * 512:(h + 1) * 512], pu[:, h, :], ACT.Relu, bias=bias).then_inc(s_hhi, 1)

            act.wait_ge(s_const, 64)
            for b in range(NTB):
                act.wait_ge(s_var, b + 1)
                act.activation(rstd[:], var[:], ACT.Sqrt).then_inc(s_sd, 1)
                for i in range(TM):
                    for half in range(2):
                        n = (b * TM + i) * 2 + half
                        act.wait_ge(s_pt, n + 1)
                        if n % (2 * TM) == 0:
                            after(act, s_upg, b * NCH * UPG)
                        act.activation(xt[:, 0, half * 4:half * 4 + 4, i * P:(i + 1) * P],
                                       pt[:, half, :].rearrange("p (k n) -> p k n", k=4), ACT.Copy).then_inc(s_xhi, 1)
                base = b * NCH * UPG

                def one(c, par):
                    act.activation(bup_c[:, par, :], bup[:, bass.ds(2 * c, 2)], ACT.Copy).then_inc(s_bc, 1)
                    act.wait_ge(s_bc, b * NCH + c + 1)
                    up_out(c, par, base)
                one(0, 0)
                one(1, 1)
                with act.Fori(1, NCH // 2) as q:
                    one(2 * q, 0)
                    one(2 * q + 1, 1)
                one(NCH - 1, (NCH - 1) % 2)

        @block.vector
        def _(dve):
            seq = Count(dve, s_seq)
            dve.wait_ge(s_bdn, 2)
            for b in range(NTB):
                dve.wait_ge(s_x, 16 * TM * (b + 1))
                for i in range(TM):
                    for j in range(2):
                        ins = dve.bn_stats(out=stats[:, j, :], in_=y[:, i, j * 512:(j + 1) * 512])
                    seq.link(ins)
                    seq.link(dve.bn_aggr(out=mv[:, i, :], in_=stats[:, :, :]))
                dve.tensor_scalar(var[:], mv[:, :, 1], EPS, None, ALU.add).then_inc(s_var, 1)
                dve.wait_ge(s_sd, b + 1)
                seq.link(dve.reciprocal(rstd[:], rstd[:]))
                inverse_root(dve, seq.link, rstd[:], var[:], tmp[:])

                def x_lo(i, half):
                    n = (b * TM + i) * 2 + half
                    dve.wait_ge(s_xhi, n + 1)
                    dst = xt[:, 1, half * 4:half * 4 + 4, i * P:(i + 1) * P]
                    dve.tensor_tensor(dst, pt[:, half, :].rearrange("p (k n) -> p k n", k=4),
                                      xt[:, 0, half * 4:half * 4 + 4, i * P:(i + 1) * P].bitcast(F32),
                                      ALU.subtract).then_inc(s_xlo, 1)
                for i in range(TM):
                    for half in range(2):
                        after(dve, s_pt, 2 * (b * TM + i) + half - 1)
                        dve.tensor_scalar(xn[:, half, :], y[:, i, half * 512:(half + 1) * 512], mv[:, i, 0:1],
                                          rstd[:, i:i + 1], ALU.subtract, ALU.mult).then_inc(s_xn, 1)
                    if i:
                        x_lo(i - 1, 0)
                        x_lo(i - 1, 1)
                x_lo(TM - 1, 0)
                x_lo(TM - 1, 1)
                base, dbase = b * NCH * UPG, b * NCH * DNG

                def h_lo(c, par):
                    for t in range(2):
                        for h in range(NH):
                            dve.wait_ge(s_hhi, base + c * UPG + t * NH + h + 1)
                            hi = ht[:, par, 0, t, h * 512:(h + 1) * 512]
                            dve.tensor_tensor(ht[:, par, 1, t, h * 512:(h + 1) * 512], hraw[:, h, :],
                                              hi.bitcast(F32), ALU.subtract).then_inc(s_hlo, 1)

                def add(c):
                    for i in range(TM):
                        for half in range(2):
                            g = 2 * i + half
                            n = dbase + c * DNG + g
                            dve.wait_ge(s_dng, n + 1)
                            cols = y[:, i, half * 512:(half + 1) * 512]
                            dve.scalar_tensor_tensor(out=cols, in0=pd[:, g % 4, :], scalar=0.5, in1=cols,
                                                     op0=ALU.mult, op1=ALU.add).then_inc(s_y, 1)

                def one(c, par):
                    h_lo(c + 1, 1 - par)
                    after(dve, s_y, dbase + c * DNG)
                    add(c)
                h_lo(0, 0)
                dve.wait_ge(s_yi, TM * (b + 1))
                one(0, 0)
                one(1, 1)
                with dve.Fori(1, NCH // 2) as q:
                    one(2 * q, 0)
                    one(2 * q + 1, 1)
                dve.wait_ge(s_y, dbase + (NCH - 1) * DNG)
                add(NCH - 1)

        @block.tensor
        def _(pe):
            pe.wait_ge(s_const, 64)
            for b in range(NTB):
                for i in range(TM):
                    for half in range(2):
                        n = (b * TM + i) * 2 + half
                        pe.wait_ge(s_xn, n + 1)
                        after(pe, s_xlo, n - 1)
                        for k in range(4):
                            ins = pe.transpose(pt[:, half, k * P:(k + 1) * P], xn[:, half, k * P:(k + 1) * P], ident[:])
                        ins.then_inc(s_pt, 1)
                pe.wait_ge(s_xlo, (b + 1) * TM * 2)
                base, dbase = b * NCH * UPG, b * NCH * DNG

                def up(c, par, pair):
                    pe.wait_ge(s_wu[par], 16 * (loads_before(b, par) + pair + 1))
                    for t in range(2):
                        for h in range(NH):
                            g = t * NH + h
                            after(pe, s_hhi, base + c * UPG + g - 1)
                            for k in range(DK):
                                for j, (wi, xi) in enumerate(((0, 0), (0, 1), (1, 0))):
                                    ins = pe.matmul(pu[:, h, :], wu[:, par, wi, k, t * P:(t + 1) * P],
                                                    xt[:, xi, k, h * 512:(h + 1) * 512],
                                                    start=(k == 0 and j == 0), stop=(k == DK - 1 and j == 2))
                            ins.then_inc(s_upg, 1)

                def down(c, par, pair):
                    pe.wait_ge(s_wd[par], 16 * (loads_before(b, par) + pair + 1))
                    pe.wait_ge(s_hlo, base + (c + 1) * UPG)
                    for i in range(TM):
                        for half in range(2):
                            g = 2 * i + half
                            after(pe, s_y, dbase + c * DNG + g - 3)
                            for t in range(2):
                                for j, (hi, wi) in enumerate(((0, 0), (0, 1), (1, 0))):
                                    ins = pe.matmul(pd[:, g % 4, :], ht[:, par, hi, t, i * P:(i + 1) * P],
                                                    wd[:, par, wi, t, half * 512:(half + 1) * 512],
                                                    start=(t == 0 and j == 0), stop=(t == 1 and j == 2))
                            ins.then_inc(s_dng, 1)
                up(0, 0, 0)
                up(1, 1, 0)
                down(0, 0, 0)
                up(2, 0, 1)
                down(1, 1, 0)
                with pe.Fori(1, NCH // 2) as q:
                    up(2 * q + 1, 1, q)
                    down(2 * q, 0, q)
                    up(2 * q + 2, 0, q + 1)
                    down(2 * q + 1, 1, q)
                down(NCH - 1, 0, NCH // 2)


def tile_loop(eng, step):
    n = T // P
    step(0, 0)
    step(1, 1)
    with eng.Fori(1, n // 2 - 1) as q:
        step(2 * q, 0)
        step(2 * q + 1, 1)
    step(n - 2, 0)
    step(n - 1, 1)


def known(m, test):
    return isinstance(m, int) and test(m)


def qkv(nc, x_dram, weights, ident_dram, rope_dram, qk_dram, v_dram):
    NT = T // P
    RT = QKVW // P
    W0 = 2 * RT
    with ExitStack() as ctx:
        m_ = Pool(nc, ctx, "qk")
        ident = m_.sb("ident", [P, P])
        wnat = m_.sb("wnat", [P, 2, D])
        wt = m_.sb("wt", [P, 2, DK, QKVW], F32R)
        x = m_.sb("x", [P, 2, D])
        rope = m_.sb("rope", [P, 2, 2 * HD])
        xn = m_.sb("xn", [P, 2, D])
        xt = m_.sb("xt", [P, 2, 2, DK, P], F32R)
        straight = m_.sb("straight", [P, QKW])
        crossed = m_.sb("crossed", [P, QKW])
        qr = m_.sb("qr", [P, QKW])
        qs = m_.sb("qs", [P, 2, 2, QKW // P, P], F32R)
        vs = m_.sb("vs", [P, 2, NKV * HD])
        stats = m_.sb("stats", [P, 2, 6])
        mv = m_.sb("mv", [P, 2])
        var = m_.sb("var", [P, 1])
        rstd = m_.sb("rstd", [P, 1])
        tmp = m_.sb("tmp", [P, 1])
        pt = m_.ps("pt", [P, 2, 512])
        pq = m_.ps("pq", [P, 3, 512])
        pr = m_.ps("pr", [P, 3, 512])
        s_const = m_.sem("const")
        s_w = [m_.sem("w0"), m_.sem("w1")]
        s_x = [m_.sem("x0"), m_.sem("x1")]
        s_passed = m_.sem("passed")
        s_rope = [m_.sem("rope0"), m_.sem("rope1")]
        s_seq, s_var, s_sd, s_xn = m_.sem("vector_seq"), m_.sem("var"), m_.sem("sd"), m_.sem("xn")
        s_pt, s_hi, s_lo = m_.sem("transposed"), m_.sem("hi"), m_.sem("lo")
        s_mm, s_rd, s_v, s_qr = m_.sem("products"), m_.sem("rope_read"), m_.sem("v"), m_.sem("rotated")
        s_qt, s_qhi, s_qlo = m_.sem("q_transposed"), m_.sem("q_hi"), m_.sem("q_lo")
        s_out = [m_.sem("out0"), m_.sem("out1")]
        rows = [(w, r) for w in weights for r in range(w.shape[0] // P)]
        assert len(rows) == RT
        qk_rows = qk_dram.rearrange("a (j p) t -> a p j t", p=P)
        width = [512, 512, QKW - 1024]

        block = ctx.enter_context(nc.Block())

        @block.sync
        def _(sp):
            sp.dma_start(ident[:], ident_dram).then_inc(s_const, 16)
            for n, (w, r) in enumerate(rows):
                after(sp, s_pt, 2 * (n - 1))
                sp.dma_start(wnat[:, n % 2, :], w[r * P:(r + 1) * P, :]).then_inc(s_w[n % 2], 16)

            def step(m, par):
                after(sp, s_xn, m - 1)
                sp.dma_start(x[:, par, :], x_dram[bass.ds(m * P, P), :]).then_inc(s_x[par], 16)
                after(sp, s_rd, 3 * m - 3)
                sp.dma_start(rope[:, par, :], rope_dram[bass.ds(m * P, P), :]).then_inc(s_rope[par], 16)
            tile_loop(sp, step)

        @block.gpsimd
        def _(pool):
            def step(m, par):
                for g in range(3):
                    cols = slice(512 * g, 512 * g + width[g])
                    after(pool, s_qt, 3 * m + g - 2)
                    pool.wait_ge(s_rd, 3 * m + g + 1)
                    pool.tensor_tensor(qr[:, cols], straight[:, cols], crossed[:, cols], ALU.add).then_inc(s_qr, 1)
                if not known(m, lambda k: k == 0):
                    store(m - 1, 1 - par)

            def store(m, par):
                pool.wait_ge(s_qlo, 3 * m + 3)
                pool.wait_ge(s_v, m + 1)
                for a in range(2):
                    pool.dma_start(qk_rows[a, :, :, bass.ds(m * P, P)], qs[:, par, a, :, :].bitcast(F32)).then_inc(s_out[par], 16)
                pool.dma_start(v_dram[bass.ds(m * P, P), :], vs[:, par, :]).then_inc(s_out[par], 16)
            tile_loop(pool, step)
            store(NT - 1, 1)
            for par in range(2):
                pool.wait_ge(s_out[par], 48 * NT // 2)

        @block.scalar
        def _(act):
            def hi(unit, dst):
                act.wait_ge(s_pt, unit + 1)
                act.activation(dst, pt[:, unit_bank(unit), :].rearrange("p (k n) -> p k n", k=4), ACT.Copy).then_inc(s_hi, 1)

            def unit_bank(unit):
                return unit % 2

            for n in range(RT):
                for half in range(2):
                    hi(2 * n + half, wt[:, 0, half * 4:half * 4 + 4, n * P:(n + 1) * P])

            def root(m):
                act.wait_ge(s_var, m + 1)
                act.activation(rstd[:], var[:], ACT.Sqrt).then_inc(s_sd, 1)

            def x_hi(m, par):
                after(act, s_mm, 3 * m - 3)
                for half in range(2):
                    act.wait_ge(s_pt, W0 + 2 * m + half + 1)
                    act.activation(xt[:, par, 0, half * 4:half * 4 + 4, :],
                                   pt[:, half, :].rearrange("p (k n) -> p k n", k=4), ACT.Copy).then_inc(s_hi, 1)

            def q_hi(m, par, pair):
                after(act, s_out[par], 48 * pair)
                for g in range(3):
                    act.wait_ge(s_qt, 3 * m + g + 1)
                    act.activation(qs[:, par, 0, 4 * g:4 * g + width[g] // P, :],
                                   pr[:, g, 0:width[g]].rearrange("p (j n) -> p j n", n=P), ACT.Copy).then_inc(s_qhi, 1)

            def v_out(m, par, pair):
                after(act, s_out[par], 48 * pair)
                act.wait_ge(s_rd, 3 * m + 3)
                act.activation(vs[:, par, :], pq[:, 2, 256:512], ACT.Copy).then_inc(s_v, 1)

            root(0)
            root(1)
            x_hi(0, 0)

            def paired(q, u):
                m = 2 * q + u
                if not known(m, lambda k: k >= NT - 1):
                    x_hi(m + 1, 1 - u)
                if not known(m, lambda k: k >= NT - 2):
                    root(m + 2)
                if not known(m, lambda k: k == 0):
                    v_out(m - 1, 1 - u, q if u else q - 1)
                    q_hi(m - 1, 1 - u, q if u else q - 1)
            paired(0, 0)
            paired(0, 1)
            with act.Fori(1, NT // 2 - 1) as q:
                paired(q, 0)
                paired(q, 1)
            paired(NT // 2 - 1, 0)
            paired(NT // 2 - 1, 1)
            v_out(NT - 1, 1, NT // 2 - 1)
            q_hi(NT - 1, 1, NT // 2 - 1)

        @block.vector
        def _(dve):
            for n in range(RT):
                for half in range(2):
                    dve.wait_ge(s_hi, 2 * n + half + 1)
                    cols = (slice(None), slice(half * 4, half * 4 + 4), slice(n * P, (n + 1) * P))
                    dve.tensor_tensor(wt[:, 1, cols[1], cols[2]], pt[:, half, :].rearrange("p (k n) -> p k n", k=4),
                                      wt[:, 0, cols[1], cols[2]].bitcast(F32), ALU.subtract).then_inc(s_lo, 1)

            PER = 7

            def norm(m, par, pair):
                seq = Count(dve, s_seq, PER * m)
                dve.wait_ge(s_x[par], 16 * pair + 16)
                for j in range(2):
                    ins = dve.bn_stats(out=stats[:, j, :], in_=x[:, par, j * 512:(j + 1) * 512])
                ins.then_inc(s_seq, 1)
                gate(dve, s_seq, PER * m + 1, s_passed)
                seq.n = PER * m + 1
                seq.link(dve.bn_aggr(out=mv[:], in_=stats[:, :, :]))
                dve.tensor_scalar(var[:], mv[:, 1:2], EPS, None, ALU.add).then_inc(s_var, 1)
                dve.wait_ge(s_sd, m + 1)
                seq.link(dve.reciprocal(rstd[:], rstd[:]))
                inverse_root(dve, seq.link, rstd[:], var[:], tmp[:])
                after(dve, s_pt, W0 + 2 * m - 2)
                dve.tensor_scalar(xn[:, par, :], x[:, par, :], mv[:, 0:1], rstd[:], ALU.subtract, ALU.mult).then_inc(s_xn, 1)

            def x_lo(m, par):
                for half in range(2):
                    dve.wait_ge(s_hi, W0 + 2 * m + half + 1)
                    dve.tensor_tensor(xt[:, par, 1, half * 4:half * 4 + 4, :], pt[:, half, :].rearrange("p (k n) -> p k n", k=4),
                                      xt[:, par, 0, half * 4:half * 4 + 4, :].bitcast(F32), ALU.subtract).then_inc(s_lo, 1)

            def q_lo(m, par):
                for g in range(3):
                    dve.wait_ge(s_qhi, 3 * m + g + 1)
                    js = slice(4 * g, 4 * g + width[g] // P)
                    dve.tensor_tensor(qs[:, par, 1, js, :], pr[:, g, 0:width[g]].rearrange("p (j n) -> p j n", n=P),
                                      qs[:, par, 0, js, :].bitcast(F32), ALU.subtract).then_inc(s_qlo, 1)

            def rotate(m, par, pair):
                dve.wait_ge(s_rope[par], 16 * pair + 16)
                for g in range(3):
                    nh = width[g] // HD
                    src = pq[:, g, 0:width[g]].rearrange("p (h r) -> p h r", r=HD)
                    cols = slice(512 * g, 512 * g + width[g])
                    st = straight[:, cols].rearrange("p (h r) -> p h r", r=HD)
                    cr = crossed[:, cols].rearrange("p (h r) -> p h r", r=HD)

                    def over_heads(a, b):
                        return rope[:, par, a:b].unsqueeze(1).to_broadcast([P, nh, b - a])
                    dve.wait_ge(s_mm, 3 * m + g + 1)
                    after(dve, s_qr, 3 * m + g - 2)
                    dve.tensor_tensor(st, src, over_heads(0, HD), ALU.mult)
                    dve.tensor_tensor(cr[:, :, 0:HD // 2], src[:, :, HD // 2:HD], over_heads(HD, HD + HD // 2), ALU.mult)
                    dve.tensor_tensor(cr[:, :, HD // 2:HD], src[:, :, 0:HD // 2], over_heads(HD + HD // 2, 2 * HD), ALU.mult)\
                        .then_inc(s_rd, 1)

            norm(0, 0, 0)
            norm(1, 1, 0)
            x_lo(0, 0)

            def paired(q, u):
                m = 2 * q + u
                if not known(m, lambda k: k == 0):
                    rotate(m - 1, 1 - u, q if u else q - 1)
                if not known(m, lambda k: k >= NT - 1):
                    x_lo(m + 1, 1 - u)
                if not known(m, lambda k: k >= NT - 2):
                    norm(m + 2, u, q + 1)
                if not known(m, lambda k: k == 0):
                    q_lo(m - 1, 1 - u)
            paired(0, 0)
            paired(0, 1)
            with dve.Fori(1, NT // 2 - 1) as q:
                paired(q, 0)
                paired(q, 1)
            paired(NT // 2 - 1, 0)
            paired(NT // 2 - 1, 1)
            rotate(NT - 1, 1, NT // 2 - 1)
            q_lo(NT - 1, 1)

        @block.tensor
        def _(pe):
            pe.wait_ge(s_const, 16)
            for n in range(RT):
                pe.wait_ge(s_w[n % 2], 16 * (n // 2 + 1))
                for half in range(2):
                    after(pe, s_lo, 2 * n + half - 1)
                    for k in range(4):
                        kk = half * 4 + k
                        ins = pe.transpose(pt[:, half, k * P:(k + 1) * P], wnat[:, n % 2, kk * P:(kk + 1) * P], ident[:])
                    ins.then_inc(s_pt, 1)

            def x_turn(m, par):
                pe.wait_ge(s_xn, m + 1)
                for half in range(2):
                    pe.wait_ge(s_lo, W0 + 2 * m + half - 1)
                    for k in range(4):
                        kk = half * 4 + k
                        ins = pe.transpose(pt[:, half, k * P:(k + 1) * P], xn[:, par, kk * P:(kk + 1) * P], ident[:])
                    ins.then_inc(s_pt, 1)

            def products(m, par, g):
                after(pe, s_rd, 3 * m + g - 2)
                if g == 2:
                    after(pe, s_v, m)
                for k in range(DK):
                    for j, (xi, wi) in enumerate(((0, 0), (0, 1), (1, 0))):
                        ins = pe.matmul(pq[:, g, :], xt[:, par, xi, k, :], wt[:, wi, k, 512 * g:512 * (g + 1)],
                                        start=(k == 0 and j == 0), stop=(k == DK - 1 and j == 2))
                ins.then_inc(s_mm, 1)

            def q_turn(m):
                for g in range(3):
                    pe.wait_ge(s_qr, 3 * m + g + 1)
                    after(pe, s_qlo, 3 * m + g - 2)
                    for j in range(width[g] // P):
                        c0 = 512 * g + j * P
                        ins = pe.transpose(pr[:, g, j * P:(j + 1) * P], qr[:, c0:c0 + P], ident[:])
                    ins.then_inc(s_qt, 1)
            x_turn(0, 0)

            def step(m, par):
                if not known(m, lambda k: k >= NT - 1):
                    x_turn(m + 1, 1 - par)
                pe.wait_ge(s_lo, W0 + 2 * m + 2)
                products(m, par, 0)
                if not known(m, lambda k: k == 0):
                    q_turn(m - 1)
                products(m, par, 1)
                products(m, par, 2)
            tile_loop(pe, step)
            q_turn(NT - 1)


def attention(nc, qk_dram, v_dram, ident_dram, causal_dram, edge_dram, older_dram, keyrows_dram, o_dram):
    QT = SEQ // P
    NC = SEQ // CHUNK
    LATE = 2
    SUMS = HD + 1
    N = BATCH * NKV
    AT = [0, 512, 896, 1152]
    with ExitStack() as ctx:
        m_ = Pool(nc, ctx, "at")
        identf = m_.sb("identf", [P, P])
        identb = m_.sb("identb", [P, P], BF16)
        causal = m_.sb("causal", [P, P])
        causalb = m_.sb("causalb", [P, P], BF16)
        edgef = m_.sb("edgef", [P, P])
        edge = m_.sb("edge", [P, P], BF16)
        older = m_.sb("older", [P, 4, 16])
        ka = m_.sb("ka", [P, 2, SEQ], F32R)
        qa = m_.sb("qa", [P, 2, GROUP, SEQ], F32R)
        vg = m_.sb("vg", [P, 2, QT, SUMS])
        cm = m_.sb("cm", [P, GROUP, NC])
        m8 = m_.sb("m8", [P, GROUP, 8])
        left = m_.sb("left", [P, GROUP, NC])
        pen = m_.sb("pen", [P, GROUP, 16])
        own = m_.sb("own", [P, GROUP, 16])
        ownsum = m_.sb("ownsum", [P, GROUP])
        mh = m_.sb("mh", [P, GROUP], F32R)
        added = m_.sb("added", [P, QT, GROUP, P])
        edgepen = m_.sb("edgepen", [P, 2, GROUP, P], BF16)
        prob = m_.sb("prob", [P, 2, GROUP, 1280])
        rec = m_.sb("rec", [P, GROUP])
        o = m_.sb("o", [P, 2, QT, GROUP * HD])
        psc = m_.ps("psc", [P, GROUP, 512])
        pa = m_.ps("pa", [P, GROUP, P])
        pst = m_.ps("pst", [P, 2, 512])
        po = m_.ps("po", [P, 512])
        s_const, s_cast, s_init = m_.sem("const"), m_.sem("cast"), m_.sem("init")
        s_keyrow = m_.sem("keyrow")
        s_ld = [m_.sem("ld0"), m_.sem("ld1")]
        s_seq = m_.sem("vector_seq")
        s_passed, s_ppassed = m_.sem("passed"), m_.sem("pool_passed")
        s_sc, s_cm, s_add = m_.sem("scores"), m_.sem("chunk_max"), m_.sem("added")
        s_pa, s_qa = m_.sem("added_turned"), m_.sem("added_placed")
        s_st, s_p, s_dg = m_.sem("scores_t"), m_.sem("prob"), m_.sem("diagonal")
        s_pv, s_rec, s_o = m_.sem("values"), m_.sem("rec"), m_.sem("o")
        s_out = [m_.sem("out0"), m_.sem("out1")]
        LINKS = [3, 3, 9, 9]
        PER = sum(LINKS)

        block = ctx.enter_context(nc.Block())

        def groups(eng, step, head=1, tail=1):
            for q in range(head):
                step(2 * q, 0, q)
                step(2 * q + 1, 1, q)
            with eng.Fori(head, N // 2 - tail) as q:
                step(2 * q, 0, q)
                step(2 * q + 1, 1, q)
            for q in range(N // 2 - tail, N // 2):
                step(2 * q, 0, q)
                step(2 * q + 1, 1, q)

        q_rows = qk_dram[:, 0:NHEAD * HD, :].rearrange("a (g h r) (b t) -> a r b g h t", g=NKV, h=GROUP, b=BATCH)
        k_rows = qk_dram[:, NHEAD * HD:QKW, :].rearrange("a (g r) (b t) -> a r b g t", g=NKV, b=BATCH)
        v_rows = v_dram.rearrange("(b j p) (g r) -> p b g j r", b=BATCH, j=QT, g=NKV)
        o_rows = o_dram.rearrange("(b j p) (g c) -> p b g j c", b=BATCH, j=QT, g=NKV)

        @block.sync
        def _(sp):
            for dst, src in ((identf[:], ident_dram), (causal[:], causal_dram), (edgef[:], edge_dram),
                             (older[:], older_dram.rearrange("p (a c) -> p a c", a=4))):
                sp.dma_start(dst, src).then_inc(s_const, 16)
            sp.wait_ge(s_init, 2)

            def load(G, par, b, g):
                after(sp, s_pv, QT * (G - 1))
                for r, a in ((0, 0), (1, 0), (2, 1)):
                    sp.dma_start(ka[32 * r:32 * r + 32, par, :].bitcast(F32), k_rows[a, :, b, g, :]).then_inc(s_ld[par], 16)
                for r, a in ((0, 0), (1, 1), (2, 0)):
                    sp.dma_start(qa[32 * r:32 * r + 32, par, :, :].bitcast(F32), q_rows[a, :, b, g, :, :]).then_inc(s_ld[par], 16)
                sp.dma_start(vg[:, par, :, 0:HD], v_rows[:, b, g, :, :]).then_inc(s_ld[par], 16)

            for b in range(BATCH):
                if b == 0:
                    load(0, 0, 0, 0)
                    load(1, 1, 0, 1)
                with sp.Fori(1 if b == 0 else 0, NKV // 2) as q:
                    load(NKV * b + 2 * q, 0, b, 2 * q)
                    load(NKV * b + 2 * q + 1, 1, b, 2 * q + 1)

        @block.gpsimd
        def _(pool):
            pool.memset(added[:, :, :, :], 0.0).then_inc(s_init, 1)
            pool.memset(vg[:, :, :, HD:SUMS], 1.0).then_inc(s_init, 1)
            for par in range(2):
                pool.dma_start(ka[96:128, par, :], keyrows_dram).then_inc(s_keyrow, 16)

            def step(G, par, b, g):
                for j in range(QT):
                    gate(pool, s_p, 16 * G + 4 * j + 4, s_ppassed)
                    block_ = prob[:, par, :, AT[j]:AT[j] + P]
                    pool.affine_select(out=block_, in_=block_, pattern=[[0, GROUP], [1, P]], compare_op=ALU.is_ge,
                                       fill=0.0, base=0, channel_multiplier=-1).then_inc(s_dg, 1)
                pool.wait_ge(s_o, QT * (G + 1))
                pool.dma_start(o_rows[:, b, g, :, :], o[:, par, :, :]).then_inc(s_out[par], 16)
            for b in range(BATCH):
                if b == 0:
                    step(0, 0, 0, 0)
                    step(1, 1, 0, 1)
                with pool.Fori(1 if b == 0 else 0, NKV // 2) as q:
                    step(NKV * b + 2 * q, 0, b, 2 * q)
                    step(NKV * b + 2 * q + 1, 1, b, 2 * q + 1)
            for par in range(2):
                pool.wait_ge(s_out[par], 16 * N // 2)

        @block.scalar
        def _(act):
            act.wait_ge(s_const, 64)
            act.activation(identb[:], identf[:], ACT.Copy).then_inc(s_cast, 1)
            act.activation(causalb[:], causal[:], ACT.Copy).then_inc(s_cast, 1)
            act.activation(edge[:], edgef[:], ACT.Copy).then_inc(s_cast, 1)

            def place(G, par, t):
                act.wait_ge(s_pa, QT * G + t + 1)
                act.activation(qa[96:128, par, :, t * P:(t + 1) * P], pa[96:128, :, :], ACT.Copy).then_inc(s_qa, 1)

            def exps(G, par, j):
                for h in range(GROUP):
                    n = 16 * G + 4 * j + h
                    act.wait_ge(s_st, n + 1)
                    if h == 0 and j == 0:
                        after(act, s_pv, QT * (G - 1))
                    act.activation(prob[:, par, h, AT[j]:AT[j] + SEQ - j * P], pst[:, h % 2, 0:SEQ - j * P],
                                   ACT.Exp, scale=SCALE).then_inc(s_p, 1)
            for t in range(QT):
                place(0, 0, t)

            def step(G, par, q):
                nxt = not known(G, lambda k: k >= N - 1)
                exps(G, par, 0)
                if nxt:
                    place(G + 1, 1 - par, 0)
                exps(G, par, 1)
                if nxt:
                    place(G + 1, 1 - par, 1)
                exps(G, par, 2)
                if nxt:
                    place(G + 1, 1 - par, 2)
                exps(G, par, 3)
                if nxt:
                    place(G + 1, 1 - par, 3)
            groups(act, step)

        @block.vector
        def _(dve):
            dve.wait_ge(s_const, 64)
            dve.wait_ge(s_cast, 3)
            dve.wait_ge(s_init, 2)

            def rows(G, t):
                seq = Count(dve, s_seq, PER * G + sum(LINKS[:t]))
                nc_t = (t + 1) * P // CHUNK
                gate(dve, s_sc, QT * G + t + 1, s_passed)
                dve.tensor_reduce(cm[:, :, 0:nc_t], psc[:, :, 0:(t + 1) * P].rearrange("p h (c k) -> p h c k", k=CHUNK),
                                  AX.X, ALU.max).then_inc(s_cm, 1)
                gate(dve, s_cm, QT * G + t + 1, s_passed)
                after(dve, s_pa, QT * (G - 1) + t + 1)
                mx = added[:, t, :, 96]
                seq.link(dve.tensor_reduce(mx, cm[:, :, 0:nc_t], AX.X, ALU.max, negate=True))
                seq.link(dve.tensor_copy(mh[:], mx))
                last = dve.tensor_tensor(added[:, t, :, 97], mx, mh[:].bitcast(F32), ALU.subtract)
                if t < LATE:
                    seq.link(last)
                    return
                L = t - LATE
                for h in range(GROUP):
                    ins = dve.max(out=m8[:, h, :], in_=cm[:, h, 0:nc_t])
                ins.then_inc(s_seq, 1)
                seq.n = seq.n + 1
                gate(dve, s_seq, seq.n, s_passed)
                for h in range(GROUP):
                    ins = dve.match_replace(out=left[:, h, 0:nc_t], in_to_replace=m8[:, h, :],
                                            in_values=cm[:, h, 0:nc_t], imm_value=3e38)
                seq.link(ins)
                seq.link(dve.tensor_scalar(pen[:], left[:, :, 8:24], 1e38, -BIG, ALU.is_lt, ALU.mult))
                seq.link(dve.tensor_tensor(own[:], pen[:], older[:, 2 + L, :].unsqueeze(1).to_broadcast([P, GROUP, 16]), ALU.mult))
                seq.link(dve.tensor_tensor(added[:, t, :, 98:114], pen[:], older[:, L, :].unsqueeze(1).to_broadcast([P, GROUP, 16]), ALU.mult))
                seq.link(dve.tensor_reduce(ownsum[:], own[:], AX.X, ALU.add))
                after(dve, s_st, 16 * G - 8 + 4 * L)
                for h in range(GROUP):
                    ins = dve.tensor_scalar(edgepen[:, L, h, :], edge[:], ownsum[:, h:h + 1], None, ALU.mult)
                seq.link(ins)

            def outputs(G, par, t, pair):
                dve.wait_ge(s_pv, QT * G + t + 1)
                if t == 0:
                    after(dve, s_out[par], 16 * pair)
                pv = po[:, 0:GROUP * SUMS].rearrange("p (h c) -> p h c", h=GROUP)
                dve.reciprocal(rec[:], pv[:, :, HD]).then_inc(s_rec, 1)
                dve.wait_ge(s_rec, QT * G + t + 1)
                dve.tensor_tensor(o[:, par, t, :].rearrange("p (h c) -> p h c", h=GROUP), pv[:, :, 0:HD],
                                  rec[:].unsqueeze(2).to_broadcast([P, GROUP, HD]), ALU.mult).then_inc(s_o, 1)
            for t in range(QT):
                rows(0, t)

            def step(G, par, q):
                nxt = not known(G, lambda k: k >= N - 1)
                for t in range(QT):
                    if nxt:
                        rows(G + 1, t)
                    if t:
                        outputs(G, par, t - 1, q)
                outputs(G, par, QT - 1, q)
            groups(dve, step)

        @block.tensor
        def _(pe):
            pe.wait_ge(s_cast, 3)
            pe.wait_ge(s_keyrow, 32)

            def scores(G, par, t, pair):
                if t == 0:
                    pe.wait_ge(s_ld[par], 112 * (pair + 1))
                after(pe, s_cm, QT * G + t)
                for h in range(GROUP):
                    pe.matmul(psc[:, h, 0:(t + 1) * P], qa[0:96, par, h, t * P:(t + 1) * P], ka[0:96, par, 0:(t + 1) * P],
                              start=True, stop=False)
                    ins = pe.matmul(psc[:, h, t * P:(t + 1) * P], identb[:], causalb[:], start=False, stop=True)
                ins.then_inc(s_sc, 1)

            def turn(G, t):
                pe.wait_ge(s_seq, PER * G + sum(LINKS[:t + 1]))
                after(pe, s_qa, QT * G + t)
                for h in range(GROUP):
                    ins = pe.transpose(pa[:, h, :], added[:, t, h, :], identf[:])
                ins.then_inc(s_pa, 1)

            def scores_t(G, par, j):
                pe.wait_ge(s_qa, QT * (G + 1))
                for h in range(GROUP):
                    n = 16 * G + 4 * j + h
                    after(pe, s_p, n - 1)
                    edged = 1 <= j <= 2
                    ins = pe.matmul(pst[:, h % 2, 0:SEQ - j * P], ka[:, par, j * P:(j + 1) * P], qa[:, par, h, j * P:SEQ],
                                    start=True, stop=not edged)
                    if edged:
                        ins = pe.matmul(pst[:, h % 2, P:2 * P], edgepen[:, j - 1, h, :], identb[:], start=False, stop=True)
                    ins.then_inc(s_st, 1)

            def values(G, par, t):
                pe.wait_ge(s_dg, QT * G + t + 1)
                after(pe, s_o, QT * G + t)
                for h in range(GROUP):
                    for j in range(t + 1):
                        c0 = AT[j] + (t - j) * P
                        ins = pe.matmul(po[:, h * SUMS:(h + 1) * SUMS], prob[:, par, h, c0:c0 + P], vg[:, par, j, :],
                                        start=(j == 0), stop=(j == t))
                ins.then_inc(s_pv, 1)
            for t in range(QT):
                scores(0, 0, t, 0)
                turn(0, t)

            def step(G, par, q):
                nxt = not known(G, lambda k: k >= N - 1)
                npair = q + 1 if par else q

                def ahead(f, *a):
                    if nxt:
                        f(G + 1, *a)
                ahead(scores, 1 - par, 0, npair)
                scores_t(G, par, 0)
                ahead(turn, 0)
                ahead(scores, 1 - par, 1, npair)
                scores_t(G, par, 1)
                ahead(turn, 1)
                ahead(scores, 1 - par, 2, npair)
                values(G, par, 0)
                scores_t(G, par, 2)
                ahead(turn, 2)
                ahead(scores, 1 - par, 3, npair)
                values(G, par, 1)
                scores_t(G, par, 3)
                values(G, par, 2)
                values(G, par, 3)
                ahead(turn, 3)
            groups(pe, step)


def output(nc, o_dram, x_dram, wo, ident_dram, y_dram):
    NT, RT = T // P, D // P
    W0 = 2 * RT
    with ExitStack() as ctx:
        m_ = Pool(nc, ctx, "ou")
        ident = m_.sb("ident", [P, P])
        wnat = m_.sb("wnat", [P, 2, D])
        wt = m_.sb("wt", [P, 2, DK, D], F32R)
        o = m_.sb("o", [P, 2, D])
        x = m_.sb("x", [P, 2, D])
        xt = m_.sb("xt", [P, 2, 2, DK, P], F32R)
        y = m_.sb("y", [P, 2, D])
        pt = m_.ps("pt", [P, 2, 512])
        py = m_.ps("py", [P, 4, 512])
        s_const = m_.sem("const")
        s_w = [m_.sem("w0"), m_.sem("w1")]
        s_x = [m_.sem("x0"), m_.sem("x1")]
        s_pt, s_hi, s_lo = m_.sem("transposed"), m_.sem("hi"), m_.sem("lo")
        s_mm, s_y = m_.sem("products"), m_.sem("y")
        s_out = [m_.sem("out0"), m_.sem("out1")]
        block = ctx.enter_context(nc.Block())

        @block.sync
        def _(sp):
            sp.dma_start(ident[:], ident_dram).then_inc(s_const, 16)
            for n in range(RT):
                after(sp, s_pt, 2 * (n - 1))
                sp.dma_start(wnat[:, n % 2, :], wo[n * P:(n + 1) * P, :]).then_inc(s_w[n % 2], 16)

            def step(m, par):
                after(sp, s_pt, W0 + 2 * m - 2 if not known(m, lambda k: k < 2) else 0)
                sp.dma_start(o[:, par, :], o_dram[bass.ds(m * P, P), :]).then_inc(s_x[par], 16)
                after(sp, s_y, 2 * m - 2)
                sp.dma_start(x[:, par, :], x_dram[bass.ds(m * P, P), :]).then_inc(s_x[par], 16)
            tile_loop(sp, step)

        @block.gpsimd
        def _(pool):
            def step(m, par):
                pool.wait_ge(s_y, 2 * m + 2)
                pool.dma_start(y_dram[bass.ds(m * P, P), :], y[:, par, :]).then_inc(s_out[par], 16)
            tile_loop(pool, step)
            for par in range(2):
                pool.wait_ge(s_out[par], 16 * NT // 2)

        @block.scalar
        def _(act):
            for n in range(RT):
                for half in range(2):
                    act.wait_ge(s_pt, 2 * n + half + 1)
                    act.activation(wt[:, 0, half * 4:half * 4 + 4, n * P:(n + 1) * P],
                                   pt[:, half, :].rearrange("p (k n) -> p k n", k=4), ACT.Copy).then_inc(s_hi, 1)

            def step(m, par):
                after(act, s_mm, 2 * m - 2)
                for half in range(2):
                    act.wait_ge(s_pt, W0 + 2 * m + half + 1)
                    act.activation(xt[:, par, 0, half * 4:half * 4 + 4, :],
                                   pt[:, half, :].rearrange("p (k n) -> p k n", k=4), ACT.Copy).then_inc(s_hi, 1)
            tile_loop(act, step)

        @block.vector
        def _(dve):
            for n in range(RT):
                for half in range(2):
                    dve.wait_ge(s_hi, 2 * n + half + 1)
                    ks, cs = slice(half * 4, half * 4 + 4), slice(n * P, (n + 1) * P)
                    dve.tensor_tensor(wt[:, 1, ks, cs], pt[:, half, :].rearrange("p (k n) -> p k n", k=4),
                                      wt[:, 0, ks, cs].bitcast(F32), ALU.subtract).then_inc(s_lo, 1)

            def x_lo(m, par):
                for half in range(2):
                    dve.wait_ge(s_hi, W0 + 2 * m + half + 1)
                    dve.tensor_tensor(xt[:, par, 1, half * 4:half * 4 + 4, :], pt[:, half, :].rearrange("p (k n) -> p k n", k=4),
                                      xt[:, par, 0, half * 4:half * 4 + 4, :].bitcast(F32), ALU.subtract).then_inc(s_lo, 1)
            x_lo(0, 0)

            def paired(q, u):
                m = 2 * q + u
                if not known(m, lambda k: k >= NT - 1):
                    x_lo(m + 1, 1 - u)
                dve.wait_ge(s_x[u], 32 * q + 32)
                after(dve, s_out[u], 16 * q)
                for half in range(2):
                    cols = slice(half * 512, (half + 1) * 512)
                    dve.wait_ge(s_mm, 2 * m + half + 1)
                    dve.tensor_tensor(y[:, u, cols], py[:, 2 * u + half, :], x[:, u, cols], ALU.add).then_inc(s_y, 1)
            paired(0, 0)
            paired(0, 1)
            with dve.Fori(1, NT // 2 - 1) as q:
                paired(q, 0)
                paired(q, 1)
            paired(NT // 2 - 1, 0)
            paired(NT // 2 - 1, 1)

        @block.tensor
        def _(pe):
            pe.wait_ge(s_const, 16)
            for n in range(RT):
                pe.wait_ge(s_w[n % 2], 16 * (n // 2 + 1))
                for half in range(2):
                    after(pe, s_lo, 2 * n + half - 1)
                    for k in range(4):
                        kk = half * 4 + k
                        ins = pe.transpose(pt[:, half, k * P:(k + 1) * P], wnat[:, n % 2, kk * P:(kk + 1) * P], ident[:])
                    ins.then_inc(s_pt, 1)

            def x_turn(m, par, pair):
                pe.wait_ge(s_x[par], 32 * pair + 32)
                for half in range(2):
                    pe.wait_ge(s_lo, W0 + 2 * m + half - 1)
                    for k in range(4):
                        kk = half * 4 + k
                        ins = pe.transpose(pt[:, half, k * P:(k + 1) * P], o[:, par, kk * P:(kk + 1) * P], ident[:])
                    ins.then_inc(s_pt, 1)

            def products(m, par):
                pe.wait_ge(s_lo, W0 + 2 * m + 2)
                after(pe, s_y, 2 * m - 2)
                for half in range(2):
                    for k in range(DK):
                        for j, (xi, wi) in enumerate(((0, 0), (0, 1), (1, 0))):
                            ins = pe.matmul(py[:, 2 * par + half, :], xt[:, par, xi, k, :],
                                            wt[:, wi, k, 512 * half:512 * (half + 1)],
                                            start=(k == 0 and j == 0), stop=(k == DK - 1 and j == 2))
                    ins.then_inc(s_mm, 1)
            x_turn(0, 0, 0)

            def paired(q, u):
                m = 2 * q + u
                if not known(m, lambda k: k >= NT - 1):
                    x_turn(m + 1, 1 - u, q + u)
                products(m, u)
            paired(0, 0)
            paired(0, 1)
            with pe.Fori(1, NT // 2 - 1) as q:
                paired(q, 0)
                paired(q, 1)
            paired(NT // 2 - 1, 0)
            paired(NT // 2 - 1, 1)


def kernel(**inputs):
    import numpy as np
    import concourse.bacc as bacc
    from concourse.bass_utils import run_bass_kernel_spmd

    nc = bacc.Bacc("TRN2", target_bir_lowering=False, num_devices=1)
    arrays, t = {}, {}
    host = {k: np.ascontiguousarray(v) for k, v in inputs.items()}
    half = HD // 2
    inv = (np.float32(1.0) / np.power(np.float32(10000.0), np.arange(0, HD, 2, dtype=np.float32) / np.float32(HD))).astype(np.float32)
    freq = np.arange(SEQ, dtype=np.float32)[:, None] * inv[None, :]
    sin = np.sin(freq).astype(np.float32)
    host["rope"] = np.concatenate([np.cos(freq), np.cos(freq), -sin, sin], axis=1).astype(np.float32)
    host["rope"] = np.tile(host["rope"], (BATCH, 1))
    host["ident"] = np.eye(P, dtype=np.float32)
    q, k = np.arange(P)[:, None], np.arange(P)[None, :]
    host["causal"] = np.where(k > q, np.float32(-BIG), np.float32(0.0))
    host["edge"] = ((k <= q) & (k // CHUNK == q // CHUNK)).astype(np.float32)
    c = np.arange(CHUNK)[None, :]
    rel = np.arange(P)[:, None] // CHUNK
    host["older"] = np.concatenate([(c < rel), (c < rel + 8), (c == rel), (c == rel + 8)], axis=1).astype(np.float32)
    key = np.arange(SEQ)
    rows = np.zeros((32, SEQ), np.float32)
    rows[0:2] = 1.0
    for j in range(16):
        rows[2 + j] = key // CHUNK == 8 + j
    host["keyrows"] = rows
    for name, a in host.items():
        arrays[name] = a
        t[name] = nc.dram_tensor(name, a.shape, mybir.dt.from_np(a.dtype), kind="ExternalInput").ap()
    out = nc.dram_tensor("out", (BATCH, SEQ, D), F32, kind="ExternalOutput").ap()
    program(nc, t, out)
    r = run_bass_kernel_spmd(nc, [arrays], core_ids=[0])
    return r.results[0]["out"]


def program(nc, t, out):
    def scratch(name, shape, dt=F32):
        return nc.dram_tensor(name, shape, dt, kind="Internal").ap()
    wup = scratch("wup", (NCH, P, 4 * 1024))
    wdn = scratch("wdn", (NCH, P, 4 * 1024))
    dequantise(nc, t["L0_ffn_w_up_codes"], t["L0_ffn_w_up_absmax"], t["L0_ffn_w_up_lora_a"], t["L0_ffn_w_up_lora_b"],
               t["L0_ffn_w_down_codes"], t["L0_ffn_w_down_absmax"], t["L0_ffn_w_down_lora_a"], t["L0_ffn_w_down_lora_b"],
               t["ident"], wup, wdn)
    x1, x2, o = scratch("x1", (T, D)), scratch("x2", (T, D)), scratch("o", (T, D))
    qk, v = scratch("qk", (2, QKW, T)), scratch("v", (T, NKV * HD))
    x0 = t["L0_attn_hidden_states"].rearrange("b s d -> (b s) d")
    y = out.rearrange("b s d -> (b s) d")
    b_up, b_down, ident = t["L0_ffn_b_up"], t["L0_ffn_b_down"], t["ident"]
    ffn(nc, "f1", x0, x1, b_up, b_down, ident, wup, wdn)
    qkv(nc, x1, (t["L0_attn_wq"], t["L0_attn_wk"], t["L0_attn_wv"]), ident, t["rope"], qk, v)
    attention(nc, qk, v, ident, t["causal"], t["edge"], t["older"], t["keyrows"], o)
    output(nc, o, x1, t["L0_attn_wo"], ident, x2)
    ffn(nc, "f2", x2, y, b_up, b_down, ident, wup, wdn)
```

```python
from contextlib import ExitStack

import concourse.bass as bass
from concourse import mybir

F32 = mybir.dt.float32
F32R = mybir.dt.float32r
BF16 = mybir.dt.bfloat16
I16 = mybir.dt.int16
ALU = mybir.AluOpType
ACT = mybir.ActivationFunctionType
AX = mybir.AxisListType

P = 128
NF4 = [-1.0, -0.6961928009986877, -0.5250730514526367, -0.39491748809814453, -0.28444138169288635,
       -0.18477343022823334, -0.09105003625154495, 0.0, 0.07958029955625534, 0.16093020141124725,
       0.24611230194568634, 0.33791524171829224, 0.44070982933044434, 0.5626170039176941,
       0.7229568362236023, 1.0]
QBLK = 64
D = 1024
DK = D // P
H = 2752
RANK = 16
CH = 256
NCH = -(-H // CH)
HT = NCH * CH // P
LAST = H - (NCH - 1) * CH
BATCH, SEQ = 4, 512
T = BATCH * SEQ
TB = 1024
NTB = T // TB
TM = TB // P
EPS = 1e-5
NHEAD, NKV, HD = 32, 8, 32
GROUP = NHEAD // NKV
QKW = (NHEAD + NKV) * HD
QKVW = (NHEAD + 2 * NKV) * HD
CHUNK = 16
BIG = 1e30
SCALE = float(HD) ** -0.5


def after(eng, sem, n):
    if not (isinstance(n, int) and n <= 0):
        eng.wait_ge(sem, n)


def gate(eng, sem, n, passed):
    after(eng, sem, n)
    if not isinstance(n, int):
        eng.sem_inc(passed, 1)


class Pool:

    def __init__(self, nc, ctx, tag):
        self.nc, self.ctx, self.tag = nc, ctx, tag

    def sb(self, name, shape, dt=F32):
        return self.ctx.enter_context(self.nc.sbuf_tensor(f"{self.tag}_{name}", shape, dt))

    def ps(self, name, shape, dt=F32):
        return self.ctx.enter_context(self.nc.psum_tensor(f"{self.tag}_{name}", shape, dt))

    def sem(self, name):
        return self.ctx.enter_context(self.nc.semaphore(f"{self.tag}_{name}"))


def leaf(i):
    import numpy as np
    lo, hi = np.float32(NF4[2 * i]), np.float32(NF4[2 * i + 1])
    s = np.float32(hi - lo)
    for cand in (s, np.nextafter(s, np.float32(4)), np.nextafter(s, np.float32(-4))):
        if np.float32(np.float64(cand) + np.float64(lo)) == hi:
            return float(cand), float(lo)
    raise AssertionError(i)


def dequantise(nc, up_codes, up_absmax, up_a, up_b, dn_codes, dn_absmax, dn_a, dn_b, ident_dram,
               wup_dram, wdn_dram):
    SUB, PART = 4, 512
    with ExitStack() as ctx:
        m = Pool(nc, ctx, "dq")
        ident = m.sb("ident", [P, P])
        codes = m.sb("codes", [P, 2, SUB * PART], I16)
        bits = m.sb("bits", [P, 2, 4, SUB * PART], I16)
        amax_up = m.sb("amax_up", [P, HT, D // QBLK])
        amax_dn = m.sb("amax_dn", [P, DK, NCH * CH // QBLK])
        even = m.sb("even", [P, 2, 4, PART])
        wnat = m.sb("wnat", [P, 2, PART])
        stage = m.sb("stage", [P, 2, 2, SUB * PART], F32R)
        a_nat = m.sb("a_nat", [P, DK, RANK])
        dna_nat = m.sb("dna_nat", [P, HT, RANK])
        upa_t = m.sb("upa_t", [RANK, D])
        upb = m.sb("upb", [RANK, NCH * CH])
        dna_t = m.sb("dna_t", [RANK, NCH * CH])
        dnb = m.sb("dnb", [RANK, D])
        upb_c = m.sb("upb_c", [RANK, 2, CH])
        dna_c = m.sb("dna_c", [RANK, 2, CH])
        ps = m.ps("ps", [P, 8, PART])
        s_in = m.sem("in")
        s_passed = m.sem("passed")
        s_zero = m.sem("zero")
        s_code = [m.sem("code_up"), m.sem("code_dn")]
        s_lt, s_ltc = m.sem("lora_t"), m.sem("lora_copied")
        s_chunk = m.sem("lora_chunk")
        s_bits, s_leaf, s_sel = m.sem("bits"), m.sem("leaf"), m.sem("selected")
        s_w, s_tr, s_hi, s_lo = m.sem("scaled"), m.sem("transposed"), m.sem("hi"), m.sem("lo")
        s_out = [m.sem("out_up"), m.sem("out_dn")]

        code_up = up_codes.rearrange("(h d) -> h d", d=D)
        code_dn = dn_codes.rearrange("(k p h) -> p k h", p=P, h=H)
        abs_up = up_absmax.rearrange("(h b) -> h b", b=D // QBLK)
        abs_dn = dn_absmax.rearrange("(k p b) -> p k b", p=P, b=H // QBLK)
        FULL = H // P
        REST = H - FULL * P

        def part_in(kind, e):
            bank = ps[:, 4 + e % 2, :]
            if kind == 0:
                return bank.rearrange("p (k h) -> p k h", k=4)
            return bank.rearrange("p (k t d) -> p t k d", k=2, t=2)

        def part_out(kind, s, hl):
            if kind == 0:
                t, half = s // 2, s % 2
                return stage[:, 0, hl, :].rearrange("p (k h) -> p k h", k=DK)[:, half * 4:half * 4 + 4, t * P:(t + 1) * P]
            return stage[:, 1, hl, :].rearrange("p (t k d) -> p t k d", t=2, k=DK)[:, :, 2 * s:2 * s + 2, :]

        def order(e):
            return e // SUB, e % SUB

        def steps(eng, step):
            step(0, 0)
            with eng.Fori(1, NCH - 3, 2) as c:
                step(c, 1)
                step(c + 1, 0)
            for c in range(NCH - 2, NCH):
                step(c, c % 2)

        block = ctx.enter_context(nc.Block())

        @block.sync
        def _(sp):
            sp.dma_start(ident[:], ident_dram).then_inc(s_in, 16)
            sp.dma_start(a_nat[:], up_a.rearrange("(k p) r -> p k r", p=P)).then_inc(s_in, 16)
            sp.wait_ge(s_zero, 4)
            sp.dma_start(dna_nat[:, 0:FULL, :], dn_a[0:FULL * P, :].rearrange("(k p) r -> p k r", p=P)).then_inc(s_in, 16)
            sp.dma_start(dna_nat[0:REST, FULL, :], dn_a[FULL * P:H, :]).then_inc(s_in, 16)
            sp.dma_start(upb[:, 0:H], up_b).then_inc(s_in, 16)
            sp.dma_start(dnb[:], dn_b).then_inc(s_in, 16)
            sp.dma_start(amax_up[:, 0:FULL, :], abs_up[0:FULL * P, :].rearrange("(k p) b -> p k b", p=P)).then_inc(s_in, 16)
            sp.dma_start(amax_up[0:REST, FULL, :], abs_up[FULL * P:H, :]).then_inc(s_in, 16)
            sp.dma_start(amax_dn[:, :, 0:H // QBLK], abs_dn).then_inc(s_in, 16)

            def step(c, par):
                for kind, dram in ((0, wup_dram), (1, wdn_dram)):
                    sp.wait_ge(s_lo, c * 8 + 4 * (kind + 1))
                    sp.dma_start(dram[bass.ds(c, 1), :, :].rearrange("o p n -> (o p) n"),
                                 stage[:, kind, :, :].rearrange("p a n -> p (a n)").bitcast(F32)).then_inc(s_out[kind], 16)
            steps(sp, step)
            for kind in range(2):
                sp.wait_ge(s_out[kind], 16 * NCH)

        @block.gpsimd
        def _(pool):
            for tile in (amax_up[:, FULL, :], amax_dn[:, :, H // QBLK:], dna_nat[:, FULL, :], upb[:, H:]):
                pool.memset(tile, 0.0).then_inc(s_zero, 1)

            def load(c, kind):
                if kind == 0:
                    src = code_up[bass.ds(c * CH, CH), :].rearrange("(t p) d -> p t d", p=P)
                    pool.dma_start(codes[:, 0, :].rearrange("p (t d) -> p t d", t=2), src).then_inc(s_code[0], 16)
                else:
                    pool.dma_start(codes[:, 1, :].rearrange("p (k h) -> p k h", k=DK),
                                   code_dn[:, :, bass.ds(c * CH, CH)]).then_inc(s_code[1], 16)

            def load_last(kind):
                c0 = (NCH - 1) * CH
                if kind == 0:
                    pool.dma_start(codes[:, 0, 0:D], code_up[c0:c0 + P, :]).then_inc(s_code[0], 16)
                    pool.dma_start(codes[0:REST, 0, D:2 * D], code_up[c0 + P:H, :]).then_inc(s_code[0], 16)
                else:
                    pool.dma_start(codes[:, 1, :].rearrange("p (k h) -> p k h", k=DK)[:, :, 0:LAST],
                                   code_dn[:, :, c0:H]).then_inc(s_code[1], 16)

            load(0, 0)
            load(0, 1)
            pool.wait_ge(s_in, 16 * 9)
            pool.wait_ge(s_ltc, 2)

            def step(c, par):
                after(pool, s_tr, c * 8 - 8)
                pool.tensor_copy(upb_c[:, par, :], upb[:, bass.ds(c * CH, CH)]).then_inc(s_chunk, 1)
                pool.tensor_copy(dna_c[:, par, :], dna_t[:, bass.ds(c * CH, CH)]).then_inc(s_chunk, 1)
                for e in range(8):
                    kind, s = order(e)
                    n = c * 8 + e
                    pool.wait_ge(s_sel, 7 * n + 7)
                    after(pool, s_tr, n - 1)
                    if kind == 0:
                        t, half = s // 2, s % 2
                        am = amax_up[:, bass.ds(c * 2 + t, 1), half * 8:half * 8 + 8].rearrange("p o b -> p (o b)")\
                            .unsqueeze(2).to_broadcast([P, 8, QBLK])
                        pool.tensor_tensor(wnat[:, e % 2, :].rearrange("p (b q) -> p b q", q=QBLK),
                                           even[:, e % 2, 0, :].rearrange("p (b q) -> p b q", q=QBLK),
                                           am, ALU.mult).then_inc(s_w, 1)
                    else:
                        am = amax_dn[:, 2 * s:2 * s + 2, bass.ds(c * 4, 4)].unsqueeze(3).to_broadcast([P, 2, 4, QBLK])
                        pool.tensor_tensor(wnat[:, e % 2, :].rearrange("p (k b q) -> p k b q", k=2, q=QBLK),
                                           even[:, e % 2, 0, :].rearrange("p (k b q) -> p k b q", k=2, q=QBLK),
                                           am, ALU.mult).then_inc(s_w, 1)
                    if s == 0 and not (isinstance(c, int) and c == NCH - 1):
                        pool.wait_ge(s_bits, c * 2 + kind + 1)
                        if isinstance(c, int) and c == NCH - 2:
                            load_last(kind)
                        else:
                            load(c + 1, kind)
            steps(pool, step)

        @block.scalar
        def _(act):
            act.wait_ge(s_lt, 1)
            act.activation(upa_t[:], ps[0:RANK, 0:2, :].rearrange("p a n -> p (a n)"), ACT.Copy).then_inc(s_ltc, 1)
            act.activation(dna_t[:], ps[0:RANK, 2:8, :].rearrange("p a n -> p (a n)")[:, 0:NCH * CH], ACT.Copy).then_inc(s_ltc, 1)

            def leaves(c, e):
                kind, s = order(e)
                n = c * 8 + e
                if s == 0:
                    act.wait_ge(s_bits, c * 2 + kind + 1)
                bit = bits[:, kind, 0, s * PART:(s + 1) * PART]
                for i in range(4):
                    after(act, s_sel, 7 * n - 6 + i)
                    sc, off = leaf(2 * i + 1)
                    act.activation(ps[:, i, :], bit, ACT.Copy, scale=sc, bias=off).then_inc(s_leaf, 1)
                    if i == 0:
                        after(act, s_w, n - 1)
                    sc, off = leaf(2 * i)
                    act.activation(even[:, e % 2, i, :], bit, ACT.Copy, scale=sc, bias=off).then_inc(s_leaf, 1)

            def hi(c, e):
                kind, s = order(e)
                n = c * 8 + e
                act.wait_ge(s_tr, n + 1)
                if s == 0:
                    after(act, s_out[kind], c * 16)
                act.activation(part_out(kind, s, 0), part_in(kind, e), ACT.Copy).then_inc(s_hi, 1)

            def step(c, par):
                for e in range(8):
                    leaves(c, e)
                    if e >= 2:
                        hi(c, e - 2)
                    elif not (isinstance(c, int) and c == 0):
                        hi(c - 1, e + 6)
            act.wait_ge(s_ltc, 2)
            steps(act, step)
            hi(NCH - 1, 6)
            hi(NCH - 1, 7)

        @block.vector
        def _(dve):
            def lo(c, e):
                kind, s = order(e)
                dve.wait_ge(s_hi, c * 8 + e + 1)
                hi_half = part_out(kind, s, 0)
                low, src = part_out(kind, s, 1), part_in(kind, e)
                if kind == 0:
                    dve.tensor_tensor(low, src, hi_half.bitcast(F32), ALU.subtract).then_inc(s_lo, 1)
                else:
                    dve.tensor_tensor(low, src, hi_half.bitcast(F32), ALU.subtract).then_inc(s_lo, 1)

            def step(c, par):
                for e in range(8):
                    kind, s = order(e)
                    n = c * 8 + e
                    if s == 0:
                        last = isinstance(c, int) and c == NCH - 1 and kind == 0
                        dve.wait_ge(s_code[kind], c * 16 + (32 if last else 16))
                        after(dve, s_leaf, 8 * n - 32)
                        for b in range(3, -1, -1):
                            ins = dve.tensor_scalar(bits[:, kind, b, :], codes[:, kind, :], 1 << b, None, ALU.bitwise_and)
                        ins.then_inc(s_bits, 1)
                        dve.wait_ge(s_bits, c * 2 + kind + 1)
                    cols = slice(s * PART, (s + 1) * PART)
                    ev = even[:, e % 2, :, :]
                    for i in range(4):
                        gate(dve, s_leaf, 8 * n + 2 * i + 2, s_passed)
                        dve.copy_predicated(ev[:, i, :], bits[:, kind, 1, cols], ps[:, i, :]).then_inc(s_sel, 1)
                    for k, (a, b, bit) in enumerate(((0, 1, 2), (2, 3, 2), (0, 2, 3))):
                        gate(dve, s_sel, 7 * n + (2, 4, 6)[k], s_passed)
                        dve.copy_predicated(ev[:, a, :], bits[:, kind, bit, cols], ev[:, b, :]).then_inc(s_sel, 1)
                    if e >= 2:
                        lo(c, e - 2)
                    elif not (isinstance(c, int) and c == 0):
                        lo(c - 1, e + 6)
            steps(dve, step)
            lo(NCH - 1, 6)
            lo(NCH - 1, 7)

        @block.tensor
        def _(pe):
            pe.wait_ge(s_in, 16 * 9)
            for k in range(DK):
                pe.transpose(ps[0:RANK, k // 4, (k % 4) * P:(k % 4 + 1) * P], a_nat[:, k, :], ident[:])
            for t in range(HT):
                ins = pe.transpose(ps[0:RANK, 2 + t // 4, (t % 4) * P:(t % 4 + 1) * P], dna_nat[:, t, :], ident[:])
            ins.then_inc(s_lt, 1)
            pe.wait_ge(s_ltc, 2)

            def step(c, par):
                pe.wait_ge(s_chunk, c * 2 + 2)
                for e in range(8):
                    kind, s = order(e)
                    n = c * 8 + e
                    pe.wait_ge(s_w, n + 1)
                    after(pe, s_lo, n - 1)
                    for j in range(4):
                        dst = ps[:, 4 + e % 2, j * P:(j + 1) * P]
                        pe.matmul(dst, wnat[:, e % 2, j * P:(j + 1) * P], ident[:], is_transpose=True, start=True, stop=False)
                        if kind == 0:
                            t, k = s // 2, (s % 2) * 4 + j
                            ins = pe.matmul(dst, upa_t[:, k * P:(k + 1) * P], upb_c[:, par, t * P:(t + 1) * P], start=False, stop=True)
                        else:
                            k, t = 2 * s + j // 2, j % 2
                            ins = pe.matmul(dst, dna_c[:, par, t * P:(t + 1) * P], dnb[:, k * P:(k + 1) * P], start=False, stop=True)
                    ins.then_inc(s_tr, 1)
            steps(pe, step)


class Count:

    def __init__(self, eng, sem, base=0):
        self.eng, self.sem, self.n = eng, sem, base

    def link(self, ins):
        ins.then_inc(self.sem, 1)
        self.n = self.n + 1
        self.eng.wait_ge(self.sem, self.n)


def inverse_root(dve, link, rstd, var, tmp):
    link(dve.tensor_tensor(tmp, rstd, rstd, ALU.mult))
    link(dve.tensor_tensor(tmp, tmp, var, ALU.mult))
    link(dve.tensor_scalar(tmp, tmp, -0.5, 1.5, ALU.mult, ALU.add))
    link(dve.tensor_tensor(rstd, rstd, tmp, ALU.mult))


def ffn(nc, tag, x_dram, y_dram, b_up, b_down, ident_dram, wup_dram, wdn_dram):
    NH = TB // 512
    UPG = 2 * NH
    DNG = TM * 2
    with ExitStack() as ctx:
        m = Pool(nc, ctx, tag)
        ident = m.sb("ident", [P, P])
        bup = m.sb("bup", [P, HT])
        bup_c = m.sb("bup_c", [P, 2, 2])
        bdn = m.sb("bdn", [P, D])
        y = m.sb("y", [P, TM, D])
        xn = m.sb("xn", [P, 2, 512])
        xt = m.sb("xt", [P, 2, DK, TB], F32R)
        wu = m.sb("wu", [P, 2, 2, DK, CH], F32R)
        wd = m.sb("wd", [P, 2, 2, 2, D], F32R)
        ht = m.sb("ht", [P, 2, 2, 2, TB], F32R)
        hraw = m.sb("hraw", [P, 2, 512])
        stats = m.sb("stats", [P, 2, 6])
        mv = m.sb("mv", [P, TM, 2])
        var = m.sb("var", [P, TM])
        rstd = m.sb("rstd", [P, TM])
        tmp = m.sb("tmp", [P, TM])
        pt = m.ps("pt", [P, 2, 512])
        pu = m.ps("pu", [P, 2, 512])
        pd = m.ps("pd", [P, 4, 512])
        s_const, s_x, s_store = m.sem("const"), m.sem("x"), m.sem("store")
        s_seq = m.sem("vector_seq")
        s_bdn, s_yi = m.sem("bdn"), m.sem("y_started")
        s_var, s_sd, s_xn = m.sem("var"), m.sem("sd"), m.sem("xn")
        s_pt, s_xhi, s_xlo = m.sem("x_transposed"), m.sem("x_hi"), m.sem("x_lo")
        s_wu = [m.sem("wu0"), m.sem("wu1")]
        s_wd = [m.sem("wd0"), m.sem("wd1")]
        s_upg, s_bc = m.sem("up_group"), m.sem("bias_chunk")
        s_raw, s_hhi, s_hlo = m.sem("h_raw"), m.sem("h_hi"), m.sem("h_lo")
        s_dng, s_y = m.sem("down_group"), m.sem("y_added")
        x_rows = x_dram.rearrange("(b m p) d -> b p m d", m=TM, p=P)
        y_rows = y_dram.rearrange("(b m p) d -> b p m d", m=TM, p=P)
        FULL = H // P

        block = ctx.enter_context(nc.Block())

        def loads_before(b, par):
            return b * ((NCH + 1) // 2 if par == 0 else NCH // 2)

        @block.sync
        def _(sp):
            sp.dma_start(ident[:], ident_dram).then_inc(s_const, 16)
            sp.dma_start(bdn[:], b_down.rearrange("(o d) -> o d", o=1).to_broadcast([P, D])).then_inc(s_const, 16)
            sp.wait_ge(s_bdn, 1)
            sp.dma_start(bup[:, 0:FULL], b_up[0:FULL * P].rearrange("(t p) -> p t", p=P), allow_slow_non_contiguous=True).then_inc(s_const, 16)
            sp.dma_start(bup[0:H - FULL * P, FULL:FULL + 1], b_up[FULL * P:H].rearrange("(p o) -> p o", o=1)).then_inc(s_const, 16)
            for b in range(NTB):
                after(sp, s_store, b * 16 * TM)
                for i in range(TM):
                    sp.dma_start(y[:, i, :], x_rows[b, :, i, :]).then_inc(s_x, 16)

                def load(c, par):
                    after(sp, s_upg, (b * NCH + c - 1) * UPG)
                    sp.dma_start(wu[:, par, :, :, :].rearrange("p a k h -> p (a k h)").bitcast(F32),
                                 wup_dram[bass.ds(c, 1), :, :].rearrange("o p n -> (o p) n")).then_inc(s_wu[par], 16)
                    after(sp, s_y, (b * NCH + c - 1) * DNG)
                    sp.dma_start(wd[:, par, :, :, :].rearrange("p a k h -> p (a k h)").bitcast(F32),
                                 wdn_dram[bass.ds(c, 1), :, :].rearrange("o p n -> (o p) n")).then_inc(s_wd[par], 16)
                load(0, 0)
                load(1, 1)
                with sp.Fori(1, NCH // 2) as q:
                    load(2 * q, 0)
                    load(2 * q + 1, 1)
                load(NCH - 1, (NCH - 1) % 2)
                for i in range(TM):
                    sp.wait_ge(s_y, ((b + 1) * NCH - 1) * DNG + 2 * (i + 1))
                    sp.dma_start(y_rows[b, :, i, :], y[:, i, :]).then_inc(s_store, 16)
            sp.wait_ge(s_store, 16 * TM * NTB)

        @block.gpsimd
        def _(pool):
            pool.memset(bup[:, FULL:FULL + 1], 0.0).then_inc(s_bdn, 1)
            pool.wait_ge(s_const, 64)
            pool.tensor_scalar(bdn[:], bdn[:], 0.5, 0.0, ALU.mult, ALU.add).then_inc(s_bdn, 1)
            pool.wait_ge(s_bdn, 2)
            for b in range(NTB):
                for i in range(TM):
                    pool.wait_ge(s_xn, 2 * (b * TM + i + 1))
                    pool.tensor_tensor(y[:, i, :], y[:, i, :], bdn[:], ALU.add).then_inc(s_yi, 1)

        @block.scalar
        def _(act):
            def up_out(c, par, base):
                for t in range(2):
                    for h in range(NH):
                        g = t * NH + h
                        n = base + c * UPG + g
                        act.wait_ge(s_upg, n + 1)
                        if g == 0:
                            after(act, s_dng, (base // UPG + c - 1) * DNG)
                        bias = bup_c[:, par, t:t + 1]
                        after(act, s_hlo, n - 1)
                        act.activation(hraw[:, h, :], pu[:, h, :], ACT.Relu, bias=bias).then_inc(s_raw, 1)
                        act.activation(ht[:, par, 0, t, h * 512:(h + 1) * 512], pu[:, h, :], ACT.Relu, bias=bias).then_inc(s_hhi, 1)

            act.wait_ge(s_const, 64)
            for b in range(NTB):
                act.wait_ge(s_var, b + 1)
                act.activation(rstd[:], var[:], ACT.Sqrt).then_inc(s_sd, 1)
                for i in range(TM):
                    for half in range(2):
                        n = (b * TM + i) * 2 + half
                        act.wait_ge(s_pt, n + 1)
                        if n % (2 * TM) == 0:
                            after(act, s_upg, b * NCH * UPG)
                        act.activation(xt[:, 0, half * 4:half * 4 + 4, i * P:(i + 1) * P],
                                       pt[:, half, :].rearrange("p (k n) -> p k n", k=4), ACT.Copy).then_inc(s_xhi, 1)
                base = b * NCH * UPG

                def one(c, par):
                    act.activation(bup_c[:, par, :], bup[:, bass.ds(2 * c, 2)], ACT.Copy).then_inc(s_bc, 1)
                    act.wait_ge(s_bc, b * NCH + c + 1)
                    up_out(c, par, base)
                one(0, 0)
                one(1, 1)
                with act.Fori(1, NCH // 2) as q:
                    one(2 * q, 0)
                    one(2 * q + 1, 1)
                one(NCH - 1, (NCH - 1) % 2)

        @block.vector
        def _(dve):
            seq = Count(dve, s_seq)
            dve.wait_ge(s_bdn, 2)
            for b in range(NTB):
                dve.wait_ge(s_x, 16 * TM * (b + 1))
                for i in range(TM):
                    for j in range(2):
                        ins = dve.bn_stats(out=stats[:, j, :], in_=y[:, i, j * 512:(j + 1) * 512])
                    seq.link(ins)
                    seq.link(dve.bn_aggr(out=mv[:, i, :], in_=stats[:, :, :]))
                dve.tensor_scalar(var[:], mv[:, :, 1], EPS, None, ALU.add).then_inc(s_var, 1)
                dve.wait_ge(s_sd, b + 1)
                seq.link(dve.reciprocal(rstd[:], rstd[:]))
                inverse_root(dve, seq.link, rstd[:], var[:], tmp[:])

                def x_lo(i, half):
                    n = (b * TM + i) * 2 + half
                    dve.wait_ge(s_xhi, n + 1)
                    dst = xt[:, 1, half * 4:half * 4 + 4, i * P:(i + 1) * P]
                    dve.tensor_tensor(dst, pt[:, half, :].rearrange("p (k n) -> p k n", k=4),
                                      xt[:, 0, half * 4:half * 4 + 4, i * P:(i + 1) * P].bitcast(F32),
                                      ALU.subtract).then_inc(s_xlo, 1)
                for i in range(TM):
                    for half in range(2):
                        after(dve, s_pt, 2 * (b * TM + i) + half - 1)
                        dve.tensor_scalar(xn[:, half, :], y[:, i, half * 512:(half + 1) * 512], mv[:, i, 0:1],
                                          rstd[:, i:i + 1], ALU.subtract, ALU.mult).then_inc(s_xn, 1)
                    if i:
                        x_lo(i - 1, 0)
                        x_lo(i - 1, 1)
                x_lo(TM - 1, 0)
                x_lo(TM - 1, 1)
                base, dbase = b * NCH * UPG, b * NCH * DNG

                def h_lo(c, par):
                    for t in range(2):
                        for h in range(NH):
                            dve.wait_ge(s_hhi, base + c * UPG + t * NH + h + 1)
                            hi = ht[:, par, 0, t, h * 512:(h + 1) * 512]
                            dve.tensor_tensor(ht[:, par, 1, t, h * 512:(h + 1) * 512], hraw[:, h, :],
                                              hi.bitcast(F32), ALU.subtract).then_inc(s_hlo, 1)

                def add(c):
                    for i in range(TM):
                        for half in range(2):
                            g = 2 * i + half
                            n = dbase + c * DNG + g
                            dve.wait_ge(s_dng, n + 1)
                            cols = y[:, i, half * 512:(half + 1) * 512]
                            dve.scalar_tensor_tensor(out=cols, in0=pd[:, g % 4, :], scalar=0.5, in1=cols,
                                                     op0=ALU.mult, op1=ALU.add).then_inc(s_y, 1)

                def one(c, par):
                    h_lo(c + 1, 1 - par)
                    after(dve, s_y, dbase + c * DNG)
                    add(c)
                h_lo(0, 0)
                dve.wait_ge(s_yi, TM * (b + 1))
                one(0, 0)
                one(1, 1)
                with dve.Fori(1, NCH // 2) as q:
                    one(2 * q, 0)
                    one(2 * q + 1, 1)
                dve.wait_ge(s_y, dbase + (NCH - 1) * DNG)
                add(NCH - 1)

        @block.tensor
        def _(pe):
            pe.wait_ge(s_const, 64)
            for b in range(NTB):
                for i in range(TM):
                    for half in range(2):
                        n = (b * TM + i) * 2 + half
                        pe.wait_ge(s_xn, n + 1)
                        after(pe, s_xlo, n - 1)
                        for k in range(4):
                            ins = pe.transpose(pt[:, half, k * P:(k + 1) * P], xn[:, half, k * P:(k + 1) * P], ident[:])
                        ins.then_inc(s_pt, 1)
                pe.wait_ge(s_xlo, (b + 1) * TM * 2)
                base, dbase = b * NCH * UPG, b * NCH * DNG

                def up(c, par, pair):
                    pe.wait_ge(s_wu[par], 16 * (loads_before(b, par) + pair + 1))
                    for t in range(2):
                        for h in range(NH):
                            g = t * NH + h
                            after(pe, s_hhi, base + c * UPG + g - 1)
                            for k in range(DK):
                                for j, (wi, xi) in enumerate(((0, 0), (0, 1), (1, 0))):
                                    ins = pe.matmul(pu[:, h, :], wu[:, par, wi, k, t * P:(t + 1) * P],
                                                    xt[:, xi, k, h * 512:(h + 1) * 512],
                                                    start=(k == 0 and j == 0), stop=(k == DK - 1 and j == 2))
                            ins.then_inc(s_upg, 1)

                def down(c, par, pair):
                    pe.wait_ge(s_wd[par], 16 * (loads_before(b, par) + pair + 1))
                    pe.wait_ge(s_hlo, base + (c + 1) * UPG)
                    for i in range(TM):
                        for half in range(2):
                            g = 2 * i + half
                            after(pe, s_y, dbase + c * DNG + g - 3)
                            for t in range(2):
                                for j, (hi, wi) in enumerate(((0, 0), (0, 1), (1, 0))):
                                    ins = pe.matmul(pd[:, g % 4, :], ht[:, par, hi, t, i * P:(i + 1) * P],
                                                    wd[:, par, wi, t, half * 512:(half + 1) * 512],
                                                    start=(t == 0 and j == 0), stop=(t == 1 and j == 2))
                            ins.then_inc(s_dng, 1)
                up(0, 0, 0)
                up(1, 1, 0)
                down(0, 0, 0)
                up(2, 0, 1)
                down(1, 1, 0)
                with pe.Fori(1, NCH // 2) as q:
                    up(2 * q + 1, 1, q)
                    down(2 * q, 0, q)
                    up(2 * q + 2, 0, q + 1)
                    down(2 * q + 1, 1, q)
                down(NCH - 1, 0, NCH // 2)


def tile_loop(eng, step):
    n = T // P
    step(0, 0)
    step(1, 1)
    with eng.Fori(1, n // 2 - 1) as q:
        step(2 * q, 0)
        step(2 * q + 1, 1)
    step(n - 2, 0)
    step(n - 1, 1)


def known(m, test):
    return isinstance(m, int) and test(m)


def qkv(nc, x_dram, weights, ident_dram, rope_dram, qk_dram, v_dram):
    NT = T // P
    RT = QKVW // P
    W0 = 2 * RT
    with ExitStack() as ctx:
        m_ = Pool(nc, ctx, "qk")
        ident = m_.sb("ident", [P, P])
        wnat = m_.sb("wnat", [P, 2, D])
        wt = m_.sb("wt", [P, 2, DK, QKVW], F32R)
        x = m_.sb("x", [P, 2, D])
        rope = m_.sb("rope", [P, 2, 2 * HD])
        xn = m_.sb("xn", [P, 2, D])
        xt = m_.sb("xt", [P, 2, 2, DK, P], F32R)
        straight = m_.sb("straight", [P, QKW])
        crossed = m_.sb("crossed", [P, QKW])
        qr = m_.sb("qr", [P, QKW])
        qs = m_.sb("qs", [P, 2, 2, QKW // P, P], F32R)
        vs = m_.sb("vs", [P, 2, NKV * HD])
        stats = m_.sb("stats", [P, 2, 6])
        mv = m_.sb("mv", [P, 2])
        var = m_.sb("var", [P, 1])
        rstd = m_.sb("rstd", [P, 1])
        tmp = m_.sb("tmp", [P, 1])
        pt = m_.ps("pt", [P, 2, 512])
        pq = m_.ps("pq", [P, 3, 512])
        pr = m_.ps("pr", [P, 3, 512])
        s_const = m_.sem("const")
        s_w = [m_.sem("w0"), m_.sem("w1")]
        s_x = [m_.sem("x0"), m_.sem("x1")]
        s_passed = m_.sem("passed")
        s_rope = [m_.sem("rope0"), m_.sem("rope1")]
        s_seq, s_var, s_sd, s_xn = m_.sem("vector_seq"), m_.sem("var"), m_.sem("sd"), m_.sem("xn")
        s_pt, s_hi, s_lo = m_.sem("transposed"), m_.sem("hi"), m_.sem("lo")
        s_mm, s_rd, s_v, s_qr = m_.sem("products"), m_.sem("rope_read"), m_.sem("v"), m_.sem("rotated")
        s_qt, s_qhi, s_qlo = m_.sem("q_transposed"), m_.sem("q_hi"), m_.sem("q_lo")
        s_out = [m_.sem("out0"), m_.sem("out1")]
        rows = [(w, r) for w in weights for r in range(w.shape[0] // P)]
        assert len(rows) == RT
        qk_rows = qk_dram.rearrange("a (j p) t -> a p j t", p=P)
        width = [512, 512, QKW - 1024]

        block = ctx.enter_context(nc.Block())

        @block.sync
        def _(sp):
            sp.dma_start(ident[:], ident_dram).then_inc(s_const, 16)
            for n, (w, r) in enumerate(rows):
                after(sp, s_pt, 2 * (n - 1))
                sp.dma_start(wnat[:, n % 2, :], w[r * P:(r + 1) * P, :]).then_inc(s_w[n % 2], 16)

            def step(m, par):
                after(sp, s_xn, m - 1)
                sp.dma_start(x[:, par, :], x_dram[bass.ds(m * P, P), :]).then_inc(s_x[par], 16)
                after(sp, s_rd, 3 * m - 3)
                sp.dma_start(rope[:, par, :], rope_dram[bass.ds(m * P, P), :]).then_inc(s_rope[par], 16)
            tile_loop(sp, step)

        @block.gpsimd
        def _(pool):
            def step(m, par):
                for g in range(3):
                    cols = slice(512 * g, 512 * g + width[g])
                    after(pool, s_qt, 3 * m + g - 2)
                    pool.wait_ge(s_rd, 3 * m + g + 1)
                    pool.tensor_tensor(qr[:, cols], straight[:, cols], crossed[:, cols], ALU.add).then_inc(s_qr, 1)
                if not known(m, lambda k: k == 0):
                    store(m - 1, 1 - par)

            def store(m, par):
                pool.wait_ge(s_qlo, 3 * m + 3)
                pool.wait_ge(s_v, m + 1)
                for a in range(2):
                    pool.dma_start(qk_rows[a, :, :, bass.ds(m * P, P)], qs[:, par, a, :, :].bitcast(F32)).then_inc(s_out[par], 16)
                pool.dma_start(v_dram[bass.ds(m * P, P), :], vs[:, par, :]).then_inc(s_out[par], 16)
            tile_loop(pool, step)
            store(NT - 1, 1)
            for par in range(2):
                pool.wait_ge(s_out[par], 48 * NT // 2)

        @block.scalar
        def _(act):
            def hi(unit, dst):
                act.wait_ge(s_pt, unit + 1)
                act.activation(dst, pt[:, unit_bank(unit), :].rearrange("p (k n) -> p k n", k=4), ACT.Copy).then_inc(s_hi, 1)

            def unit_bank(unit):
                return unit % 2

            for n in range(RT):
                for half in range(2):
                    hi(2 * n + half, wt[:, 0, half * 4:half * 4 + 4, n * P:(n + 1) * P])

            def root(m):
                act.wait_ge(s_var, m + 1)
                act.activation(rstd[:], var[:], ACT.Sqrt).then_inc(s_sd, 1)

            def x_hi(m, par):
                after(act, s_mm, 3 * m - 3)
                for half in range(2):
                    act.wait_ge(s_pt, W0 + 2 * m + half + 1)
                    act.activation(xt[:, par, 0, half * 4:half * 4 + 4, :],
                                   pt[:, half, :].rearrange("p (k n) -> p k n", k=4), ACT.Copy).then_inc(s_hi, 1)

            def q_hi(m, par, pair):
                after(act, s_out[par], 48 * pair)
                for g in range(3):
                    act.wait_ge(s_qt, 3 * m + g + 1)
                    act.activation(qs[:, par, 0, 4 * g:4 * g + width[g] // P, :],
                                   pr[:, g, 0:width[g]].rearrange("p (j n) -> p j n", n=P), ACT.Copy).then_inc(s_qhi, 1)

            def v_out(m, par, pair):
                after(act, s_out[par], 48 * pair)
                act.wait_ge(s_rd, 3 * m + 3)
                act.activation(vs[:, par, :], pq[:, 2, 256:512], ACT.Copy).then_inc(s_v, 1)

            root(0)
            root(1)
            x_hi(0, 0)

            def paired(q, u):
                m = 2 * q + u
                if not known(m, lambda k: k >= NT - 1):
                    x_hi(m + 1, 1 - u)
                if not known(m, lambda k: k >= NT - 2):
                    root(m + 2)
                if not known(m, lambda k: k == 0):
                    v_out(m - 1, 1 - u, q if u else q - 1)
                    q_hi(m - 1, 1 - u, q if u else q - 1)
            paired(0, 0)
            paired(0, 1)
            with act.Fori(1, NT // 2 - 1) as q:
                paired(q, 0)
                paired(q, 1)
            paired(NT // 2 - 1, 0)
            paired(NT // 2 - 1, 1)
            v_out(NT - 1, 1, NT // 2 - 1)
            q_hi(NT - 1, 1, NT // 2 - 1)

        @block.vector
        def _(dve):
            for n in range(RT):
                for half in range(2):
                    dve.wait_ge(s_hi, 2 * n + half + 1)
                    cols = (slice(None), slice(half * 4, half * 4 + 4), slice(n * P, (n + 1) * P))
                    dve.tensor_tensor(wt[:, 1, cols[1], cols[2]], pt[:, half, :].rearrange("p (k n) -> p k n", k=4),
                                      wt[:, 0, cols[1], cols[2]].bitcast(F32), ALU.subtract).then_inc(s_lo, 1)

            PER = 7

            def norm(m, par, pair):
                seq = Count(dve, s_seq, PER * m)
                dve.wait_ge(s_x[par], 16 * pair + 16)
                for j in range(2):
                    ins = dve.bn_stats(out=stats[:, j, :], in_=x[:, par, j * 512:(j + 1) * 512])
                ins.then_inc(s_seq, 1)
                gate(dve, s_seq, PER * m + 1, s_passed)
                seq.n = PER * m + 1
                seq.link(dve.bn_aggr(out=mv[:], in_=stats[:, :, :]))
                dve.tensor_scalar(var[:], mv[:, 1:2], EPS, None, ALU.add).then_inc(s_var, 1)
                dve.wait_ge(s_sd, m + 1)
                seq.link(dve.reciprocal(rstd[:], rstd[:]))
                inverse_root(dve, seq.link, rstd[:], var[:], tmp[:])
                after(dve, s_pt, W0 + 2 * m - 2)
                dve.tensor_scalar(xn[:, par, :], x[:, par, :], mv[:, 0:1], rstd[:], ALU.subtract, ALU.mult).then_inc(s_xn, 1)

            def x_lo(m, par):
                for half in range(2):
                    dve.wait_ge(s_hi, W0 + 2 * m + half + 1)
                    dve.tensor_tensor(xt[:, par, 1, half * 4:half * 4 + 4, :], pt[:, half, :].rearrange("p (k n) -> p k n", k=4),
                                      xt[:, par, 0, half * 4:half * 4 + 4, :].bitcast(F32), ALU.subtract).then_inc(s_lo, 1)

            def q_lo(m, par):
                for g in range(3):
                    dve.wait_ge(s_qhi, 3 * m + g + 1)
                    js = slice(4 * g, 4 * g + width[g] // P)
                    dve.tensor_tensor(qs[:, par, 1, js, :], pr[:, g, 0:width[g]].rearrange("p (j n) -> p j n", n=P),
                                      qs[:, par, 0, js, :].bitcast(F32), ALU.subtract).then_inc(s_qlo, 1)

            def rotate(m, par, pair):
                dve.wait_ge(s_rope[par], 16 * pair + 16)
                for g in range(3):
                    nh = width[g] // HD
                    src = pq[:, g, 0:width[g]].rearrange("p (h r) -> p h r", r=HD)
                    cols = slice(512 * g, 512 * g + width[g])
                    st = straight[:, cols].rearrange("p (h r) -> p h r", r=HD)
                    cr = crossed[:, cols].rearrange("p (h r) -> p h r", r=HD)

                    def over_heads(a, b):
                        return rope[:, par, a:b].unsqueeze(1).to_broadcast([P, nh, b - a])
                    dve.wait_ge(s_mm, 3 * m + g + 1)
                    after(dve, s_qr, 3 * m + g - 2)
                    dve.tensor_tensor(st, src, over_heads(0, HD), ALU.mult)
                    dve.tensor_tensor(cr[:, :, 0:HD // 2], src[:, :, HD // 2:HD], over_heads(HD, HD + HD // 2), ALU.mult)
                    dve.tensor_tensor(cr[:, :, HD // 2:HD], src[:, :, 0:HD // 2], over_heads(HD + HD // 2, 2 * HD), ALU.mult)\
                        .then_inc(s_rd, 1)

            norm(0, 0, 0)
            norm(1, 1, 0)
            x_lo(0, 0)

            def paired(q, u):
                m = 2 * q + u
                if not known(m, lambda k: k == 0):
                    rotate(m - 1, 1 - u, q if u else q - 1)
                if not known(m, lambda k: k >= NT - 1):
                    x_lo(m + 1, 1 - u)
                if not known(m, lambda k: k >= NT - 2):
                    norm(m + 2, u, q + 1)
                if not known(m, lambda k: k == 0):
                    q_lo(m - 1, 1 - u)
            paired(0, 0)
            paired(0, 1)
            with dve.Fori(1, NT // 2 - 1) as q:
                paired(q, 0)
                paired(q, 1)
            paired(NT // 2 - 1, 0)
            paired(NT // 2 - 1, 1)
            rotate(NT - 1, 1, NT // 2 - 1)
            q_lo(NT - 1, 1)

        @block.tensor
        def _(pe):
            pe.wait_ge(s_const, 16)
            for n in range(RT):
                pe.wait_ge(s_w[n % 2], 16 * (n // 2 + 1))
                for half in range(2):
                    after(pe, s_lo, 2 * n + half - 1)
                    for k in range(4):
                        kk = half * 4 + k
                        ins = pe.transpose(pt[:, half, k * P:(k + 1) * P], wnat[:, n % 2, kk * P:(kk + 1) * P], ident[:])
                    ins.then_inc(s_pt, 1)

            def x_turn(m, par):
                pe.wait_ge(s_xn, m + 1)
                for half in range(2):
                    pe.wait_ge(s_lo, W0 + 2 * m + half - 1)
                    for k in range(4):
                        kk = half * 4 + k
                        ins = pe.transpose(pt[:, half, k * P:(k + 1) * P], xn[:, par, kk * P:(kk + 1) * P], ident[:])
                    ins.then_inc(s_pt, 1)

            def products(m, par, g):
                after(pe, s_rd, 3 * m + g - 2)
                if g == 2:
                    after(pe, s_v, m)
                for k in range(DK):
                    for j, (xi, wi) in enumerate(((0, 0), (0, 1), (1, 0))):
                        ins = pe.matmul(pq[:, g, :], xt[:, par, xi, k, :], wt[:, wi, k, 512 * g:512 * (g + 1)],
                                        start=(k == 0 and j == 0), stop=(k == DK - 1 and j == 2))
                ins.then_inc(s_mm, 1)

            def q_turn(m):
                for g in range(3):
                    pe.wait_ge(s_qr, 3 * m + g + 1)
                    after(pe, s_qlo, 3 * m + g - 2)
                    for j in range(width[g] // P):
                        c0 = 512 * g + j * P
                        ins = pe.transpose(pr[:, g, j * P:(j + 1) * P], qr[:, c0:c0 + P], ident[:])
                    ins.then_inc(s_qt, 1)
            x_turn(0, 0)

            def step(m, par):
                if not known(m, lambda k: k >= NT - 1):
                    x_turn(m + 1, 1 - par)
                pe.wait_ge(s_lo, W0 + 2 * m + 2)
                products(m, par, 0)
                if not known(m, lambda k: k == 0):
                    q_turn(m - 1)
                products(m, par, 1)
                products(m, par, 2)
            tile_loop(pe, step)
            q_turn(NT - 1)


def attention(nc, qk_dram, v_dram, ident_dram, causal_dram, edge_dram, older_dram, keyrows_dram, o_dram, sum_dram):
    QT = SEQ // P
    NC = SEQ // CHUNK
    LATE = 2
    SUMS = 2 * HD
    N = BATCH * NKV
    SLOTS = BATCH
    AT = [0, 512, 896, 1152]
    SCORE, TURN, EXP, VALUE = "score", "turn", "exp", "value"
    ORDER = [(SCORE, 3), (EXP, 3, 0), (EXP, 3, 1), (EXP, 3, 2), (EXP, 3, 3), (TURN, 1),
             (VALUE, 0, 0), (EXP, 2, 0), (VALUE, 0, 1), (EXP, 2, 1), (VALUE, 0, 2), (EXP, 2, 2), (VALUE, 0, 3), (EXP, 2, 3),
             (SCORE, 2), (TURN, 0),
             (VALUE, 1, 0), (EXP, 1, 0), (VALUE, 1, 1), (EXP, 1, 1), (VALUE, 1, 2), (EXP, 1, 2), (VALUE, 1, 3), (EXP, 1, 3),
             (TURN, 3), (VALUE, 2, 0), (EXP, 0, 0), (VALUE, 2, 1), (EXP, 0, 1), (SCORE, 1),
             (VALUE, 2, 2), (EXP, 0, 2), (VALUE, 2, 3), (EXP, 0, 3), (SCORE, 0),
             (VALUE, 3, 0), (VALUE, 3, 1), (VALUE, 3, 2), (VALUE, 3, 3), (TURN, 2)]
    EARLY = (3, 2)
    with ExitStack() as ctx:
        m_ = Pool(nc, ctx, "at")
        identf = m_.sb("identf", [P, P])
        identb = m_.sb("identb", [P, P], BF16)
        causal = m_.sb("causal", [P, P])
        causalb = m_.sb("causalb", [P, P], BF16)
        edgef = m_.sb("edgef", [P, P])
        edge = m_.sb("edge", [P, P], BF16)
        older = m_.sb("older", [P, 4, 16])
        ka = m_.sb("ka", [P, SLOTS, SEQ], F32R)
        qa = m_.sb("qa", [P, SLOTS, GROUP, SEQ], F32R)
        vg = m_.sb("vg", [P, SLOTS, QT, SUMS])
        cm = m_.sb("cm", [P, GROUP, NC])
        m8 = m_.sb("m8", [P, GROUP, 8])
        left = m_.sb("left", [P, GROUP, NC])
        pen = m_.sb("pen", [P, GROUP, 16])
        own = m_.sb("own", [P, GROUP, 16])
        ownsum = m_.sb("ownsum", [P, GROUP])
        mh = m_.sb("mh", [P, GROUP], F32R)
        added = m_.sb("added", [P, QT, GROUP, P])
        edgepen = m_.sb("edgepen", [P, 2, 2, GROUP, P], BF16)
        prob = m_.sb("prob", [P, 2, GROUP, 1280])
        ov = m_.sb("ov", [SUMS, 2, GROUP, SEQ])
        psc = m_.ps("psc", [P, GROUP, 512])
        pa = m_.ps("pa", [P, GROUP, P])
        pst = m_.ps("pst", [P, 2, 512])
        po = m_.ps("po", [P, 512])
        s_const, s_cast, s_init = m_.sem("const"), m_.sem("cast"), m_.sem("init")
        s_keyrow = m_.sem("keyrow")
        s_ld = [m_.sem(f"ld{i}") for i in range(SLOTS)]
        s_seq = m_.sem("vector_seq")
        s_passed, s_ppassed = m_.sem("passed"), m_.sem("pool_passed")
        s_sc, s_cm, s_add = m_.sem("scores"), m_.sem("chunk_max"), m_.sem("added")
        s_pa, s_qa = m_.sem("added_turned"), m_.sem("added_placed")
        s_st, s_p, s_dg = m_.sem("scores_t"), m_.sem("prob"), m_.sem("diagonal")
        s_pv, s_ov = m_.sem("values"), m_.sem("values_copied")
        s_out = [m_.sem("out0"), m_.sem("out1")]
        LINKS = [3, 3, 9, 9]
        PER = sum(LINKS)

        block = ctx.enter_context(nc.Block())

        q_rows = qk_dram[:, 0:NHEAD * HD, :].rearrange("a (g h r) (b t) -> a r b g h t", g=NKV, h=GROUP, b=BATCH)
        k_rows = qk_dram[:, NHEAD * HD:QKW, :].rearrange("a (g r) (b t) -> a r b g t", g=NKV, b=BATCH)
        v_rows = v_dram.rearrange("(b j p) (g r) -> p b g j r", b=BATCH, j=QT, g=NKV)
        o_rows = o_dram.rearrange("(g h r) (b t) -> r b g h t", g=NKV, h=GROUP, b=BATCH)
        sum_rows = sum_dram.rearrange("(g h) (b t) -> b g h t", g=NKV, b=BATCH)

        def groups(step):
            def run(eng):
                for u in range(SLOTS):
                    step(u, u, 0)
                with eng.Fori(1, N // SLOTS - 1) as q:
                    for u in range(SLOTS):
                        step(SLOTS * q + u, u, q)
                for u in range(SLOTS):
                    step(N - SLOTS + u, u, N // SLOTS - 1)
            return run

        @block.sync
        def _(sp):
            for dst, src in ((identf[:], ident_dram), (causal[:], causal_dram), (edgef[:], edge_dram),
                             (older[:], older_dram.rearrange("p (a c) -> p a c", a=4))):
                sp.dma_start(dst, src).then_inc(s_const, 16)

            def load(G, slot, g):
                b = slot
                after(sp, s_pv, GROUP * (G - SLOTS + 1))
                for r, a in ((0, 0), (1, 0), (2, 1)):
                    sp.dma_start(ka[32 * r:32 * r + 32, slot, :].bitcast(F32), k_rows[a, :, b, g, :]).then_inc(s_ld[slot], 16)
                for r, a in ((0, 0), (1, 1), (2, 0)):
                    sp.dma_start(qa[32 * r:32 * r + 32, slot, :, :].bitcast(F32), q_rows[a, :, b, g, :, :]).then_inc(s_ld[slot], 16)
                sp.dma_start(vg[:, slot, :, 0:HD], v_rows[:, b, g, :, :]).then_inc(s_ld[slot], 16)
                if not known(G, lambda k: k < SLOTS):
                    store(G - SLOTS, slot, g - 1)

            def store(G, slot, g):
                sp.wait_ge(s_ov, GROUP * (G + 1))
                sp.dma_start(o_rows[:, slot, g, :, :], ov[0:HD, slot % 2, :, :]).then_inc(s_out[slot % 2], 16)
                sp.dma_start(sum_rows[slot:slot + 1, g, :, :], ov[HD:HD + 1, slot % 2, :, :]).then_inc(s_out[slot % 2], 16)
            groups(load)(sp)
            for slot in range(SLOTS):
                store(N - SLOTS + slot, slot, NKV - 1)
            for par in range(2):
                sp.wait_ge(s_out[par], 32 * N // 2)

        @block.gpsimd
        def _(pool):
            pool.memset(added[:, :, :, :], 0.0).then_inc(s_init, 1)
            pool.memset(vg[:, :, :, HD:SUMS], 1.0).then_inc(s_init, 1)
            for slot in range(SLOTS):
                pool.dma_start(ka[96:128, slot, :], keyrows_dram).then_inc(s_keyrow, 16)

            def diagonal(G, par, j):
                gate(pool, s_p, 16 * G + GROUP * (QT - j), s_ppassed)
                block_ = prob[:, par, :, AT[j]:AT[j] + P]
                pool.affine_select(out=block_, in_=block_, pattern=[[0, GROUP], [1, P]], compare_op=ALU.is_ge,
                                   fill=0.0, base=0, channel_multiplier=-1).then_inc(s_dg, 1)

            def step(G, slot, q):
                for j in reversed(range(QT)):
                    diagonal(G, slot % 2, j)
            groups(step)(pool)

        @block.scalar
        def _(act):
            act.wait_ge(s_const, 64)
            act.activation(identb[:], identf[:], ACT.Copy).then_inc(s_cast, 1)
            act.activation(causalb[:], causal[:], ACT.Copy).then_inc(s_cast, 1)
            act.activation(edge[:], edgef[:], ACT.Copy).then_inc(s_cast, 1)

            def place(G, slot, t):
                act.wait_ge(s_pa, QT * G + QT - t)
                act.activation(qa[96:128, slot, :, t * P:(t + 1) * P], pa[96:128, :, :], ACT.Copy).then_inc(s_qa, 1)

            def exp(G, par, j, h):
                n = 16 * G + GROUP * (QT - 1 - j) + h
                if j == QT - 1 and h == 0:
                    after(act, s_pv, GROUP * (G - 1))
                act.wait_ge(s_st, n + 1)
                act.activation(prob[:, par, h, AT[j]:AT[j] + SEQ - j * P], pst[:, h % 2, 0:SEQ - j * P],
                               ACT.Exp, scale=SCALE).then_inc(s_p, 1)

            def copy(G, par, h, pair):
                if h == 0:
                    after(act, s_out[par], 32 * pair)
                act.wait_ge(s_pv, GROUP * G + h + 1)
                act.activation(ov[:, par, h, :], po[0:SUMS, :], ACT.Copy).then_inc(s_ov, 1)
            for t in EARLY:
                place(0, 0, t)

            def step(G, slot, q):
                ahead = not known(G, lambda k: k >= N - 1)
                behind = not known(G, lambda k: k < 1)
                for kind, *at in ORDER:
                    if kind == EXP:
                        exp(G, slot % 2, *at)
                    if kind == TURN and at[0] not in EARLY:
                        place(G, slot, at[0])
                    if kind == TURN and at[0] in EARLY and ahead:
                        place(G + 1, (slot + 1) % SLOTS, at[0])
                    if kind == VALUE and at[1] == QT - 1 and behind:
                        copy(G - 1, 1 - slot % 2, at[0], 2 * q + (slot - 1) // 2)
            groups(step)(act)
            for h in range(GROUP):
                copy(N - 1, 1, h, N // 2 - 1)

        @block.vector
        def _(dve):
            dve.wait_ge(s_const, 64)
            dve.wait_ge(s_cast, 3)
            dve.wait_ge(s_init, 2)

            def rows(G, par, t):
                seq = Count(dve, s_seq, PER * G + sum(LINKS[t + 1:]))
                turn = QT * G + QT - 1 - t
                nc_t = (t + 1) * P // CHUNK
                gate(dve, s_sc, turn + 1, s_passed)
                dve.tensor_reduce(cm[:, :, 0:nc_t], psc[:, :, 0:(t + 1) * P].rearrange("p h (c k) -> p h c k", k=CHUNK),
                                  AX.X, ALU.max).then_inc(s_cm, 1)
                after(dve, s_pa, turn - QT + 1)
                gate(dve, s_cm, turn + 1, s_passed)
                mx = added[:, t, :, 96]
                seq.link(dve.tensor_reduce(mx, cm[:, :, 0:nc_t], AX.X, ALU.max, negate=True))
                seq.link(dve.tensor_copy(mh[:], mx))
                last = dve.tensor_tensor(added[:, t, :, 97], mx, mh[:].bitcast(F32), ALU.subtract)
                if t < LATE:
                    seq.link(last)
                    return
                L = t - LATE
                for h in range(GROUP):
                    ins = dve.max(out=m8[:, h, :], in_=cm[:, h, 0:nc_t])
                ins.then_inc(s_seq, 1)
                seq.n = seq.n + 1
                gate(dve, s_seq, seq.n, s_passed)
                for h in range(GROUP):
                    ins = dve.match_replace(out=left[:, h, 0:nc_t], in_to_replace=m8[:, h, :],
                                            in_values=cm[:, h, 0:nc_t], imm_value=3e38)
                seq.link(ins)
                seq.link(dve.tensor_scalar(pen[:], left[:, :, 8:24], 1e38, -BIG, ALU.is_lt, ALU.mult))
                seq.link(dve.tensor_tensor(own[:], pen[:], older[:, 2 + L, :].unsqueeze(1).to_broadcast([P, GROUP, 16]), ALU.mult))
                seq.link(dve.tensor_tensor(added[:, t, :, 98:114], pen[:], older[:, L, :].unsqueeze(1).to_broadcast([P, GROUP, 16]), ALU.mult))
                seq.link(dve.tensor_reduce(ownsum[:], own[:], AX.X, ALU.add))
                after(dve, s_st, 16 * (G - 1))
                for h in range(GROUP):
                    ins = dve.tensor_scalar(edgepen[:, par, L, h, :], edge[:], ownsum[:, h:h + 1], None, ALU.mult)
                seq.link(ins)

            for t in reversed(range(QT)):
                rows(0, 0, t)

            def step(G, slot, q):
                if not known(G, lambda k: k >= N - 1):
                    for t in reversed(range(QT)):
                        rows(G + 1, 1 - slot % 2, t)
            groups(step)(dve)

        @block.tensor
        def _(pe):
            pe.wait_ge(s_cast, 3)
            pe.wait_ge(s_keyrow, 16 * SLOTS)
            pe.wait_ge(s_init, 2)

            def scores(G, slot, t, quad):
                if t == QT - 1:
                    pe.wait_ge(s_ld[slot], 112 * (quad + 1))
                after(pe, s_cm, QT * G + QT - 1 - t)
                for h in range(GROUP):
                    pe.matmul(psc[:, h, 0:(t + 1) * P], qa[0:96, slot, h, t * P:(t + 1) * P], ka[0:96, slot, 0:(t + 1) * P],
                              start=True, stop=False)
                    ins = pe.matmul(psc[:, h, t * P:(t + 1) * P], identb[:], causalb[:], start=False, stop=True)
                ins.then_inc(s_sc, 1)

            def turn(G, t):
                pe.wait_ge(s_seq, PER * G + sum(LINKS[t:]))
                after(pe, s_qa, QT * G + QT - 1 - t)
                for h in range(GROUP):
                    ins = pe.transpose(pa[:, h, :], added[:, t, h, :], identf[:])
                ins.then_inc(s_pa, 1)

            def score_t(G, slot, j, h):
                n = 16 * G + GROUP * (QT - 1 - j) + h
                if h == 0:
                    pe.wait_ge(s_qa, QT * G + QT - j)
                after(pe, s_p, n - 1)
                edged = 1 <= j <= 2
                ins = pe.matmul(pst[:, h % 2, 0:SEQ - j * P], ka[:, slot, j * P:(j + 1) * P], qa[:, slot, h, j * P:SEQ],
                                start=True, stop=not edged)
                if edged:
                    ins = pe.matmul(pst[:, h % 2, P:2 * P], edgepen[:, slot % 2, j - 1, h, :], identb[:], start=False, stop=True)
                ins.then_inc(s_st, 1)

            def value(G, slot, h, j):
                if h == 0 and j == 0:
                    pe.wait_ge(s_dg, QT * (G + 1))
                if j == 0:
                    after(pe, s_ov, GROUP * G + h)
                ins = pe.matmul(po[0:SUMS, j * P:SEQ], vg[:, slot, j, :], prob[:, slot % 2, h, AT[j]:AT[j] + SEQ - j * P],
                                start=(j == 0), stop=(j == QT - 1))
                if j == QT - 1:
                    ins.then_inc(s_pv, 1)
            for t in reversed(range(QT)):
                scores(0, 0, t, 0)
                if t in EARLY:
                    turn(0, t)

            def step(G, slot, q):
                ahead = not known(G, lambda k: k >= N - 1)
                behind = not known(G, lambda k: k < 1)
                nslot = (slot + 1) % SLOTS
                for kind, *at in ORDER:
                    if kind == SCORE and ahead:
                        scores(G + 1, nslot, at[0], q + 1 if nslot == 0 else q)
                    if kind == TURN and at[0] not in EARLY:
                        turn(G, at[0])
                    if kind == TURN and at[0] in EARLY and ahead:
                        turn(G + 1, at[0])
                    if kind == EXP:
                        score_t(G, slot, *at)
                    if kind == VALUE and behind:
                        value(G - 1, (slot - 1) % SLOTS, *at)
            groups(step)(pe)
            for h in range(GROUP):
                for j in range(QT):
                    value(N - 1, SLOTS - 1, h, j)


def output(nc, o_dram, sum_dram, x_dram, wo, ident_dram, rec_dram, y_dram):
    NT, RT = T // P, D // P
    W0 = 2 * RT
    with ExitStack() as ctx:
        m_ = Pool(nc, ctx, "ou")
        ident = m_.sb("ident", [P, P])
        wnat = m_.sb("wnat", [P, 2, D])
        wt = m_.sb("wt", [P, 2, DK, D], F32R)
        sums = m_.sb("sums", [P, NHEAD * T // P])
        o = m_.sb("o", [P, 2, DK, P])
        rec = m_.sb("rec", [P, 2, DK, P])
        od = m_.sb("od", [P, 2, DK, P])
        x = m_.sb("x", [P, 2, D])
        xt = m_.sb("xt", [P, 2, 2, DK, P], F32R)
        y = m_.sb("y", [P, 2, D])
        pt = m_.ps("pt", [P, 2, 512])
        py = m_.ps("py", [P, 4, 512])
        s_const = m_.sem("const")
        s_w = [m_.sem("w0"), m_.sem("w1")]
        s_o = [m_.sem("o0"), m_.sem("o1")]
        s_sum, s_inv, s_rec = m_.sem("sums"), m_.sem("inverted"), m_.sem("rec_stored")
        s_od = m_.sem("divided")
        s_x = [m_.sem("x0"), m_.sem("x1")]
        s_pt, s_hi, s_lo = m_.sem("transposed"), m_.sem("hi"), m_.sem("lo")
        s_mm, s_y = m_.sem("products"), m_.sem("y")
        o_cols = o_dram.rearrange("(k p) t -> p k t", p=P)
        rec_cols = rec_dram.rearrange("(k h) t -> h k t", h=P // HD)

        def flat(ap):
            return ap.rearrange("h (a t) -> (h a) t", t=NHEAD * T // P)
        s_out = [m_.sem("out0"), m_.sem("out1")]
        block = ctx.enter_context(nc.Block())

        @block.sync
        def _(sp):
            sp.dma_start(sums[:], flat(sum_dram)).then_inc(s_sum, 16)
            sp.dma_start(ident[:], ident_dram).then_inc(s_const, 16)
            for n in range(RT):
                after(sp, s_pt, 2 * (n - 1))
                sp.dma_start(wnat[:, n % 2, :], wo[n * P:(n + 1) * P, :]).then_inc(s_w[n % 2], 16)

            sp.wait_ge(s_inv, 1)
            sp.dma_start(flat(rec_dram), sums[:]).then_inc(s_rec, 16)
            sp.wait_ge(s_rec, 16)

            def step(m, par):
                after(sp, s_od, m - 1)
                sp.dma_start(o[:, par, :, :], o_cols[:, :, bass.ds(m * P, P)]).then_inc(s_o[par], 16)
                for h in range(P // HD):
                    row = rec_cols[h:h + 1, :, bass.ds(m * P, P)]
                    sp.dma_start(rec[h * HD:(h + 1) * HD, par, :, :], row.to_broadcast([HD, DK, P])).then_inc(s_o[par], 16)
                after(sp, s_y, 2 * m - 2)
                sp.dma_start(x[:, par, :], x_dram[bass.ds(m * P, P), :]).then_inc(s_x[par], 16)
            tile_loop(sp, step)

        @block.gpsimd
        def _(pool):
            def divide(m, par, pair):
                if not known(m, lambda k: k < 2):
                    pool.wait_ge(s_lo, W0 + m - 1)
                pool.wait_ge(s_o[par], 80 * pair + 80)
                pool.tensor_tensor(od[:, par, :, :], o[:, par, :, :], rec[:, par, :, :], ALU.mult).then_inc(s_od, 1)
            divide(0, 0, 0)

            def paired(q, u):
                m = 2 * q + u
                if not known(m, lambda k: k >= NT - 1):
                    divide(m + 1, 1 - u, q + u)
                pool.wait_ge(s_y, 2 * m + 2)
                pool.dma_start(y_dram[bass.ds(m * P, P), :], y[:, u, :]).then_inc(s_out[u], 16)
            paired(0, 0)
            paired(0, 1)
            with pool.Fori(1, NT // 2 - 1) as q:
                paired(q, 0)
                paired(q, 1)
            paired(NT // 2 - 1, 0)
            paired(NT // 2 - 1, 1)
            for par in range(2):
                pool.wait_ge(s_out[par], 16 * NT // 2)

        @block.scalar
        def _(act):
            for n in range(RT):
                for half in range(2):
                    act.wait_ge(s_pt, 2 * n + half + 1)
                    act.activation(wt[:, 0, half * 4:half * 4 + 4, n * P:(n + 1) * P],
                                   pt[:, half, :].rearrange("p (k n) -> p k n", k=4), ACT.Copy).then_inc(s_hi, 1)

            def x_hi(m, par):
                after(act, s_mm, 2 * m - 2)
                act.wait_ge(s_od, m + 1)
                act.activation(xt[:, par, 0, :, :], od[:, par, :, :], ACT.Copy).then_inc(s_hi, 1)
            tile_loop(act, x_hi)

        @block.vector
        def _(dve):
            dve.wait_ge(s_sum, 16)
            dve.reciprocal(sums[:], sums[:]).then_inc(s_inv, 1)
            for n in range(RT):
                for half in range(2):
                    dve.wait_ge(s_hi, 2 * n + half + 1)
                    ks, cs = slice(half * 4, half * 4 + 4), slice(n * P, (n + 1) * P)
                    dve.tensor_tensor(wt[:, 1, ks, cs], pt[:, half, :].rearrange("p (k n) -> p k n", k=4),
                                      wt[:, 0, ks, cs].bitcast(F32), ALU.subtract).then_inc(s_lo, 1)

            def x_lo(m, par):
                dve.wait_ge(s_hi, W0 + m + 1)
                dve.tensor_tensor(xt[:, par, 1, :, :], od[:, par, :, :], xt[:, par, 0, :, :].bitcast(F32),
                                  ALU.subtract).then_inc(s_lo, 1)
            x_lo(0, 0)

            def paired(q, u):
                m = 2 * q + u
                if not known(m, lambda k: k >= NT - 1):
                    x_lo(m + 1, 1 - u)
                dve.wait_ge(s_x[u], 16 * q + 16)
                after(dve, s_out[u], 16 * q)
                for half in range(2):
                    cols = slice(half * 512, (half + 1) * 512)
                    dve.wait_ge(s_mm, 2 * m + half + 1)
                    dve.tensor_tensor(y[:, u, cols], py[:, 2 * u + half, :], x[:, u, cols], ALU.add).then_inc(s_y, 1)
            paired(0, 0)
            paired(0, 1)
            with dve.Fori(1, NT // 2 - 1) as q:
                paired(q, 0)
                paired(q, 1)
            paired(NT // 2 - 1, 0)
            paired(NT // 2 - 1, 1)

        @block.tensor
        def _(pe):
            pe.wait_ge(s_const, 16)
            for n in range(RT):
                pe.wait_ge(s_w[n % 2], 16 * (n // 2 + 1))
                for half in range(2):
                    after(pe, s_lo, 2 * n + half - 1)
                    for k in range(4):
                        kk = half * 4 + k
                        ins = pe.transpose(pt[:, half, k * P:(k + 1) * P], wnat[:, n % 2, kk * P:(kk + 1) * P], ident[:])
                    ins.then_inc(s_pt, 1)

            def products(m, par):
                pe.wait_ge(s_lo, W0 + m + 1)
                after(pe, s_y, 2 * m - 2)
                for half in range(2):
                    for k in range(DK):
                        for j, (xi, wi) in enumerate(((0, 0), (0, 1), (1, 0))):
                            ins = pe.matmul(py[:, 2 * par + half, :], xt[:, par, xi, k, :],
                                            wt[:, wi, k, 512 * half:512 * (half + 1)],
                                            start=(k == 0 and j == 0), stop=(k == DK - 1 and j == 2))
                    ins.then_inc(s_mm, 1)
            tile_loop(pe, products)


def kernel(**inputs):
    import numpy as np
    import concourse.bacc as bacc
    from concourse.bass_utils import run_bass_kernel_spmd

    nc = bacc.Bacc("TRN2", target_bir_lowering=False, num_devices=1)
    arrays, t = {}, {}
    host = {k: np.ascontiguousarray(v) for k, v in inputs.items()}
    half = HD // 2
    inv = (np.float32(1.0) / np.power(np.float32(10000.0), np.arange(0, HD, 2, dtype=np.float32) / np.float32(HD))).astype(np.float32)
    freq = np.arange(SEQ, dtype=np.float32)[:, None] * inv[None, :]
    sin = np.sin(freq).astype(np.float32)
    host["rope"] = np.concatenate([np.cos(freq), np.cos(freq), -sin, sin], axis=1).astype(np.float32)
    host["rope"] = np.tile(host["rope"], (BATCH, 1))
    host["ident"] = np.eye(P, dtype=np.float32)
    q, k = np.arange(P)[:, None], np.arange(P)[None, :]
    host["causal"] = np.where(k > q, np.float32(-BIG), np.float32(0.0))
    host["edge"] = ((k <= q) & (k // CHUNK == q // CHUNK)).astype(np.float32)
    c = np.arange(CHUNK)[None, :]
    rel = np.arange(P)[:, None] // CHUNK
    host["older"] = np.concatenate([(c < rel), (c < rel + 8), (c == rel), (c == rel + 8)], axis=1).astype(np.float32)
    key = np.arange(SEQ)
    rows = np.zeros((32, SEQ), np.float32)
    rows[0:2] = 1.0
    for j in range(16):
        rows[2 + j] = key // CHUNK == 8 + j
    host["keyrows"] = rows
    for name, a in host.items():
        arrays[name] = a
        t[name] = nc.dram_tensor(name, a.shape, mybir.dt.from_np(a.dtype), kind="ExternalInput").ap()
    out = nc.dram_tensor("out", (BATCH, SEQ, D), F32, kind="ExternalOutput").ap()
    program(nc, t, out)
    r = run_bass_kernel_spmd(nc, [arrays], core_ids=[0])
    return r.results[0]["out"]


def program(nc, t, out):
    def scratch(name, shape, dt=F32):
        return nc.dram_tensor(name, shape, dt, kind="Internal").ap()
    wup = scratch("wup", (NCH, P, 4 * 1024))
    wdn = scratch("wdn", (NCH, P, 4 * 1024))
    dequantise(nc, t["L0_ffn_w_up_codes"], t["L0_ffn_w_up_absmax"], t["L0_ffn_w_up_lora_a"], t["L0_ffn_w_up_lora_b"],
               t["L0_ffn_w_down_codes"], t["L0_ffn_w_down_absmax"], t["L0_ffn_w_down_lora_a"], t["L0_ffn_w_down_lora_b"],
               t["ident"], wup, wdn)
    x1, x2, o = scratch("x1", (T, D)), scratch("x2", (T, D)), scratch("o", (D, T))
    sums, rec = scratch("sums", (NHEAD, T)), scratch("rec", (NHEAD, T))
    qk, v = scratch("qk", (2, QKW, T)), scratch("v", (T, NKV * HD))
    x0 = t["L0_attn_hidden_states"].rearrange("b s d -> (b s) d")
    y = out.rearrange("b s d -> (b s) d")
    b_up, b_down, ident = t["L0_ffn_b_up"], t["L0_ffn_b_down"], t["ident"]
    ffn(nc, "f1", x0, x1, b_up, b_down, ident, wup, wdn)
    qkv(nc, x1, (t["L0_attn_wq"], t["L0_attn_wk"], t["L0_attn_wv"]), ident, t["rope"], qk, v)
    attention(nc, qk, v, ident, t["causal"], t["edge"], t["older"], t["keyrows"], o, sums)
    output(nc, o, sums, x1, t["L0_attn_wo"], ident, rec, x2)
    ffn(nc, "f2", x2, y, b_up, b_down, ident, wup, wdn)
```

```python
from contextlib import ExitStack

import concourse.bass as bass
from concourse import mybir

F32 = mybir.dt.float32
F32R = mybir.dt.float32r
BF16 = mybir.dt.bfloat16
I16 = mybir.dt.int16
ALU = mybir.AluOpType
ACT = mybir.ActivationFunctionType
AX = mybir.AxisListType

P = 128
NF4 = [-1.0, -0.6961928009986877, -0.5250730514526367, -0.39491748809814453, -0.28444138169288635,
       -0.18477343022823334, -0.09105003625154495, 0.0, 0.07958029955625534, 0.16093020141124725,
       0.24611230194568634, 0.33791524171829224, 0.44070982933044434, 0.5626170039176941,
       0.7229568362236023, 1.0]
QBLK = 64
D = 1024
DK = D // P
H = 2752
RANK = 16
CH = 256
NCH = -(-H // CH)
HT = NCH * CH // P
LAST = H - (NCH - 1) * CH
BATCH, SEQ = 4, 512
T = BATCH * SEQ
TB = 1024
NTB = T // TB
TM = TB // P
EPS = 1e-5
NHEAD, NKV, HD = 32, 8, 32
GROUP = NHEAD // NKV
QKW = (NHEAD + NKV) * HD
QKVW = (NHEAD + 2 * NKV) * HD
CHUNK = 16
BIG = 1e30
SCALE = float(HD) ** -0.5


def after(eng, sem, n):
    if not (isinstance(n, int) and n <= 0):
        eng.wait_ge(sem, n)


def gate(eng, sem, n, passed):
    after(eng, sem, n)
    if not isinstance(n, int):
        eng.sem_inc(passed, 1)


class Pool:

    def __init__(self, nc, ctx, tag):
        self.nc, self.ctx, self.tag = nc, ctx, tag

    def sb(self, name, shape, dt=F32):
        return self.ctx.enter_context(self.nc.sbuf_tensor(f"{self.tag}_{name}", shape, dt))

    def ps(self, name, shape, dt=F32):
        return self.ctx.enter_context(self.nc.psum_tensor(f"{self.tag}_{name}", shape, dt))

    def sem(self, name):
        return self.ctx.enter_context(self.nc.semaphore(f"{self.tag}_{name}"))


def leaf(i):
    import numpy as np
    lo, hi = np.float32(NF4[2 * i]), np.float32(NF4[2 * i + 1])
    s = np.float32(hi - lo)
    for cand in (s, np.nextafter(s, np.float32(4)), np.nextafter(s, np.float32(-4))):
        if np.float32(np.float64(cand) + np.float64(lo)) == hi:
            return float(cand), float(lo)
    raise AssertionError(i)


def dequantise(nc, up_codes, up_absmax, up_a, up_b, dn_codes, dn_absmax, dn_a, dn_b, ident_dram,
               wup_dram, wdn_dram):
    SUB, PART = 4, 512
    with ExitStack() as ctx:
        m = Pool(nc, ctx, "dq")
        ident = m.sb("ident", [P, P])
        codes = m.sb("codes", [P, 2, SUB * PART], I16)
        bits = m.sb("bits", [P, 2, 4, SUB * PART], I16)
        amax_up = m.sb("amax_up", [P, HT, D // QBLK])
        amax_dn = m.sb("amax_dn", [P, DK, NCH * CH // QBLK])
        even = m.sb("even", [P, 2, 4, PART])
        wnat = m.sb("wnat", [P, 2, PART])
        stage = m.sb("stage", [P, 2, 2, SUB * PART], F32R)
        a_nat = m.sb("a_nat", [P, DK, RANK])
        dna_nat = m.sb("dna_nat", [P, HT, RANK])
        upa_t = m.sb("upa_t", [RANK, D])
        upb = m.sb("upb", [RANK, NCH * CH])
        dna_t = m.sb("dna_t", [RANK, NCH * CH])
        dnb = m.sb("dnb", [RANK, D])
        upb_c = m.sb("upb_c", [RANK, 2, CH])
        dna_c = m.sb("dna_c", [RANK, 2, CH])
        ps = m.ps("ps", [P, 8, PART])
        s_in = m.sem("in")
        s_passed = m.sem("passed")
        s_zero = m.sem("zero")
        s_code = [m.sem("code_up"), m.sem("code_dn")]
        s_lt, s_ltc = m.sem("lora_t"), m.sem("lora_copied")
        s_chunk = m.sem("lora_chunk")
        s_bits, s_leaf, s_sel = m.sem("bits"), m.sem("leaf"), m.sem("selected")
        s_w, s_tr, s_hi, s_lo = m.sem("scaled"), m.sem("transposed"), m.sem("hi"), m.sem("lo")
        s_out = [m.sem("out_up"), m.sem("out_dn")]

        code_up = up_codes.rearrange("(h d) -> h d", d=D)
        code_dn = dn_codes.rearrange("(k p h) -> p k h", p=P, h=H)
        abs_up = up_absmax.rearrange("(h b) -> h b", b=D // QBLK)
        abs_dn = dn_absmax.rearrange("(k p b) -> p k b", p=P, b=H // QBLK)
        FULL = H // P
        REST = H - FULL * P

        def part_in(kind, e):
            bank = ps[:, 4 + e % 2, :]
            if kind == 0:
                return bank.rearrange("p (k h) -> p k h", k=4)
            return bank.rearrange("p (k t d) -> p t k d", k=2, t=2)

        def part_out(kind, s, hl):
            if kind == 0:
                t, half = s // 2, s % 2
                return stage[:, 0, hl, :].rearrange("p (k h) -> p k h", k=DK)[:, half * 4:half * 4 + 4, t * P:(t + 1) * P]
            return stage[:, 1, hl, :].rearrange("p (t k d) -> p t k d", t=2, k=DK)[:, :, 2 * s:2 * s + 2, :]

        def order(e):
            return e // SUB, e % SUB

        def steps(eng, step):
            step(0, 0)
            with eng.Fori(1, NCH - 3, 2) as c:
                step(c, 1)
                step(c + 1, 0)
            for c in range(NCH - 2, NCH):
                step(c, c % 2)

        block = ctx.enter_context(nc.Block())

        @block.sync
        def _(sp):
            sp.dma_start(ident[:], ident_dram).then_inc(s_in, 16)
            sp.dma_start(a_nat[:], up_a.rearrange("(k p) r -> p k r", p=P)).then_inc(s_in, 16)
            sp.wait_ge(s_zero, 4)
            sp.dma_start(dna_nat[:, 0:FULL, :], dn_a[0:FULL * P, :].rearrange("(k p) r -> p k r", p=P)).then_inc(s_in, 16)
            sp.dma_start(dna_nat[0:REST, FULL, :], dn_a[FULL * P:H, :]).then_inc(s_in, 16)
            sp.dma_start(upb[:, 0:H], up_b).then_inc(s_in, 16)
            sp.dma_start(dnb[:], dn_b).then_inc(s_in, 16)
            sp.dma_start(amax_up[:, 0:FULL, :], abs_up[0:FULL * P, :].rearrange("(k p) b -> p k b", p=P)).then_inc(s_in, 16)
            sp.dma_start(amax_up[0:REST, FULL, :], abs_up[FULL * P:H, :]).then_inc(s_in, 16)
            sp.dma_start(amax_dn[:, :, 0:H // QBLK], abs_dn).then_inc(s_in, 16)

            def step(c, par):
                for kind, dram in ((0, wup_dram), (1, wdn_dram)):
                    sp.wait_ge(s_lo, c * 8 + 4 * (kind + 1))
                    sp.dma_start(dram[bass.ds(c, 1), :, :].rearrange("o p n -> (o p) n"),
                                 stage[:, kind, :, :].rearrange("p a n -> p (a n)").bitcast(F32)).then_inc(s_out[kind], 16)
            steps(sp, step)
            for kind in range(2):
                sp.wait_ge(s_out[kind], 16 * NCH)

        @block.gpsimd
        def _(pool):
            for tile in (amax_up[:, FULL, :], amax_dn[:, :, H // QBLK:], dna_nat[:, FULL, :], upb[:, H:]):
                pool.memset(tile, 0.0).then_inc(s_zero, 1)

            def load(c, kind):
                if kind == 0:
                    src = code_up[bass.ds(c * CH, CH), :].rearrange("(t p) d -> p t d", p=P)
                    pool.dma_start(codes[:, 0, :].rearrange("p (t d) -> p t d", t=2), src).then_inc(s_code[0], 16)
                else:
                    pool.dma_start(codes[:, 1, :].rearrange("p (k h) -> p k h", k=DK),
                                   code_dn[:, :, bass.ds(c * CH, CH)]).then_inc(s_code[1], 16)

            def load_last(kind):
                c0 = (NCH - 1) * CH
                if kind == 0:
                    pool.dma_start(codes[:, 0, 0:D], code_up[c0:c0 + P, :]).then_inc(s_code[0], 16)
                    pool.dma_start(codes[0:REST, 0, D:2 * D], code_up[c0 + P:H, :]).then_inc(s_code[0], 16)
                else:
                    pool.dma_start(codes[:, 1, :].rearrange("p (k h) -> p k h", k=DK)[:, :, 0:LAST],
                                   code_dn[:, :, c0:H]).then_inc(s_code[1], 16)

            load(0, 0)
            load(0, 1)
            pool.wait_ge(s_in, 16 * 9)
            pool.wait_ge(s_ltc, 2)

            def step(c, par):
                after(pool, s_tr, c * 8 - 8)
                pool.tensor_copy(upb_c[:, par, :], upb[:, bass.ds(c * CH, CH)]).then_inc(s_chunk, 1)
                pool.tensor_copy(dna_c[:, par, :], dna_t[:, bass.ds(c * CH, CH)]).then_inc(s_chunk, 1)
                for e in range(8):
                    kind, s = order(e)
                    n = c * 8 + e
                    pool.wait_ge(s_sel, 7 * n + 7)
                    after(pool, s_tr, n - 1)
                    if kind == 0:
                        t, half = s // 2, s % 2
                        am = amax_up[:, bass.ds(c * 2 + t, 1), half * 8:half * 8 + 8].rearrange("p o b -> p (o b)")\
                            .unsqueeze(2).to_broadcast([P, 8, QBLK])
                        pool.tensor_tensor(wnat[:, e % 2, :].rearrange("p (b q) -> p b q", q=QBLK),
                                           even[:, e % 2, 0, :].rearrange("p (b q) -> p b q", q=QBLK),
                                           am, ALU.mult).then_inc(s_w, 1)
                    else:
                        am = amax_dn[:, 2 * s:2 * s + 2, bass.ds(c * 4, 4)].unsqueeze(3).to_broadcast([P, 2, 4, QBLK])
                        pool.tensor_tensor(wnat[:, e % 2, :].rearrange("p (k b q) -> p k b q", k=2, q=QBLK),
                                           even[:, e % 2, 0, :].rearrange("p (k b q) -> p k b q", k=2, q=QBLK),
                                           am, ALU.mult).then_inc(s_w, 1)
                    if s == 0 and not (isinstance(c, int) and c == NCH - 1):
                        pool.wait_ge(s_bits, c * 2 + kind + 1)
                        if isinstance(c, int) and c == NCH - 2:
                            load_last(kind)
                        else:
                            load(c + 1, kind)
            steps(pool, step)

        @block.scalar
        def _(act):
            act.wait_ge(s_lt, 1)
            act.activation(upa_t[:], ps[0:RANK, 0:2, :].rearrange("p a n -> p (a n)"), ACT.Copy).then_inc(s_ltc, 1)
            act.activation(dna_t[:], ps[0:RANK, 2:8, :].rearrange("p a n -> p (a n)")[:, 0:NCH * CH], ACT.Copy).then_inc(s_ltc, 1)

            def leaves(c, e):
                kind, s = order(e)
                n = c * 8 + e
                if s == 0:
                    act.wait_ge(s_bits, c * 2 + kind + 1)
                bit = bits[:, kind, 0, s * PART:(s + 1) * PART]
                for i in range(4):
                    after(act, s_sel, 7 * n - 6 + i)
                    sc, off = leaf(2 * i + 1)
                    act.activation(ps[:, i, :], bit, ACT.Copy, scale=sc, bias=off).then_inc(s_leaf, 1)
                    if i == 0:
                        after(act, s_w, n - 1)
                    sc, off = leaf(2 * i)
                    act.activation(even[:, e % 2, i, :], bit, ACT.Copy, scale=sc, bias=off).then_inc(s_leaf, 1)

            def hi(c, e):
                kind, s = order(e)
                n = c * 8 + e
                act.wait_ge(s_tr, n + 1)
                if s == 0:
                    after(act, s_out[kind], c * 16)
                act.activation(part_out(kind, s, 0), part_in(kind, e), ACT.Copy).then_inc(s_hi, 1)

            def step(c, par):
                for e in range(8):
                    leaves(c, e)
                    if e >= 2:
                        hi(c, e - 2)
                    elif not (isinstance(c, int) and c == 0):
                        hi(c - 1, e + 6)
            act.wait_ge(s_ltc, 2)
            steps(act, step)
            hi(NCH - 1, 6)
            hi(NCH - 1, 7)

        @block.vector
        def _(dve):
            def lo(c, e):
                kind, s = order(e)
                dve.wait_ge(s_hi, c * 8 + e + 1)
                hi_half = part_out(kind, s, 0)
                low, src = part_out(kind, s, 1), part_in(kind, e)
                dve.tensor_tensor(low, src, hi_half.bitcast(F32), ALU.subtract).then_inc(s_lo, 1)

            def step(c, par):
                for e in range(8):
                    kind, s = order(e)
                    n = c * 8 + e
                    if s == 0:
                        last = isinstance(c, int) and c == NCH - 1 and kind == 0
                        dve.wait_ge(s_code[kind], c * 16 + (32 if last else 16))
                        after(dve, s_leaf, 8 * n - 32)
                        for b in range(3, -1, -1):
                            ins = dve.tensor_scalar(bits[:, kind, b, :], codes[:, kind, :], 1 << b, None, ALU.bitwise_and)
                        ins.then_inc(s_bits, 1)
                        dve.wait_ge(s_bits, c * 2 + kind + 1)
                    cols = slice(s * PART, (s + 1) * PART)
                    ev = even[:, e % 2, :, :]
                    for i in range(4):
                        gate(dve, s_leaf, 8 * n + 2 * i + 2, s_passed)
                        dve.copy_predicated(ev[:, i, :], bits[:, kind, 1, cols], ps[:, i, :]).then_inc(s_sel, 1)
                    for k, (a, b, bit) in enumerate(((0, 1, 2), (2, 3, 2), (0, 2, 3))):
                        gate(dve, s_sel, 7 * n + (2, 4, 6)[k], s_passed)
                        dve.copy_predicated(ev[:, a, :], bits[:, kind, bit, cols], ev[:, b, :]).then_inc(s_sel, 1)
                    if e >= 2:
                        lo(c, e - 2)
                    elif not (isinstance(c, int) and c == 0):
                        lo(c - 1, e + 6)
            steps(dve, step)
            lo(NCH - 1, 6)
            lo(NCH - 1, 7)

        @block.tensor
        def _(pe):
            pe.wait_ge(s_in, 16 * 9)
            for k in range(DK):
                pe.transpose(ps[0:RANK, k // 4, (k % 4) * P:(k % 4 + 1) * P], a_nat[:, k, :], ident[:])
            for t in range(HT):
                ins = pe.transpose(ps[0:RANK, 2 + t // 4, (t % 4) * P:(t % 4 + 1) * P], dna_nat[:, t, :], ident[:])
            ins.then_inc(s_lt, 1)
            pe.wait_ge(s_ltc, 2)

            def step(c, par):
                pe.wait_ge(s_chunk, c * 2 + 2)
                for e in range(8):
                    kind, s = order(e)
                    n = c * 8 + e
                    pe.wait_ge(s_w, n + 1)
                    after(pe, s_lo, n - 1)
                    for j in range(4):
                        dst = ps[:, 4 + e % 2, j * P:(j + 1) * P]
                        pe.matmul(dst, wnat[:, e % 2, j * P:(j + 1) * P], ident[:], is_transpose=True, start=True, stop=False)
                        if kind == 0:
                            t, k = s // 2, (s % 2) * 4 + j
                            ins = pe.matmul(dst, upa_t[:, k * P:(k + 1) * P], upb_c[:, par, t * P:(t + 1) * P], start=False, stop=True)
                        else:
                            k, t = 2 * s + j // 2, j % 2
                            ins = pe.matmul(dst, dna_c[:, par, t * P:(t + 1) * P], dnb[:, k * P:(k + 1) * P], start=False, stop=True)
                    ins.then_inc(s_tr, 1)
            steps(pe, step)


class Count:

    def __init__(self, eng, sem, base=0):
        self.eng, self.sem, self.n = eng, sem, base

    def link(self, ins):
        ins.then_inc(self.sem, 1)
        self.n = self.n + 1
        self.eng.wait_ge(self.sem, self.n)


def inverse_root(dve, link, rstd, var, tmp):
    link(dve.tensor_scalar(tmp, rstd, rstd, var, ALU.mult, ALU.mult))
    link(dve.tensor_scalar(tmp, tmp, -0.5, 1.5, ALU.mult, ALU.add))
    link(dve.tensor_tensor(rstd, rstd, tmp, ALU.mult))


def ffn(nc, tag, x_dram, y_dram, b_up, b_down, ident_dram, wup_dram, wdn_dram):
    NH = TB // 512
    UPG = 2 * NH
    DNG = TM * 2
    LAG = 3
    assert NH == 2 and NCH % 2 == 1
    with ExitStack() as ctx:
        m = Pool(nc, ctx, tag)
        ident = m.sb("ident", [P, P])
        bup = m.sb("bup", [P, HT])
        bup_c = m.sb("bup_c", [P, 2, 2])
        bdn = m.sb("bdn", [P, D])
        y = m.sb("y", [P, TM, D])
        xn = m.sb("xn", [P, 2, 512])
        xt = m.sb("xt", [P, 2, DK, TB], F32R)
        wu = m.sb("wu", [P, 2, 2, DK, CH], F32R)
        wd = m.sb("wd", [P, 2, 2, 2, D], F32R)
        ht = m.sb("ht", [P, 2, 2, 2, TB], F32R)
        hraw = m.sb("hraw", [P, 2, 512])
        stats = m.sb("stats", [P, 2, 6])
        mv = m.sb("mv", [P, TM, 2])
        var = m.sb("var", [P, TM])
        rstd = m.sb("rstd", [P, TM])
        shift = m.sb("shift", [P, TM])
        tmp = m.sb("tmp", [P, TM])
        pt = m.ps("pt", [P, 2, 512])
        pu = m.ps("pu", [P, 2, 512])
        pd = m.ps("pd", [P, 4, 512])
        s_const, s_ident = m.sem("const"), m.sem("ident")
        s_x = [m.sem(f"x{i}") for i in range(TM)]
        s_store = [m.sem("store0"), m.sem("store1")]
        s_seq = m.sem("vector_seq")
        s_bdn, s_yi = m.sem("bdn"), m.sem("y_started")
        s_var, s_sd, s_ln, s_xn = m.sem("var"), m.sem("sd"), m.sem("rstd"), m.sem("xn")
        s_pt, s_xhi, s_xlo = m.sem("x_transposed"), m.sem("x_hi"), m.sem("x_lo")
        s_wu = [m.sem("wu0"), m.sem("wu1")]
        s_wd = [m.sem("wd0"), m.sem("wd1")]
        s_upg, s_bc = m.sem("up_group"), m.sem("bias_chunk")
        s_raw, s_hhi, s_hlo = m.sem("h_raw"), m.sem("h_hi"), m.sem("h_lo")
        s_dng, s_y = m.sem("down_group"), m.sem("y_added")
        x_rows = x_dram.rearrange("(b m p) d -> b p m d", m=TM, p=P)
        y_rows = y_dram.rearrange("(b m p) d -> b p m d", m=TM, p=P)
        FULL = H // P

        block = ctx.enter_context(nc.Block())

        def loads_before(b, par):
            return b * ((NCH + 1) // 2 if par == 0 else NCH // 2)

        @block.sync
        def _(sp):
            def x_load(b, i):
                if b:
                    sp.wait_ge(s_store[i % 2], 16 * ((b - 1) * TM // 2 + i // 2 + 1))
                sp.dma_start(y[:, i, :], x_rows[b, :, i, :]).then_inc(s_x[i], 16)

            def up_load(c, par, done):
                after(sp, s_upg, done * UPG)
                sp.dma_start(wu[:, par, :, :, :].rearrange("p a k h -> p (a k h)").bitcast(F32),
                             wup_dram[bass.ds(c, 1), :, :].rearrange("o p n -> (o p) n")).then_inc(s_wu[par], 16)

            def down_load(c, par, done):
                after(sp, s_dng, done * DNG)
                sp.dma_start(wd[:, par, :, :, :].rearrange("p a k h -> p (a k h)").bitcast(F32),
                             wdn_dram[bass.ds(c, 1), :, :].rearrange("o p n -> (o p) n")).then_inc(s_wd[par], 16)

            def load(c, par, done):
                up_load(c, par, done)
                down_load(c, par, done)
            for i in range(TM // 2):
                x_load(0, i)
                if i == 0:
                    sp.dma_start(ident[:], ident_dram).then_inc(s_ident, 16)
            sp.dma_start(bdn[:], b_down.rearrange("(o d) -> o d", o=1).to_broadcast([P, D])).then_inc(s_const, 16)
            sp.wait_ge(s_bdn, 1)
            sp.dma_start(bup[:, 0:FULL], b_up[0:FULL * P].rearrange("(t p) -> p t", p=P), allow_slow_non_contiguous=True).then_inc(s_const, 16)
            sp.dma_start(bup[0:H - FULL * P, FULL:FULL + 1], b_up[FULL * P:H].rearrange("(p o) -> p o", o=1)).then_inc(s_const, 16)
            up_load(0, 0, 0)
            for i in range(TM // 2, TM):
                x_load(0, i)
            down_load(0, 0, 0)
            load(1, 1, 0)
            for b in range(NTB):
                done = b * NCH
                with sp.Fori(1, NCH // 2) as q:
                    load(2 * q, 0, done + 2 * q - 1)
                    load(2 * q + 1, 1, done + 2 * q)
                load(NCH - 1, 0, done + NCH - 2)
                if b < NTB - 1:
                    up_load(0, 0, done + NCH)
                    load(1, 1, done + NCH - 1)
                for i in range(TM):
                    sp.wait_ge(s_y, (done + NCH - 1) * DNG + 2 * (i + 1))
                    sp.dma_start(y_rows[b, :, i, :], y[:, i, :]).then_inc(s_store[i % 2], 16)
                    if i and b < NTB - 1:
                        x_load(b + 1, i - 1)
                if b < NTB - 1:
                    x_load(b + 1, TM - 1)
                    down_load(0, 0, done + NCH)
            for par in range(2):
                sp.wait_ge(s_store[par], 16 * NTB * TM // 2)

        @block.gpsimd
        def _(pool):
            pool.memset(bup[:, FULL:FULL + 1], 0.0).then_inc(s_bdn, 1)
            pool.wait_ge(s_const, 48)
            pool.tensor_scalar(bdn[:], bdn[:], 0.5, 0.0, ALU.mult, ALU.add).then_inc(s_bdn, 1)
            pool.wait_ge(s_bdn, 2)
            for b in range(NTB):
                for i in range(TM):
                    pool.wait_ge(s_xn, 2 * (b * TM + i + 1))
                    pool.tensor_tensor(y[:, i, :], y[:, i, :], bdn[:], ALU.add).then_inc(s_yi, 1)

        @block.scalar
        def _(act):
            def up_out(c, par, b, groups):
                for g in groups:
                    h, t = g // 2, g % 2
                    n = (b * NCH + c) * UPG + g
                    act.wait_ge(s_upg, n + 1)
                    if g == 0:
                        after(act, s_dng, (b * NCH if known(c, lambda k: k == 0) else b * NCH + c - 1) * DNG)
                    bias = bup_c[:, par, t:t + 1]
                    after(act, s_hlo, n - 1)
                    act.activation(hraw[:, t, :], pu[:, t, :], ACT.Relu, bias=bias).then_inc(s_raw, 1)
                    act.activation(ht[:, par, 0, t, h * 512:(h + 1) * 512], pu[:, t, :], ACT.Relu, bias=bias).then_inc(s_hhi, 1)

            def root(b, i):
                act.wait_ge(s_var, b * TM + i + 1)
                act.activation(rstd[:, i:i + 1], var[:, i:i + 1], ACT.Sqrt).then_inc(s_sd, 1)

            def x_hi(b, i):
                for half in range(2):
                    n = (b * TM + i) * 2 + half
                    act.wait_ge(s_pt, n + 1)
                    if n % (2 * TM) == 0:
                        after(act, s_upg, b * NCH * UPG)
                    act.activation(xt[:, 0, half * 4:half * 4 + 4, i * P:(i + 1) * P],
                                   pt[:, half, :].rearrange("p (k n) -> p k n", k=4), ACT.Copy).then_inc(s_xhi, 1)

            def normal(b, i):
                act.wait_ge(s_ln, b * TM + i + 1)
                for half in range(2):
                    after(act, s_pt, 2 * (b * TM + i) + half - 1)
                    act.activation(xn[:, half, :], y[:, i, half * 512:(half + 1) * 512], ACT.Identity,
                                   scale=rstd[:, i:i + 1], bias=shift[:, i:i + 1]).then_inc(s_xn, 1)

            def biases(b, c, par):
                act.activation(bup_c[:, par, :], bup[:, bass.ds(2 * c, 2)], ACT.Copy).then_inc(s_bc, 1)
                act.wait_ge(s_bc, b * NCH + c + 1)

            for b in range(NTB):
                root(b, 0)
                for i in range(6):
                    root(b, i + 1)
                    if i:
                        x_hi(b, i - 1)
                    normal(b, i)
                root(b, 7)
                act.wait_ge(s_const, 48)
                biases(b, 0, 0)
                up_out(0, 0, b, [0])
                x_hi(b, 5)
                normal(b, 6)
                up_out(0, 0, b, [1])
                x_hi(b, 6)
                normal(b, 7)
                x_hi(b, 7)
                up_out(0, 0, b, [2, 3])

                def one(c, par):
                    biases(b, c, par)
                    up_out(c, par, b, range(UPG))
                one(1, 1)
                with act.Fori(1, NCH // 2) as q:
                    one(2 * q, 0)
                    one(2 * q + 1, 1)
                one(NCH - 1, 0)

        @block.vector
        def _(dve):
            seq = Count(dve, s_seq)

            def moments(b, i):
                dve.wait_ge(s_x[i], 16 * (b + 1))
                for j in range(2):
                    ins = dve.bn_stats(out=stats[:, j, :], in_=y[:, i, j * 512:(j + 1) * 512])
                seq.link(ins)
                seq.link(dve.bn_aggr(out=mv[:, i, :], in_=stats[:, :, :]))
                dve.tensor_scalar(var[:, i:i + 1], mv[:, i, 1:2], EPS, None, ALU.add).then_inc(s_var, 1)

            def invert(b, i):
                r = rstd[:, i:i + 1]
                dve.wait_ge(s_sd, b * TM + i + 1)
                seq.link(dve.reciprocal(r, r))
                inverse_root(dve, seq.link, r, var[:, i:i + 1], tmp[:, i:i + 1])
                dve.tensor_scalar(shift[:, i:i + 1], mv[:, i, 0:1], r, -1.0, ALU.mult, ALU.mult).then_inc(s_ln, 1)

            def x_lo(b, i):
                for half in range(2):
                    dve.wait_ge(s_xhi, (b * TM + i) * 2 + half + 1)
                    dst = xt[:, 1, half * 4:half * 4 + 4, i * P:(i + 1) * P]
                    dve.tensor_tensor(dst, pt[:, half, :].rearrange("p (k n) -> p k n", k=4),
                                      xt[:, 0, half * 4:half * 4 + 4, i * P:(i + 1) * P].bitcast(F32),
                                      ALU.subtract).then_inc(s_xlo, 1)

            def first(b, j):
                if j == 0:
                    moments(b, 0)
                moments(b, j + 1)
                invert(b, j)
                if j:
                    x_lo(b, j - 1)

            def h_lo(b, c, par, groups=range(UPG)):
                for g in groups:
                    h, t = g // 2, g % 2
                    dve.wait_ge(s_hhi, (b * NCH + c) * UPG + g + 1)
                    hi = ht[:, par, 0, t, h * 512:(h + 1) * 512]
                    dve.tensor_tensor(ht[:, par, 1, t, h * 512:(h + 1) * 512], hraw[:, t, :],
                                      hi.bitcast(F32), ALU.subtract).then_inc(s_hlo, 1)

            def add(b, c, i):
                for half in range(2):
                    g = 2 * i + half
                    dve.wait_ge(s_dng, (b * NCH + c) * DNG + g + 1)
                    cols = y[:, i, half * 512:(half + 1) * 512]
                    dve.scalar_tensor_tensor(out=cols, in0=pd[:, g % 4, :], scalar=0.5, in1=cols,
                                             op0=ALU.mult, op1=ALU.add).then_inc(s_y, 1)
            for j in range(5):
                first(0, j)
            for b in range(NTB):
                moments(b, 6)
                invert(b, 5)
                x_lo(b, 4)
                moments(b, 7)
                invert(b, 6)
                invert(b, 7)
                h_lo(b, 0, 0, [0])
                x_lo(b, 5)
                h_lo(b, 0, 0, [1])
                x_lo(b, 6)
                x_lo(b, 7)
                h_lo(b, 0, 0, [2, 3])
                dve.wait_ge(s_yi, TM * (b + 1))

                def one(c, par):
                    h_lo(b, c + 1, 1 - par)
                    after(dve, s_y, (b * NCH + c) * DNG)
                    for i in range(TM):
                        add(b, c, i)
                one(0, 0)
                one(1, 1)
                with dve.Fori(1, NCH // 2) as q:
                    one(2 * q, 0)
                    one(2 * q + 1, 1)
                dve.wait_ge(s_y, (b * NCH + NCH - 1) * DNG)
                for i in range(TM):
                    add(b, NCH - 1, i)
                    if i >= LAG and b < NTB - 1:
                        first(b + 1, i - LAG)

        @block.tensor
        def _(pe):
            pe.wait_ge(s_ident, 16)

            def turn(b, i):
                for half in range(2):
                    n = (b * TM + i) * 2 + half
                    pe.wait_ge(s_xn, n + 1)
                    after(pe, s_xlo, n - 1)
                    for k in range(4):
                        ins = pe.transpose(pt[:, half, k * P:(k + 1) * P], xn[:, half, k * P:(k + 1) * P], ident[:])
                    ins.then_inc(s_pt, 1)

            def up(b, c, par, groups=range(UPG)):
                for g in groups:
                    h, t = g // 2, g % 2
                    if known(c, lambda k: k == 0) and t == 0:
                        pe.wait_ge(s_xlo, (b * TM + (h + 1) * TM // 2) * 2)
                    after(pe, s_hhi, (b * NCH + c) * UPG + g - 1)
                    for k in range(DK):
                        for j, (wi, xi) in enumerate(((0, 0), (0, 1), (1, 0))):
                            ins = pe.matmul(pu[:, t, :], wu[:, par, wi, k, t * P:(t + 1) * P],
                                            xt[:, xi, k, h * 512:(h + 1) * 512],
                                            start=(k == 0 and j == 0), stop=(k == DK - 1 and j == 2))
                    ins.then_inc(s_upg, 1)

            def down(b, c, par, pair, turns=False):
                pe.wait_ge(s_wd[par], 16 * (loads_before(b, par) + pair + 1))
                pe.wait_ge(s_hlo, (b * NCH + c + 1) * UPG)
                for i in range(TM):
                    for half in range(2):
                        g = 2 * i + half
                        after(pe, s_y, (b * NCH + c) * DNG + g - 3)
                        for t in range(2):
                            for j, (hi, wi) in enumerate(((0, 0), (0, 1), (1, 0))):
                                ins = pe.matmul(pd[:, g % 4, :], ht[:, par, hi, t, i * P:(i + 1) * P],
                                                wd[:, par, wi, t, half * 512:(half + 1) * 512],
                                                start=(t == 0 and j == 0), stop=(t == 1 and j == 2))
                        ins.then_inc(s_dng, 1)
                    if turns and i > LAG + 1:
                        turn(b + 1, i - LAG - 2)

            def weights(b, par, pair):
                pe.wait_ge(s_wu[par], 16 * (loads_before(b, par) + pair + 1))
            for i in range(3):
                turn(0, i)
            for b in range(NTB):
                turn(b, 3)
                turn(b, 4)
                weights(b, 0, 0)
                up(b, 0, 0, [0])
                turn(b, 5)
                up(b, 0, 0, [1])
                turn(b, 6)
                turn(b, 7)
                up(b, 0, 0, [2, 3])
                weights(b, 1, 0)
                up(b, 1, 1)
                down(b, 0, 0, 0)
                weights(b, 0, 1)
                up(b, 2, 0)
                down(b, 1, 1, 0)
                with pe.Fori(1, NCH // 2) as q:
                    weights(b, 1, q)
                    up(b, 2 * q + 1, 1)
                    down(b, 2 * q, 0, q)
                    weights(b, 0, q + 1)
                    up(b, 2 * q + 2, 0)
                    down(b, 2 * q + 1, 1, q)
                down(b, NCH - 1, 0, NCH // 2, turns=b < NTB - 1)


def tile_loop(eng, step, between=None):
    n = T // P
    step(0, 0)
    step(1, 1)
    if between:
        between()
    with eng.Fori(1, n // 2 - 1) as q:
        step(2 * q, 0)
        step(2 * q + 1, 1)
    step(n - 2, 0)
    step(n - 1, 1)


def known(m, test):
    return isinstance(m, int) and test(m)


def qkv(nc, x_dram, weights, ident_dram, rope_dram, qk_dram, v_dram):
    NT = T // P
    RT = QKVW // P
    W0 = 2 * RT
    WB = 4
    with ExitStack() as ctx:
        m_ = Pool(nc, ctx, "qk")
        ident = m_.sb("ident", [P, P])
        wnat = m_.sb("wnat", [P, WB, D])
        wt = m_.sb("wt", [P, 2, DK, QKVW], F32R)
        x = m_.sb("x", [P, 2, D])
        rope = m_.sb("rope", [P, 2, 2 * HD])
        xn = m_.sb("xn", [P, 2, D])
        xt = m_.sb("xt", [P, 2, 2, DK, P], F32R)
        straight = m_.sb("straight", [P, QKW])
        crossed = m_.sb("crossed", [P, QKW])
        qr = m_.sb("qr", [P, QKW])
        qs = m_.sb("qs", [P, 2, 2, QKW // P, P], F32R)
        vs = m_.sb("vs", [P, 2, NKV * HD])
        stats = m_.sb("stats", [P, 2, 6])
        mv = m_.sb("mv", [P, 2])
        var = m_.sb("var", [P, 1])
        rstd = m_.sb("rstd", [P, 1])
        tmp = m_.sb("tmp", [P, 1])
        pt = m_.ps("pt", [P, 2, 512])
        pq = m_.ps("pq", [P, 3, 512])
        pr = m_.ps("pr", [P, 3, 512])
        s_const = m_.sem("const")
        s_w = [m_.sem(f"w{i}") for i in range(WB)]
        wbanks = [pt[:, 0, :], pt[:, 1, :], pq[:, 0, :], pq[:, 1, :], pq[:, 2, :], pr[:, 0, :]]
        s_x = [m_.sem("x0"), m_.sem("x1")]
        s_passed = m_.sem("passed")
        s_rope = [m_.sem("rope0"), m_.sem("rope1")]
        s_seq, s_var, s_sd, s_xn = m_.sem("vector_seq"), m_.sem("var"), m_.sem("sd"), m_.sem("xn")
        s_pt, s_hi, s_lo = m_.sem("transposed"), m_.sem("hi"), m_.sem("lo")
        s_mm, s_rd, s_v, s_qr = m_.sem("products"), m_.sem("rope_read"), m_.sem("v"), m_.sem("rotated")
        s_qt, s_qhi, s_qlo = m_.sem("q_transposed"), m_.sem("q_hi"), m_.sem("q_lo")
        s_out = [m_.sem("out0"), m_.sem("out1")]
        rows = [(w, r) for w in weights for r in range(w.shape[0] // P)]
        assert len(rows) == RT
        qk_rows = qk_dram.rearrange("a (j p) t -> a p j t", p=P)
        width = [512, 512, QKW - 1024]

        block = ctx.enter_context(nc.Block())

        @block.sync
        def _(sp):
            sp.dma_start(ident[:], ident_dram).then_inc(s_const, 16)

            def weights():
                for n, (w, r) in enumerate(rows):
                    after(sp, s_pt, 2 * (n - WB + 1))
                    sp.dma_start(wnat[:, n % WB, :], w[r * P:(r + 1) * P, :]).then_inc(s_w[n % WB], 16)

            def step(m, par):
                after(sp, s_xn, m - 1)
                sp.dma_start(x[:, par, :], x_dram[bass.ds(m * P, P), :]).then_inc(s_x[par], 16)
                after(sp, s_rd, 3 * m - 3)
                sp.dma_start(rope[:, par, :], rope_dram[bass.ds(m * P, P), :]).then_inc(s_rope[par], 16)
            tile_loop(sp, step, between=weights)

        @block.gpsimd
        def _(pool):
            def step(m, par):
                for g in range(3):
                    cols = slice(512 * g, 512 * g + width[g])
                    after(pool, s_qt, 3 * m + g - 2)
                    pool.wait_ge(s_rd, 3 * m + g + 1)
                    pool.tensor_tensor(qr[:, cols], straight[:, cols], crossed[:, cols], ALU.add).then_inc(s_qr, 1)
                if not known(m, lambda k: k == 0):
                    store(m - 1, 1 - par)

            def store(m, par):
                pool.wait_ge(s_qlo, 3 * m + 3)
                pool.wait_ge(s_v, m + 1)
                for a in range(2):
                    pool.dma_start(qk_rows[a, :, :, bass.ds(m * P, P)], qs[:, par, a, :, :].bitcast(F32)).then_inc(s_out[par], 16)
                pool.dma_start(v_dram[bass.ds(m * P, P), :], vs[:, par, :]).then_inc(s_out[par], 16)
            tile_loop(pool, step)
            store(NT - 1, 1)
            for par in range(2):
                pool.wait_ge(s_out[par], 48 * NT // 2)

        @block.scalar
        def _(act):
            def root(m):
                act.wait_ge(s_var, m + 1)
                act.activation(rstd[:], var[:], ACT.Sqrt).then_inc(s_sd, 1)
            root(0)
            root(1)
            for unit in range(W0):
                n, half = unit // 2, unit % 2
                act.wait_ge(s_pt, unit + 1)
                act.activation(wt[:, 0, half * 4:half * 4 + 4, n * P:(n + 1) * P],
                               wbanks[unit % 6].rearrange("p (k n) -> p k n", k=4), ACT.Copy).then_inc(s_hi, 1)

            def x_hi(m, par):
                after(act, s_mm, 3 * m - 3)
                for half in range(2):
                    act.wait_ge(s_pt, W0 + 2 * m + half + 1)
                    act.activation(xt[:, par, 0, half * 4:half * 4 + 4, :],
                                   pt[:, half, :].rearrange("p (k n) -> p k n", k=4), ACT.Copy).then_inc(s_hi, 1)

            def q_hi(m, par, pair):
                after(act, s_out[par], 48 * pair)
                for g in range(3):
                    act.wait_ge(s_qt, 3 * m + g + 1)
                    act.activation(qs[:, par, 0, 4 * g:4 * g + width[g] // P, :],
                                   pr[:, g, 0:width[g]].rearrange("p (j n) -> p j n", n=P), ACT.Copy).then_inc(s_qhi, 1)

            def v_out(m, par, pair):
                after(act, s_out[par], 48 * pair)
                act.wait_ge(s_rd, 3 * m + 3)
                act.activation(vs[:, par, :], pq[:, 2, 256:512], ACT.Copy).then_inc(s_v, 1)

            x_hi(0, 0)

            def paired(q, u):
                m = 2 * q + u
                if not known(m, lambda k: k >= NT - 1):
                    x_hi(m + 1, 1 - u)
                if not known(m, lambda k: k >= NT - 2):
                    root(m + 2)
                if not known(m, lambda k: k == 0):
                    v_out(m - 1, 1 - u, q if u else q - 1)
                    q_hi(m - 1, 1 - u, q if u else q - 1)
            paired(0, 0)
            paired(0, 1)
            with act.Fori(1, NT // 2 - 1) as q:
                paired(q, 0)
                paired(q, 1)
            paired(NT // 2 - 1, 0)
            paired(NT // 2 - 1, 1)
            v_out(NT - 1, 1, NT // 2 - 1)
            q_hi(NT - 1, 1, NT // 2 - 1)

        @block.vector
        def _(dve):
            PER = 6

            def norm(m, par, pair):
                seq = Count(dve, s_seq, PER * m)
                dve.wait_ge(s_x[par], 16 * pair + 16)
                for j in range(2):
                    ins = dve.bn_stats(out=stats[:, j, :], in_=x[:, par, j * 512:(j + 1) * 512])
                ins.then_inc(s_seq, 1)
                gate(dve, s_seq, PER * m + 1, s_passed)
                seq.n = PER * m + 1
                seq.link(dve.bn_aggr(out=mv[:], in_=stats[:, :, :]))
                dve.tensor_scalar(var[:], mv[:, 1:2], EPS, None, ALU.add).then_inc(s_var, 1)
                dve.wait_ge(s_sd, m + 1)
                seq.link(dve.reciprocal(rstd[:], rstd[:]))
                inverse_root(dve, seq.link, rstd[:], var[:], tmp[:])
                if not known(m, lambda k: k < 2):
                    dve.wait_ge(s_pt, W0 + 2 * m - 2)
                dve.tensor_scalar(xn[:, par, :], x[:, par, :], mv[:, 0:1], rstd[:], ALU.subtract, ALU.mult).then_inc(s_xn, 1)

            def x_lo(m, par):
                for half in range(2):
                    dve.wait_ge(s_hi, W0 + 2 * m + half + 1)
                    dve.tensor_tensor(xt[:, par, 1, half * 4:half * 4 + 4, :], pt[:, half, :].rearrange("p (k n) -> p k n", k=4),
                                      xt[:, par, 0, half * 4:half * 4 + 4, :].bitcast(F32), ALU.subtract).then_inc(s_lo, 1)

            def q_lo(m, par):
                for g in range(3):
                    dve.wait_ge(s_qhi, 3 * m + g + 1)
                    js = slice(4 * g, 4 * g + width[g] // P)
                    dve.tensor_tensor(qs[:, par, 1, js, :], pr[:, g, 0:width[g]].rearrange("p (j n) -> p j n", n=P),
                                      qs[:, par, 0, js, :].bitcast(F32), ALU.subtract).then_inc(s_qlo, 1)

            def rotate(m, par, pair):
                dve.wait_ge(s_rope[par], 16 * pair + 16)
                for g in range(3):
                    nh = width[g] // HD
                    src = pq[:, g, 0:width[g]].rearrange("p (h r) -> p h r", r=HD)
                    cols = slice(512 * g, 512 * g + width[g])
                    st = straight[:, cols].rearrange("p (h r) -> p h r", r=HD)
                    cr = crossed[:, cols].rearrange("p (h r) -> p h r", r=HD)

                    def over_heads(a, b):
                        return rope[:, par, a:b].unsqueeze(1).to_broadcast([P, nh, b - a])
                    dve.wait_ge(s_mm, 3 * m + g + 1)
                    after(dve, s_qr, 3 * m + g - 2)
                    dve.tensor_tensor(st, src, over_heads(0, HD), ALU.mult)
                    dve.tensor_tensor(cr[:, :, 0:HD // 2], src[:, :, HD // 2:HD], over_heads(HD, HD + HD // 2), ALU.mult)
                    dve.tensor_tensor(cr[:, :, HD // 2:HD], src[:, :, 0:HD // 2], over_heads(HD + HD // 2, 2 * HD), ALU.mult)\
                        .then_inc(s_rd, 1)

            norm(0, 0, 0)
            norm(1, 1, 0)
            for unit in range(W0):
                n, half = unit // 2, unit % 2
                dve.wait_ge(s_hi, unit + 1)
                ks, cs = slice(half * 4, half * 4 + 4), slice(n * P, (n + 1) * P)
                dve.tensor_tensor(wt[:, 1, ks, cs], wbanks[unit % 6].rearrange("p (k n) -> p k n", k=4),
                                  wt[:, 0, ks, cs].bitcast(F32), ALU.subtract).then_inc(s_lo, 1)
            x_lo(0, 0)

            def paired(q, u):
                m = 2 * q + u
                if not known(m, lambda k: k == 0):
                    rotate(m - 1, 1 - u, q if u else q - 1)
                if not known(m, lambda k: k >= NT - 1):
                    x_lo(m + 1, 1 - u)
                if not known(m, lambda k: k >= NT - 2):
                    norm(m + 2, u, q + 1)
                if not known(m, lambda k: k == 0):
                    q_lo(m - 1, 1 - u)
            paired(0, 0)
            paired(0, 1)
            with dve.Fori(1, NT // 2 - 1) as q:
                paired(q, 0)
                paired(q, 1)
            paired(NT // 2 - 1, 0)
            paired(NT // 2 - 1, 1)
            rotate(NT - 1, 1, NT // 2 - 1)
            q_lo(NT - 1, 1)

        @block.tensor
        def _(pe):
            pe.wait_ge(s_const, 16)
            for unit in range(W0):
                n, half = unit // 2, unit % 2
                if half == 0:
                    pe.wait_ge(s_w[n % WB], 16 * (n // WB + 1))
                after(pe, s_lo, unit - 5)
                for k in range(4):
                    kk = half * 4 + k
                    ins = pe.transpose(wbanks[unit % 6][:, k * P:(k + 1) * P], wnat[:, n % WB, kk * P:(kk + 1) * P], ident[:])
                ins.then_inc(s_pt, 1)

            def x_turn(m, par):
                pe.wait_ge(s_xn, m + 1)
                for half in range(2):
                    pe.wait_ge(s_lo, W0 + 2 * m + half - 1)
                    for k in range(4):
                        kk = half * 4 + k
                        ins = pe.transpose(pt[:, half, k * P:(k + 1) * P], xn[:, par, kk * P:(kk + 1) * P], ident[:])
                    ins.then_inc(s_pt, 1)

            def products(m, par, g):
                after(pe, s_rd, 3 * m + g - 2)
                if g == 2:
                    after(pe, s_v, m)
                for k in range(DK):
                    for j, (xi, wi) in enumerate(((0, 0), (0, 1), (1, 0))):
                        ins = pe.matmul(pq[:, g, :], xt[:, par, xi, k, :], wt[:, wi, k, 512 * g:512 * (g + 1)],
                                        start=(k == 0 and j == 0), stop=(k == DK - 1 and j == 2))
                ins.then_inc(s_mm, 1)

            def q_turn(m):
                for g in range(3):
                    pe.wait_ge(s_qr, 3 * m + g + 1)
                    after(pe, s_qlo, 3 * m + g - 2)
                    for j in range(width[g] // P):
                        c0 = 512 * g + j * P
                        ins = pe.transpose(pr[:, g, j * P:(j + 1) * P], qr[:, c0:c0 + P], ident[:])
                    ins.then_inc(s_qt, 1)
            x_turn(0, 0)

            def step(m, par):
                if not known(m, lambda k: k >= NT - 1):
                    x_turn(m + 1, 1 - par)
                pe.wait_ge(s_lo, W0 + 2 * m + 2)
                products(m, par, 0)
                if not known(m, lambda k: k == 0):
                    q_turn(m - 1)
                products(m, par, 1)
                products(m, par, 2)
            tile_loop(pe, step)
            q_turn(NT - 1)


def attention(nc, qk_dram, v_dram, ident_dram, causal_dram, edge_dram, older_dram, keyrows_dram, o_dram, sum_dram):
    QT = SEQ // P
    NC = SEQ // CHUNK
    LATE = 2
    SUMS = 2 * HD
    N = BATCH * NKV
    SLOTS = BATCH
    AT = [0, 512, 896, 1152]
    SCORE, TURN, EXP, VALUE = "score", "turn", "exp", "value"
    ORDER = [(SCORE, 3), (EXP, 3, 0), (EXP, 3, 1), (EXP, 3, 2), (EXP, 3, 3), (TURN, 1),
             (VALUE, 0, 0), (EXP, 2, 0), (VALUE, 0, 1), (EXP, 2, 1), (VALUE, 0, 2), (EXP, 2, 2), (VALUE, 0, 3), (EXP, 2, 3),
             (SCORE, 2), (TURN, 0),
             (VALUE, 1, 0), (EXP, 1, 0), (VALUE, 1, 1), (EXP, 1, 1), (VALUE, 1, 2), (EXP, 1, 2), (VALUE, 1, 3), (EXP, 1, 3),
             (TURN, 3), (VALUE, 2, 0), (EXP, 0, 0), (VALUE, 2, 1), (EXP, 0, 1), (SCORE, 1),
             (VALUE, 2, 2), (EXP, 0, 2), (VALUE, 2, 3), (EXP, 0, 3), (SCORE, 0),
             (VALUE, 3, 0), (VALUE, 3, 1), (VALUE, 3, 2), (VALUE, 3, 3), (TURN, 2)]
    EARLY = (3, 2)
    with ExitStack() as ctx:
        m_ = Pool(nc, ctx, "at")
        identf = m_.sb("identf", [P, P])
        identb = m_.sb("identb", [P, P], BF16)
        causal = m_.sb("causal", [P, P])
        causalb = m_.sb("causalb", [P, P], BF16)
        edgef = m_.sb("edgef", [P, P])
        edge = m_.sb("edge", [P, P], BF16)
        older = m_.sb("older", [P, 4, 16])
        ka = m_.sb("ka", [P, SLOTS, SEQ], F32R)
        qa = m_.sb("qa", [P, SLOTS, GROUP, SEQ], F32R)
        vg = m_.sb("vg", [P, SLOTS, QT, SUMS])
        cm = m_.sb("cm", [P, GROUP, NC])
        m8 = m_.sb("m8", [P, GROUP, 8])
        left = m_.sb("left", [P, GROUP, NC])
        pen = m_.sb("pen", [P, GROUP, 16])
        own = m_.sb("own", [P, GROUP, 16])
        ownsum = m_.sb("ownsum", [P, GROUP])
        mh = m_.sb("mh", [P, GROUP], F32R)
        added = m_.sb("added", [P, QT, GROUP, P])
        edgepen = m_.sb("edgepen", [P, 2, 2, GROUP, P], BF16)
        prob = m_.sb("prob", [P, 2, GROUP, 1280])
        ov = m_.sb("ov", [SUMS, 2, GROUP, SEQ])
        psc = m_.ps("psc", [P, GROUP, 512])
        pa = m_.ps("pa", [P, GROUP, P])
        pst = m_.ps("pst", [P, 2, 512])
        po = m_.ps("po", [P, 512])
        s_const, s_cast, s_init = m_.sem("const"), m_.sem("cast"), m_.sem("init")
        s_keyrow = m_.sem("keyrow")
        s_ld = [m_.sem(f"ld{i}") for i in range(SLOTS)]
        s_seq = m_.sem("vector_seq")
        s_passed, s_ppassed = m_.sem("passed"), m_.sem("pool_passed")
        s_sc, s_cm, s_add = m_.sem("scores"), m_.sem("chunk_max"), m_.sem("added")
        s_pa, s_qa = m_.sem("added_turned"), m_.sem("added_placed")
        s_st, s_p, s_dg = m_.sem("scores_t"), m_.sem("prob"), m_.sem("diagonal")
        s_pv, s_ov = m_.sem("values"), m_.sem("values_copied")
        s_out = [m_.sem("out0"), m_.sem("out1")]
        LINKS = [3, 3, 9, 9]
        PER = sum(LINKS)

        block = ctx.enter_context(nc.Block())

        q_rows = qk_dram[:, 0:NHEAD * HD, :].rearrange("a (g h r) (b t) -> a r b g h t", g=NKV, h=GROUP, b=BATCH)
        k_rows = qk_dram[:, NHEAD * HD:QKW, :].rearrange("a (g r) (b t) -> a r b g t", g=NKV, b=BATCH)
        v_rows = v_dram.rearrange("(b j p) (g r) -> p b g j r", b=BATCH, j=QT, g=NKV)
        o_rows = o_dram.rearrange("(g h r) (b t) -> r b g h t", g=NKV, h=GROUP, b=BATCH)
        sum_rows = sum_dram.rearrange("(g h) (b t) -> b g h t", g=NKV, b=BATCH)

        def groups(step):
            def run(eng):
                for u in range(SLOTS):
                    step(u, u, 0)
                with eng.Fori(1, N // SLOTS - 1) as q:
                    for u in range(SLOTS):
                        step(SLOTS * q + u, u, q)
                for u in range(SLOTS):
                    step(N - SLOTS + u, u, N // SLOTS - 1)
            return run

        @block.sync
        def _(sp):
            for dst, src in ((identf[:], ident_dram), (causal[:], causal_dram), (edgef[:], edge_dram),
                             (older[:], older_dram.rearrange("p (a c) -> p a c", a=4))):
                sp.dma_start(dst, src).then_inc(s_const, 16)

            def load(G, slot, g):
                b = slot
                after(sp, s_pv, GROUP * (G - SLOTS + 1))
                for r, a in ((0, 0), (1, 0), (2, 1)):
                    sp.dma_start(ka[32 * r:32 * r + 32, slot, :].bitcast(F32), k_rows[a, :, b, g, :]).then_inc(s_ld[slot], 16)
                for r, a in ((0, 0), (1, 1), (2, 0)):
                    sp.dma_start(qa[32 * r:32 * r + 32, slot, :, :].bitcast(F32), q_rows[a, :, b, g, :, :]).then_inc(s_ld[slot], 16)
                sp.dma_start(vg[:, slot, :, 0:HD], v_rows[:, b, g, :, :]).then_inc(s_ld[slot], 16)
                if not known(G, lambda k: k < SLOTS):
                    store(G - SLOTS, slot, g - 1)

            def store(G, slot, g):
                sp.wait_ge(s_ov, GROUP * (G + 1))
                sp.dma_start(o_rows[:, slot, g, :, :], ov[0:HD, slot % 2, :, :]).then_inc(s_out[slot % 2], 16)
                sp.dma_start(sum_rows[slot:slot + 1, g, :, :], ov[HD:HD + 1, slot % 2, :, :]).then_inc(s_out[slot % 2], 16)
            groups(load)(sp)
            for slot in range(SLOTS):
                store(N - SLOTS + slot, slot, NKV - 1)
            for par in range(2):
                sp.wait_ge(s_out[par], 32 * N // 2)

        @block.gpsimd
        def _(pool):
            pool.memset(added[:, :, :, :], 0.0).then_inc(s_init, 1)
            pool.memset(vg[:, :, :, HD:SUMS], 1.0).then_inc(s_init, 1)
            for slot in range(SLOTS):
                pool.dma_start(ka[96:128, slot, :], keyrows_dram).then_inc(s_keyrow, 16)

            def diagonal(G, par, j):
                gate(pool, s_p, 16 * G + GROUP * (QT - j), s_ppassed)
                block_ = prob[:, par, :, AT[j]:AT[j] + P]
                pool.affine_select(out=block_, in_=block_, pattern=[[0, GROUP], [1, P]], compare_op=ALU.is_ge,
                                   fill=0.0, base=0, channel_multiplier=-1).then_inc(s_dg, 1)

            def step(G, slot, q):
                for j in reversed(range(QT)):
                    diagonal(G, slot % 2, j)
            groups(step)(pool)

        @block.scalar
        def _(act):
            act.wait_ge(s_const, 64)
            act.activation(identb[:], identf[:], ACT.Copy).then_inc(s_cast, 1)
            act.activation(causalb[:], causal[:], ACT.Copy).then_inc(s_cast, 1)
            act.activation(edge[:], edgef[:], ACT.Copy).then_inc(s_cast, 1)

            def place(G, slot, t):
                act.wait_ge(s_pa, QT * G + QT - t)
                act.activation(qa[96:128, slot, :, t * P:(t + 1) * P], pa[96:128, :, :], ACT.Copy).then_inc(s_qa, 1)

            def exp(G, par, j, h):
                n = 16 * G + GROUP * (QT - 1 - j) + h
                if j == QT - 1 and h == 0:
                    after(act, s_pv, GROUP * (G - 1))
                act.wait_ge(s_st, n + 1)
                act.activation(prob[:, par, h, AT[j]:AT[j] + SEQ - j * P], pst[:, h % 2, 0:SEQ - j * P],
                               ACT.Exp, scale=SCALE).then_inc(s_p, 1)

            def copy(G, par, h, pair):
                if h == 0:
                    after(act, s_out[par], 32 * pair)
                act.wait_ge(s_pv, GROUP * G + h + 1)
                act.activation(ov[:, par, h, :], po[0:SUMS, :], ACT.Copy).then_inc(s_ov, 1)
            for t in EARLY:
                place(0, 0, t)

            def step(G, slot, q):
                ahead = not known(G, lambda k: k >= N - 1)
                behind = not known(G, lambda k: k < 1)
                for kind, *at in ORDER:
                    if kind == EXP:
                        exp(G, slot % 2, *at)
                    if kind == TURN and at[0] not in EARLY:
                        place(G, slot, at[0])
                    if kind == TURN and at[0] in EARLY and ahead:
                        place(G + 1, (slot + 1) % SLOTS, at[0])
                    if kind == VALUE and at[1] == QT - 1 and behind:
                        copy(G - 1, 1 - slot % 2, at[0], 2 * q + (slot - 1) // 2)
            groups(step)(act)
            for h in range(GROUP):
                copy(N - 1, 1, h, N // 2 - 1)

        @block.vector
        def _(dve):
            dve.wait_ge(s_const, 64)
            dve.wait_ge(s_cast, 3)
            dve.wait_ge(s_init, 2)

            def rows(G, par, t):
                seq = Count(dve, s_seq, PER * G + sum(LINKS[t + 1:]))
                turn = QT * G + QT - 1 - t
                nc_t = (t + 1) * P // CHUNK
                gate(dve, s_sc, turn + 1, s_passed)
                dve.tensor_reduce(cm[:, :, 0:nc_t], psc[:, :, 0:(t + 1) * P].rearrange("p h (c k) -> p h c k", k=CHUNK),
                                  AX.X, ALU.max).then_inc(s_cm, 1)
                after(dve, s_pa, turn - QT + 1)
                gate(dve, s_cm, turn + 1, s_passed)
                mx = added[:, t, :, 96]
                seq.link(dve.tensor_reduce(mx, cm[:, :, 0:nc_t], AX.X, ALU.max, negate=True))
                seq.link(dve.tensor_copy(mh[:], mx))
                last = dve.tensor_tensor(added[:, t, :, 97], mx, mh[:].bitcast(F32), ALU.subtract)
                if t < LATE:
                    seq.link(last)
                    return
                L = t - LATE
                for h in range(GROUP):
                    ins = dve.max(out=m8[:, h, :], in_=cm[:, h, 0:nc_t])
                ins.then_inc(s_seq, 1)
                seq.n = seq.n + 1
                gate(dve, s_seq, seq.n, s_passed)
                for h in range(GROUP):
                    ins = dve.match_replace(out=left[:, h, 0:nc_t], in_to_replace=m8[:, h, :],
                                            in_values=cm[:, h, 0:nc_t], imm_value=3e38)
                seq.link(ins)
                seq.link(dve.tensor_scalar(pen[:], left[:, :, 8:24], 1e38, -BIG, ALU.is_lt, ALU.mult))
                seq.link(dve.tensor_tensor(own[:], pen[:], older[:, 2 + L, :].unsqueeze(1).to_broadcast([P, GROUP, 16]), ALU.mult))
                seq.link(dve.tensor_tensor(added[:, t, :, 98:114], pen[:], older[:, L, :].unsqueeze(1).to_broadcast([P, GROUP, 16]), ALU.mult))
                seq.link(dve.tensor_reduce(ownsum[:], own[:], AX.X, ALU.add))
                after(dve, s_st, 16 * (G - 1))
                for h in range(GROUP):
                    ins = dve.tensor_scalar(edgepen[:, par, L, h, :], edge[:], ownsum[:, h:h + 1], None, ALU.mult)
                seq.link(ins)

            for t in reversed(range(QT)):
                rows(0, 0, t)

            def step(G, slot, q):
                if not known(G, lambda k: k >= N - 1):
                    for t in reversed(range(QT)):
                        rows(G + 1, 1 - slot % 2, t)
            groups(step)(dve)

        @block.tensor
        def _(pe):
            pe.wait_ge(s_cast, 3)
            pe.wait_ge(s_keyrow, 16 * SLOTS)
            pe.wait_ge(s_init, 2)

            def scores(G, slot, t, quad):
                if t == QT - 1:
                    pe.wait_ge(s_ld[slot], 112 * (quad + 1))
                after(pe, s_cm, QT * G + QT - 1 - t)
                for h in range(GROUP):
                    pe.matmul(psc[:, h, 0:(t + 1) * P], qa[0:96, slot, h, t * P:(t + 1) * P], ka[0:96, slot, 0:(t + 1) * P],
                              start=True, stop=False)
                    ins = pe.matmul(psc[:, h, t * P:(t + 1) * P], identb[:], causalb[:], start=False, stop=True)
                ins.then_inc(s_sc, 1)

            def turn(G, t):
                pe.wait_ge(s_seq, PER * G + sum(LINKS[t:]))
                after(pe, s_qa, QT * G + QT - 1 - t)
                for h in range(GROUP):
                    ins = pe.transpose(pa[:, h, :], added[:, t, h, :], identf[:])
                ins.then_inc(s_pa, 1)

            def score_t(G, slot, j, h):
                n = 16 * G + GROUP * (QT - 1 - j) + h
                if h == 0:
                    pe.wait_ge(s_qa, QT * G + QT - j)
                after(pe, s_p, n - 1)
                edged = 1 <= j <= 2
                ins = pe.matmul(pst[:, h % 2, 0:SEQ - j * P], ka[:, slot, j * P:(j + 1) * P], qa[:, slot, h, j * P:SEQ],
                                start=True, stop=not edged)
                if edged:
                    ins = pe.matmul(pst[:, h % 2, P:2 * P], edgepen[:, slot % 2, j - 1, h, :], identb[:], start=False, stop=True)
                ins.then_inc(s_st, 1)

            def value(G, slot, h, j):
                if h == 0 and j == 0:
                    pe.wait_ge(s_dg, QT * (G + 1))
                if j == 0:
                    after(pe, s_ov, GROUP * G + h)
                ins = pe.matmul(po[0:SUMS, j * P:SEQ], vg[:, slot, j, :], prob[:, slot % 2, h, AT[j]:AT[j] + SEQ - j * P],
                                start=(j == 0), stop=(j == QT - 1))
                if j == QT - 1:
                    ins.then_inc(s_pv, 1)
            for t in reversed(range(QT)):
                scores(0, 0, t, 0)
                if t in EARLY:
                    turn(0, t)

            def step(G, slot, q):
                ahead = not known(G, lambda k: k >= N - 1)
                behind = not known(G, lambda k: k < 1)
                nslot = (slot + 1) % SLOTS
                for kind, *at in ORDER:
                    if kind == SCORE and ahead:
                        scores(G + 1, nslot, at[0], q + 1 if nslot == 0 else q)
                    if kind == TURN and at[0] not in EARLY:
                        turn(G, at[0])
                    if kind == TURN and at[0] in EARLY and ahead:
                        turn(G + 1, at[0])
                    if kind == EXP:
                        score_t(G, slot, *at)
                    if kind == VALUE and behind:
                        value(G - 1, (slot - 1) % SLOTS, *at)
            groups(step)(pe)
            for h in range(GROUP):
                for j in range(QT):
                    value(N - 1, SLOTS - 1, h, j)


def output(nc, o_dram, sum_dram, x_dram, wo, ident_dram, rec_dram, y_dram):
    NT, RT = T // P, D // P
    W0 = 2 * RT
    WB = 4
    with ExitStack() as ctx:
        m_ = Pool(nc, ctx, "ou")
        ident = m_.sb("ident", [P, P])
        wnat = m_.sb("wnat", [P, WB, D])
        wt = m_.sb("wt", [P, 2, DK, D], F32R)
        sums = m_.sb("sums", [P, NHEAD * T // P])
        o = m_.sb("o", [P, 2, DK, P])
        rec = m_.sb("rec", [P, 2, DK, P])
        od = m_.sb("od", [P, 2, DK, P])
        x = m_.sb("x", [P, 2, D])
        xt = m_.sb("xt", [P, 2, 2, DK, P], F32R)
        y = m_.sb("y", [P, 2, D])
        pt = m_.ps("pt", [P, 2, 512])
        py = m_.ps("py", [P, 4, 512])
        s_const = m_.sem("const")
        s_w = [m_.sem(f"w{i}") for i in range(WB)]
        wbanks = [pt[:, 0, :], pt[:, 1, :]] + [py[:, i, :] for i in range(4)]
        s_o = [m_.sem("o0"), m_.sem("o1")]
        s_sum, s_inv, s_rec = m_.sem("sums"), m_.sem("inverted"), m_.sem("rec_stored")
        s_od = m_.sem("divided")
        s_x = [m_.sem("x0"), m_.sem("x1")]
        s_pt, s_hi, s_lo = m_.sem("transposed"), m_.sem("hi"), m_.sem("lo")
        s_mm, s_y = m_.sem("products"), m_.sem("y")
        o_cols = o_dram.rearrange("(k p) t -> p k t", p=P)
        rec_cols = rec_dram.rearrange("(k h) t -> h k t", h=P // HD)

        def flat(ap):
            return ap.rearrange("h (a t) -> (h a) t", t=NHEAD * T // P)
        s_out = [m_.sem("out0"), m_.sem("out1")]
        block = ctx.enter_context(nc.Block())

        @block.sync
        def _(sp):
            sp.dma_start(sums[:], flat(sum_dram)).then_inc(s_sum, 16)
            sp.dma_start(ident[:], ident_dram).then_inc(s_const, 16)

            def weight_rows(n):
                after(sp, s_pt, 2 * (n - WB + 1))
                sp.dma_start(wnat[:, n % WB, :], wo[n * P:(n + 1) * P, :]).then_inc(s_w[n % WB], 16)
            for n in range(WB):
                weight_rows(n)
            sp.wait_ge(s_inv, 1)
            sp.dma_start(flat(rec_dram), sums[:]).then_inc(s_rec, 16)
            for n in range(WB, RT):
                weight_rows(n)
            sp.wait_ge(s_rec, 16)

            def step(m, par):
                after(sp, s_od, m - 1)
                sp.dma_start(o[:, par, :, :], o_cols[:, :, bass.ds(m * P, P)]).then_inc(s_o[par], 16)
                for h in range(P // HD):
                    row = rec_cols[h:h + 1, :, bass.ds(m * P, P)]
                    sp.dma_start(rec[h * HD:(h + 1) * HD, par, :, :], row.to_broadcast([HD, DK, P])).then_inc(s_o[par], 16)
                after(sp, s_y, 2 * m - 2)
                sp.dma_start(x[:, par, :], x_dram[bass.ds(m * P, P), :]).then_inc(s_x[par], 16)
            tile_loop(sp, step)

        @block.gpsimd
        def _(pool):
            def divide(m, par, pair):
                if not known(m, lambda k: k < 2):
                    pool.wait_ge(s_lo, W0 + m - 1)
                pool.wait_ge(s_o[par], 80 * pair + 80)
                pool.tensor_tensor(od[:, par, :, :], o[:, par, :, :], rec[:, par, :, :], ALU.mult).then_inc(s_od, 1)
            divide(0, 0, 0)

            def paired(q, u):
                m = 2 * q + u
                if not known(m, lambda k: k >= NT - 1):
                    divide(m + 1, 1 - u, q + u)
                pool.wait_ge(s_y, 2 * m + 2)
                pool.dma_start(y_dram[bass.ds(m * P, P), :], y[:, u, :]).then_inc(s_out[u], 16)
            paired(0, 0)
            paired(0, 1)
            with pool.Fori(1, NT // 2 - 1) as q:
                paired(q, 0)
                paired(q, 1)
            paired(NT // 2 - 1, 0)
            paired(NT // 2 - 1, 1)
            for par in range(2):
                pool.wait_ge(s_out[par], 16 * NT // 2)

        @block.scalar
        def _(act):
            for unit in range(W0):
                n, half = unit // 2, unit % 2
                act.wait_ge(s_pt, unit + 1)
                act.activation(wt[:, 0, half * 4:half * 4 + 4, n * P:(n + 1) * P],
                               wbanks[unit % 6].rearrange("p (k n) -> p k n", k=4), ACT.Copy).then_inc(s_hi, 1)

            def x_hi(m, par):
                after(act, s_mm, 2 * m - 2)
                act.wait_ge(s_od, m + 1)
                act.activation(xt[:, par, 0, :, :], od[:, par, :, :], ACT.Copy).then_inc(s_hi, 1)
            tile_loop(act, x_hi)

        @block.vector
        def _(dve):
            dve.wait_ge(s_sum, 16)
            dve.reciprocal(sums[:], sums[:]).then_inc(s_inv, 1)
            for unit in range(W0):
                n, half = unit // 2, unit % 2
                dve.wait_ge(s_hi, unit + 1)
                ks, cs = slice(half * 4, half * 4 + 4), slice(n * P, (n + 1) * P)
                dve.tensor_tensor(wt[:, 1, ks, cs], wbanks[unit % 6].rearrange("p (k n) -> p k n", k=4),
                                  wt[:, 0, ks, cs].bitcast(F32), ALU.subtract).then_inc(s_lo, 1)

            def x_lo(m, par):
                dve.wait_ge(s_hi, W0 + m + 1)
                dve.tensor_tensor(xt[:, par, 1, :, :], od[:, par, :, :], xt[:, par, 0, :, :].bitcast(F32),
                                  ALU.subtract).then_inc(s_lo, 1)
            x_lo(0, 0)

            def paired(q, u):
                m = 2 * q + u
                if not known(m, lambda k: k >= NT - 1):
                    x_lo(m + 1, 1 - u)
                dve.wait_ge(s_x[u], 16 * q + 16)
                after(dve, s_out[u], 16 * q)
                for half in range(2):
                    cols = slice(half * 512, (half + 1) * 512)
                    dve.wait_ge(s_mm, 2 * m + half + 1)
                    dve.tensor_tensor(y[:, u, cols], py[:, 2 * u + half, :], x[:, u, cols], ALU.add).then_inc(s_y, 1)
            paired(0, 0)
            paired(0, 1)
            with dve.Fori(1, NT // 2 - 1) as q:
                paired(q, 0)
                paired(q, 1)
            paired(NT // 2 - 1, 0)
            paired(NT // 2 - 1, 1)

        @block.tensor
        def _(pe):
            pe.wait_ge(s_const, 16)
            for unit in range(W0):
                n, half = unit // 2, unit % 2
                if half == 0:
                    pe.wait_ge(s_w[n % WB], 16 * (n // WB + 1))
                after(pe, s_lo, unit - 5)
                for k in range(4):
                    kk = half * 4 + k
                    ins = pe.transpose(wbanks[unit % 6][:, k * P:(k + 1) * P], wnat[:, n % WB, kk * P:(kk + 1) * P], ident[:])
                ins.then_inc(s_pt, 1)

            def products(m, par):
                pe.wait_ge(s_lo, W0 + m + 1)
                after(pe, s_y, 2 * m - 2)
                for half in range(2):
                    for k in range(DK):
                        for j, (xi, wi) in enumerate(((0, 0), (0, 1), (1, 0))):
                            ins = pe.matmul(py[:, 2 * par + half, :], xt[:, par, xi, k, :],
                                            wt[:, wi, k, 512 * half:512 * (half + 1)],
                                            start=(k == 0 and j == 0), stop=(k == DK - 1 and j == 2))
                    ins.then_inc(s_mm, 1)
            tile_loop(pe, products)


def kernel(**inputs):
    import numpy as np
    import concourse.bacc as bacc
    from concourse.bass_utils import run_bass_kernel_spmd

    nc = bacc.Bacc("TRN2", target_bir_lowering=False, num_devices=1)
    arrays, t = {}, {}
    host = {k: np.ascontiguousarray(v) for k, v in inputs.items()}
    half = HD // 2
    inv = (np.float32(1.0) / np.power(np.float32(10000.0), np.arange(0, HD, 2, dtype=np.float32) / np.float32(HD))).astype(np.float32)
    freq = np.arange(SEQ, dtype=np.float32)[:, None] * inv[None, :]
    sin = np.sin(freq).astype(np.float32)
    host["rope"] = np.concatenate([np.cos(freq), np.cos(freq), -sin, sin], axis=1).astype(np.float32)
    host["rope"] = np.tile(host["rope"], (BATCH, 1))
    host["ident"] = np.eye(P, dtype=np.float32)
    q, k = np.arange(P)[:, None], np.arange(P)[None, :]
    host["causal"] = np.where(k > q, np.float32(-BIG), np.float32(0.0))
    host["edge"] = ((k <= q) & (k // CHUNK == q // CHUNK)).astype(np.float32)
    c = np.arange(CHUNK)[None, :]
    rel = np.arange(P)[:, None] // CHUNK
    host["older"] = np.concatenate([(c < rel), (c < rel + 8), (c == rel), (c == rel + 8)], axis=1).astype(np.float32)
    key = np.arange(SEQ)
    rows = np.zeros((32, SEQ), np.float32)
    rows[0:2] = 1.0
    for j in range(16):
        rows[2 + j] = key // CHUNK == 8 + j
    host["keyrows"] = rows
    for name, a in host.items():
        arrays[name] = a
        t[name] = nc.dram_tensor(name, a.shape, mybir.dt.from_np(a.dtype), kind="ExternalInput").ap()
    out = nc.dram_tensor("out", (BATCH, SEQ, D), F32, kind="ExternalOutput").ap()
    program(nc, t, out)
    r = run_bass_kernel_spmd(nc, [arrays], core_ids=[0])
    return r.results[0]["out"]


def program(nc, t, out):
    def scratch(name, shape, dt=F32):
        return nc.dram_tensor(name, shape, dt, kind="Internal").ap()
    wup = scratch("wup", (NCH, P, 4 * 1024))
    wdn = scratch("wdn", (NCH, P, 4 * 1024))
    dequantise(nc, t["L0_ffn_w_up_codes"], t["L0_ffn_w_up_absmax"], t["L0_ffn_w_up_lora_a"], t["L0_ffn_w_up_lora_b"],
               t["L0_ffn_w_down_codes"], t["L0_ffn_w_down_absmax"], t["L0_ffn_w_down_lora_a"], t["L0_ffn_w_down_lora_b"],
               t["ident"], wup, wdn)
    x1, x2, o = scratch("x1", (T, D)), scratch("x2", (T, D)), scratch("o", (D, T))
    sums, rec = scratch("sums", (NHEAD, T)), scratch("rec", (NHEAD, T))
    qk, v = scratch("qk", (2, QKW, T)), scratch("v", (T, NKV * HD))
    x0 = t["L0_attn_hidden_states"].rearrange("b s d -> (b s) d")
    y = out.rearrange("b s d -> (b s) d")
    b_up, b_down, ident = t["L0_ffn_b_up"], t["L0_ffn_b_down"], t["ident"]
    ffn(nc, "f1", x0, x1, b_up, b_down, ident, wup, wdn)
    qkv(nc, x1, (t["L0_attn_wq"], t["L0_attn_wk"], t["L0_attn_wv"]), ident, t["rope"], qk, v)
    attention(nc, qk, v, ident, t["causal"], t["edge"], t["older"], t["keyrows"], o, sums)
    output(nc, o, sums, x1, t["L0_attn_wo"], ident, rec, x2)
    ffn(nc, "f2", x2, y, b_up, b_down, ident, wup, wdn)
```
